# Optimizing a Trainium2 kernel written in Bass

```python
import numpy as np
import jax
import jax.numpy as jnp

def _softmax(x, axis=-1):
    return jax.nn.softmax(x, axis=axis)

def _gelu(x):
    return jax.nn.gelu(x, approximate=True)

def _silu(x):
    return jax.nn.silu(x)

def _sigmoid(x):
    return jax.nn.sigmoid(x)

def _layernorm(x, axis=-1, eps=1e-05):
    m = jnp.mean(x, axis=axis, keepdims=True)
    v = jnp.var(x, axis=axis, keepdims=True)
    return (x - m) / jnp.sqrt(v + eps)

def _scatter_add(tgt, idx, src, axis=0):
    return tgt.at[idx].add(src)

def _segment_sum(src, seg, n):
    return jax.ops.segment_sum(src, seg, n)
kernel_name = 'mk_gnn_ffn_d1_gnn_r8_c554b6'

def setup_inputs(seed: int=0):
    np.random.seed(seed)
    _w = jnp.asarray

    def _rec_inputs():
        import jax
        import jax.numpy as jnp
        _gk = jax.random.key(seed)
        x = -0.0001126 + 1 * jax.random.normal(jax.random.fold_in(_gk, 1), (1250, 768), jnp.float32)
        src = jax.random.randint(jax.random.fold_in(_gk, 2), (20000,), 0, 1250, jnp.int32)
        dst = jnp.minimum((1250 * jax.random.uniform(jax.random.fold_in(_gk, 3), (20000,)) ** 2.0).astype(jnp.int32), 9999)
        _o = jnp.argsort(dst, stable=True)
        src = src[_o]
        dst = dst[_o]
        return (x, src, dst)
    x, src, dst = _rec_inputs()

    def _L0_gnn_setup():
        import jax, jax.numpy as jnp
        import numpy as np
        N, E, DM, H, L = (1250, 20000, 768, 8, 2)
        HD = DM // H
        LN_EPS = 1e-05
        SLOPE = 0.2

        def layer_norm(x, w, b):
            mu = jnp.mean(x, axis=-1, keepdims=True)
            var = jnp.mean(jnp.square(x - mu), axis=-1, keepdims=True)
            return (x - mu) * jax.lax.rsqrt(var + LN_EPS) * w + b

        def gatv2_layer(x, Ws, bs, Wd, bd, attn, src, dst):
            hs = (x @ Ws + bs).reshape(N, H, HD)
            hd = (x @ Wd + bd).reshape(N, H, HD)
            hs_e = hs[src]
            e = jax.nn.leaky_relu(hs_e + hd[dst], SLOPE)
            logits = jnp.einsum('ehd,hd->eh', e, attn)
            m = jax.ops.segment_max(logits, dst, num_segments=N)
            ex = jnp.exp(logits - m[dst])
            s = jax.ops.segment_sum(ex, dst, num_segments=N)
            alpha = ex / s[dst]
            out = jax.ops.segment_sum(alpha[..., None] * hs_e, dst, num_segments=N)
            return jax.nn.elu(out).reshape(N, DM)
        key = jax.random.key(seed)
        ks = jax.random.split(key, 12)
        xav = 1.0 / np.sqrt(DM)
        return {'x': jax.random.normal(ks[0], (N, DM), jnp.float32), 'Wsrc': jax.random.uniform(ks[1], (L, DM, DM), jnp.float32, -xav, xav), 'bsrc': jnp.zeros((L, DM), jnp.float32), 'Wdst': jax.random.uniform(ks[2], (L, DM, DM), jnp.float32, -xav, xav), 'bdst': jnp.zeros((L, DM), jnp.float32), 'attn': jax.random.normal(ks[3], (L, H, HD), jnp.float32) * (1.0 / np.sqrt(HD)), 'ln_w': jnp.ones((L, DM), jnp.float32), 'ln_b': jnp.zeros((L, DM), jnp.float32), 'on_w': jnp.ones((DM,), jnp.float32), 'on_b': jnp.zeros((DM,), jnp.float32), 'src': jax.random.randint(ks[4], (E,), 0, N, jnp.int32), 'dst': jax.random.randint(ks[5], (E,), 0, N, jnp.int32)}
    _L0_gnn_all = _L0_gnn_setup()
    _L0_gnn_in = {k: v for k, v in _L0_gnn_all.items() if k in ('Wsrc', 'bsrc', 'Wdst', 'bdst', 'attn', 'ln_w', 'ln_b', 'on_w', 'on_b')}
    del _L0_gnn_all

    def _L0_ffn_setup():
        import math
        import jax, jax.numpy as jnp
        import numpy as np
        N_HEAD = 12
        N_EXP = 8
        TOP_K = 2
        TRAIN_CAPACITY = 1.25
        MIN_CAPACITY = 4
        LN_EPS = 1e-05
        NEG_INF = -1e+30

        def _layer_norm(x, w, b):
            mu = jnp.mean(x, axis=-1, keepdims=True)
            var = jnp.var(x, axis=-1, keepdims=True)
            return (x - mu) * jax.lax.rsqrt(var + LN_EPS) * w + b

        def _attention(x, qkv_w, qkv_b, proj_w, proj_b):
            B, T, C = x.shape
            H, D = (N_HEAD, C // N_HEAD)
            qkv = x @ qkv_w + qkv_b
            q, k, v = jnp.split(qkv, 3, axis=-1)
            q = q.reshape(B, T, H, D).transpose(0, 2, 1, 3)
            k = k.reshape(B, T, H, D).transpose(0, 2, 1, 3)
            v = v.reshape(B, T, H, D).transpose(0, 2, 1, 3)
            scores = jnp.einsum('bhqd,bhkd->bhqk', q, k) / math.sqrt(D)
            causal = jnp.tril(jnp.ones((T, T), bool))
            scores = jnp.where(causal, scores, NEG_INF)
            attn = jax.nn.softmax(scores, axis=-1)
            y = jnp.einsum('bhqk,bhkd->bhqd', attn, v)
            y = y.transpose(0, 2, 1, 3).reshape(B, T, C)
            return y @ proj_w + proj_b

        def _moe(x, w_g, fc_w, fc_b, pj_w, pj_b):
            B, T, C = x.shape
            N, E, K = (B * T, N_EXP, TOP_K)
            cap = int(math.floor(K * TRAIN_CAPACITY * N / E))
            cap += cap % 2
            cap = max(cap, MIN_CAPACITY)
            logits = (x @ w_g).reshape(N, E)
            _, topk_idx = jax.lax.top_k(logits, K)
            hot = jax.nn.one_hot(topk_idx, E, dtype=jnp.int32)
            sel = hot.sum(axis=1) > 0
            router_probs = jax.nn.softmax(jnp.where(sel, logits, NEG_INF), axis=-1)
            exp_mask = hot.transpose(1, 0, 2)
            exp_rank = jnp.cumsum(exp_mask.reshape(K * N, E), axis=0) - 1
            exp_rank = exp_rank.reshape(K, N, E)
            exp_mask = exp_mask * (exp_rank < cap).astype(jnp.int32)
            exp_rank = jnp.sum(exp_mask * exp_rank, axis=-1)
            exp_weights = exp_mask.astype(x.dtype) * router_probs[None]
            rank_sc = jax.nn.one_hot(exp_rank, cap, dtype=x.dtype)
            cb_weight = jnp.einsum('kne,knc->nec', exp_weights, rank_sc)
            sec_mask = (cb_weight != 0).astype(x.dtype)
            xf = x.reshape(N, C)
            xb = jnp.einsum('nec,nd->ecd', sec_mask, xf)
            h = jax.nn.gelu(jnp.einsum('ecd,edf->ecf', xb, fc_w) + fc_b, approximate=False)
            out = jnp.einsum('ecf,efd->ecd', h, pj_w) + pj_b
            y = jnp.einsum('nec,ecd->nd', cb_weight, out)
            return y.reshape(B, T, C)
        key = jax.random.key(seed)
        ks = jax.random.split(key, 12)
        B, T, C = (4, 1024, 768)
        E, F = (N_EXP, 4 * C)
        s = 0.02
        return {'x': jax.random.normal(ks[0], (B, T, C), jnp.float32), 'ln1_w': jnp.ones((C,), jnp.float32), 'ln1_b': jnp.zeros((C,), jnp.float32), 'ln2_w': jnp.ones((C,), jnp.float32), 'ln2_b': jnp.zeros((C,), jnp.float32), 'attn_qkv_w': jax.random.normal(ks[1], (C, 3 * C), jnp.float32) * s, 'attn_qkv_b': jnp.zeros((3 * C,), jnp.float32), 'attn_proj_w': jax.random.normal(ks[2], (C, C), jnp.float32) * s, 'attn_proj_b': jnp.zeros((C,), jnp.float32), 'w_g': jax.random.normal(ks[3], (C, E), jnp.float32) * s, 'exp_fc_w': jax.random.normal(ks[4], (E, C, F), jnp.float32) * s, 'exp_fc_b': jnp.zeros((E, 1, F), jnp.float32), 'exp_proj_w': jax.random.normal(ks[5], (E, F, C), jnp.float32) * s, 'exp_proj_b': jnp.zeros((E, 1, C), jnp.float32)}
    _L0_ffn_all = _L0_ffn_setup()
    _L0_ffn_in = {k: v for k, v in _L0_ffn_all.items() if k in ('ln1_w', 'ln1_b', 'ln2_w', 'ln2_b', 'attn_qkv_w', 'attn_qkv_b', 'attn_proj_w', 'attn_proj_b', 'w_g', 'exp_fc_w', 'exp_fc_b', 'exp_proj_w', 'exp_proj_b')}
    del _L0_ffn_all
    return {'x': x, 'src': src, 'dst': dst, 'L0_gnn_Wsrc': _L0_gnn_in['Wsrc'], 'L0_gnn_bsrc': _L0_gnn_in['bsrc'], 'L0_gnn_Wdst': _L0_gnn_in['Wdst'], 'L0_gnn_bdst': _L0_gnn_in['bdst'], 'L0_gnn_attn': _L0_gnn_in['attn'], 'L0_gnn_ln_w': _L0_gnn_in['ln_w'], 'L0_gnn_ln_b': _L0_gnn_in['ln_b'], 'L0_gnn_on_w': _L0_gnn_in['on_w'], 'L0_gnn_on_b': _L0_gnn_in['on_b'], 'L0_ffn_ln1_w': _L0_ffn_in['ln1_w'], 'L0_ffn_ln1_b': _L0_ffn_in['ln1_b'], 'L0_ffn_ln2_w': _L0_ffn_in['ln2_w'], 'L0_ffn_ln2_b': _L0_ffn_in['ln2_b'], 'L0_ffn_attn_qkv_w': _L0_ffn_in['attn_qkv_w'], 'L0_ffn_attn_qkv_b': _L0_ffn_in['attn_qkv_b'], 'L0_ffn_attn_proj_w': _L0_ffn_in['attn_proj_w'], 'L0_ffn_attn_proj_b': _L0_ffn_in['attn_proj_b'], 'L0_ffn_w_g': _L0_ffn_in['w_g'], 'L0_ffn_exp_fc_w': _L0_ffn_in['exp_fc_w'], 'L0_ffn_exp_fc_b': _L0_ffn_in['exp_fc_b'], 'L0_ffn_exp_proj_w': _L0_ffn_in['exp_proj_w'], 'L0_ffn_exp_proj_b': _L0_ffn_in['exp_proj_b']}

def reference(x, src, dst, L0_gnn_Wsrc, L0_gnn_bsrc, L0_gnn_Wdst, L0_gnn_bdst, L0_gnn_attn, L0_gnn_ln_w, L0_gnn_ln_b, L0_gnn_on_w, L0_gnn_on_b, L0_ffn_ln1_w, L0_ffn_ln1_b, L0_ffn_ln2_w, L0_ffn_ln2_b, L0_ffn_attn_qkv_w, L0_ffn_attn_qkv_b, L0_ffn_attn_proj_w, L0_ffn_attn_proj_b, L0_ffn_w_g, L0_ffn_exp_fc_w, L0_ffn_exp_fc_b, L0_ffn_exp_proj_w, L0_ffn_exp_proj_b):
    import jax
    import jax.numpy as jnp

    def _L0_gnn_ref(x, Wsrc, bsrc, Wdst, bdst, attn, ln_w, ln_b, on_w, on_b, src, dst):
        import jax, jax.numpy as jnp
        import numpy as np
        N, E, DM, H, L = (1250, 20000, 768, 8, 2)
        HD = DM // H
        LN_EPS = 1e-05
        SLOPE = 0.2

        def layer_norm(x, w, b):
            mu = jnp.mean(x, axis=-1, keepdims=True)
            var = jnp.mean(jnp.square(x - mu), axis=-1, keepdims=True)
            return (x - mu) * jax.lax.rsqrt(var + LN_EPS) * w + b

        def gatv2_layer(x, Ws, bs, Wd, bd, attn, src, dst):
            hs = (x @ Ws + bs).reshape(N, H, HD)
            hd = (x @ Wd + bd).reshape(N, H, HD)
            hs_e = hs[src]
            e = jax.nn.leaky_relu(hs_e + hd[dst], SLOPE)
            logits = jnp.einsum('ehd,hd->eh', e, attn)
            m = jax.ops.segment_max(logits, dst, num_segments=N)
            ex = jnp.exp(logits - m[dst])
            s = jax.ops.segment_sum(ex, dst, num_segments=N)
            alpha = ex / s[dst]
            out = jax.ops.segment_sum(alpha[..., None] * hs_e, dst, num_segments=N)
            return jax.nn.elu(out).reshape(N, DM)
        h = x
        for l in range(L):
            h_new = gatv2_layer(h, Wsrc[l], bsrc[l], Wdst[l], bdst[l], attn[l], src, dst)
            h = layer_norm(h_new + h, ln_w[l], ln_b[l])
        return layer_norm(h, on_w, on_b)

    def _L0_ffn_ref(x, ln1_w, ln1_b, ln2_w, ln2_b, attn_qkv_w, attn_qkv_b, attn_proj_w, attn_proj_b, w_g, exp_fc_w, exp_fc_b, exp_proj_w, exp_proj_b):
        import math
        import jax, jax.numpy as jnp
        import numpy as np
        N_HEAD = 12
        N_EXP = 8
        TOP_K = 2
        TRAIN_CAPACITY = 1.25
        MIN_CAPACITY = 4
        LN_EPS = 1e-05
        NEG_INF = -1e+30

        def _layer_norm(x, w, b):
            mu = jnp.mean(x, axis=-1, keepdims=True)
            var = jnp.var(x, axis=-1, keepdims=True)
            return (x - mu) * jax.lax.rsqrt(var + LN_EPS) * w + b

        def _attention(x, qkv_w, qkv_b, proj_w, proj_b):
            B, T, C = x.shape
            H, D = (N_HEAD, C // N_HEAD)
            qkv = x @ qkv_w + qkv_b
            q, k, v = jnp.split(qkv, 3, axis=-1)
            q = q.reshape(B, T, H, D).transpose(0, 2, 1, 3)
            k = k.reshape(B, T, H, D).transpose(0, 2, 1, 3)
            v = v.reshape(B, T, H, D).transpose(0, 2, 1, 3)
            scores = jnp.einsum('bhqd,bhkd->bhqk', q, k) / math.sqrt(D)
            causal = jnp.tril(jnp.ones((T, T), bool))
            scores = jnp.where(causal, scores, NEG_INF)
            attn = jax.nn.softmax(scores, axis=-1)
            y = jnp.einsum('bhqk,bhkd->bhqd', attn, v)
            y = y.transpose(0, 2, 1, 3).reshape(B, T, C)
            return y @ proj_w + proj_b

        def _moe(x, w_g, fc_w, fc_b, pj_w, pj_b):
            B, T, C = x.shape
            N, E, K = (B * T, N_EXP, TOP_K)
            cap = int(math.floor(K * TRAIN_CAPACITY * N / E))
            cap += cap % 2
            cap = max(cap, MIN_CAPACITY)
            logits = (x @ w_g).reshape(N, E)
            _, topk_idx = jax.lax.top_k(logits, K)
            hot = jax.nn.one_hot(topk_idx, E, dtype=jnp.int32)
            sel = hot.sum(axis=1) > 0
            router_probs = jax.nn.softmax(jnp.where(sel, logits, NEG_INF), axis=-1)
            exp_mask = hot.transpose(1, 0, 2)
            exp_rank = jnp.cumsum(exp_mask.reshape(K * N, E), axis=0) - 1
            exp_rank = exp_rank.reshape(K, N, E)
            exp_mask = exp_mask * (exp_rank < cap).astype(jnp.int32)
            exp_rank = jnp.sum(exp_mask * exp_rank, axis=-1)
            exp_weights = exp_mask.astype(x.dtype) * router_probs[None]
            rank_sc = jax.nn.one_hot(exp_rank, cap, dtype=x.dtype)
            cb_weight = jnp.einsum('kne,knc->nec', exp_weights, rank_sc)
            sec_mask = (cb_weight != 0).astype(x.dtype)
            xf = x.reshape(N, C)
            xb = jnp.einsum('nec,nd->ecd', sec_mask, xf)
            h = jax.nn.gelu(jnp.einsum('ecd,edf->ecf', xb, fc_w) + fc_b, approximate=False)
            out = jnp.einsum('ecf,efd->ecd', h, pj_w) + pj_b
            y = jnp.einsum('nec,ecd->nd', cb_weight, out)
            return y.reshape(B, T, C)
        x = x + _attention(_layer_norm(x, ln1_w, ln1_b), attn_qkv_w, attn_qkv_b, attn_proj_w, attn_proj_b)
        x = x + _moe(_layer_norm(x, ln2_w, ln2_b), w_g, exp_fc_w, exp_fc_b, exp_proj_w, exp_proj_b)
        return x
    x = x + _L0_gnn_ref(_layernorm(x, axis=-1), L0_gnn_Wsrc, L0_gnn_bsrc, L0_gnn_Wdst, L0_gnn_bdst, L0_gnn_attn, L0_gnn_ln_w, L0_gnn_ln_b, L0_gnn_on_w, L0_gnn_on_b, src, dst)
    x = x + _L0_ffn_ref(_layernorm(x, axis=-1)[None], L0_ffn_ln1_w, L0_ffn_ln1_b, L0_ffn_ln2_w, L0_ffn_ln2_b, L0_ffn_attn_qkv_w, L0_ffn_attn_qkv_b, L0_ffn_attn_proj_w, L0_ffn_attn_proj_b, L0_ffn_w_g, L0_ffn_exp_fc_w, L0_ffn_exp_fc_b, L0_ffn_exp_proj_w, L0_ffn_exp_proj_b)[0]
    return x

_drawn_inputs = setup_inputs


def setup_inputs(seed=0):
    import zlib

    import numpy as np

    out = dict(_drawn_inputs(seed))
    spreads = {'L0_gnn_bsrc': (0.0, 0.1),
     'L0_gnn_bdst': (0.0, 2.0),
     'L0_gnn_ln_w': (1.0, 0.2),
     'L0_gnn_ln_b': (0.0, 0.1),
     'L0_gnn_on_w': (1.0, 0.2),
     'L0_gnn_on_b': (0.0, 0.1),
     'L0_ffn_ln1_w': (1.0, 0.6),
     'L0_ffn_ln1_b': (0.0, 0.421),
     'L0_ffn_ln2_w': (1.0, 0.2),
     'L0_ffn_ln2_b': (0.0, 0.1),
     'L0_ffn_attn_qkv_b': (0.0, 0.286),
     'L0_ffn_attn_proj_b': (0.0, 0.1),
     'L0_ffn_exp_fc_b': (0.0, 0.487),
     'L0_ffn_exp_proj_b': (0.0, 0.342)}
    factors = {'L0_gnn_Wdst': 2.954}
    for name, (base, spread) in spreads.items():
        noise = np.random.default_rng([zlib.crc32(name.encode()), seed]).standard_normal(out[name].shape)
        drawn = base * np.exp(spread * noise) if base else spread * noise
        out[name] = jnp.asarray(drawn.astype(out[name].dtype))
    for name, factor in factors.items():
        out[name] = (out[name] * factor).astype(out[name].dtype)
    return out
```

```python
from contextlib import ExitStack

import concourse.bass as bass
from concourse import mybir

ALU = mybir.AluOpType
ACT = mybir.ActivationFunctionType
AX = mybir.AxisListType
F32 = mybir.dt.float32
F32R = mybir.dt.float32r
BF16 = mybir.dt.bfloat16
I32 = mybir.dt.int32
U32 = mybir.dt.uint32

N, D = 1250, 768
P, NT = 125, 10
KC = D // 128
E, EP = 20000, 128
ET = -(-E // EP)
ETP = 160
ITEMS = 172
GH, GD = 8, D // 8
DX = D + GH
L = 2
CH = 16
CE = E // CH
NH, HD = 12, 64
PAIRS = NH // 2
NX, F = 8, 4 * D
CAP = 390
SLOTS = NX * CAP
FG = 12
FJ = F // 128 // FG
ROWS = [(0, 128), (128, 128), (256, 128), (384, 6)]
LN_EPS = 1e-5
SLOPE = 0.2
BIG = 1e30
FAR = 1e6
GROUPS = [(0, 4), (4, 4), (8, 2)]


def past(t, n):
    return not isinstance(t, int) or t >= n


class Chain:

    def __init__(self, eng, sem, base=0):
        self.eng, self.sem, self.base, self.n = eng, sem, base, 0

    def do(self, ins):
        ins.then_inc(self.sem, 1)
        self.n += 1

    def wait(self):
        self.eng.wait_ge(self.sem, self.base + self.n)

    def link(self, ins):
        self.do(ins)
        self.wait()


def laps(eng, n, body):
    body(0)
    with eng.Fori(1, n) as i:
        body(i)


def build(nc, a, out):
    with ExitStack() as top:
        def sb(name, shape, dt=F32, ctx=top):
            return ctx.enter_context(nc.sbuf_tensor(name, shape, dt))

        def ps(name, shape, ctx, dt=F32):
            return ctx.enter_context(nc.psum_tensor(name, shape, dt))

        live = []

        def sem(name):
            live.append(nc.alloc_semaphore(name=name))
            return live[-1]

        def end_stage():
            nc.clear_and_free_semaphores(live)
            live.clear()
            nc.all_engine_barrier()

        def dram(name, shape, dt=F32):
            return nc.dram_tensor(name, shape, dt, kind="Internal").ap()

        def spread(row, parts):
            return row.partition_broadcast(parts)

        def rows(t):
            return t.rearrange("(t p) d -> p t d", p=P)

        hs_dram = dram("hs_dram", (N, DX))
        hd_dram = dram("hd_dram", (N, DX))
        logit_dram = dram("logit_dram", (GH, ETP * EP))
        ex_dram = dram("ex_dram", (GH, ETP * EP))
        pair_dram = dram("pair_dram", (128, 2))
        top_dram = dram("top_dram", (128, 2))
        slot_in = dram("slot_in", (SLOTS + 2 * N, D))
        slot_out = dram("slot_out", (SLOTS, D))

        x = sb("x", [P, NT, D])
        wgt = sb("wgt", [P, 2 * NT])
        slot_read = sb("slot_read", [P, 2 * NT], I32)
        ident = sb("ident", [128, 128])
        mid = top.enter_context(ExitStack())
        h = sb("h", [P, NT, D], F32, mid)
        ones = sb("ones", [128, 128], F32, mid)
        edge = mid.enter_context(ExitStack())
        lanes = sb("lanes", [128, P], F32, edge)
        src_item = sb("src_item", [128, ITEMS], I32, edge)
        dst_idx = sb("dst_idx", [128, ETP], I32, edge)
        dst_rel = sb("dst_rel", [128, ITEMS], F32, edge)
        win = sb("win", [1, ITEMS], I32, edge)
        cut_tile = sb("cut_tile", [128, NT - 1], I32, edge)
        dstc = sb("dstc", [128, CE], F32, edge)
        change = sb("change", [128, CE + 1], F32, edge)
        change2 = sb("change2", [GH, 2 * CH + 1], F32, edge)

        def layer_norm(ch, source, dest, temps, w=None, b=None):
            stats, mv, rstd, var_ready, std_ready = temps
            for t in range(NT):
                for k in range(2):
                    ch.do(nc.vector.bn_stats(stats[:, t, 6 * k:6 * k + 6], source[:, t, 384 * k:384 * k + 384]))
            ch.wait()
            for t in range(NT):
                ch.do(nc.vector.bn_aggr(mv[:, t, :], stats[:, t, :]))
            ch.wait()
            nc.vector.tensor_scalar(rstd[:, :], mv[:, :, 1], LN_EPS, None, ALU.add).then_inc(var_ready, 1)
            ch.eng.wait_ge(std_ready, 1)
            ch.link(nc.vector.reciprocal(rstd[:, :], rstd[:, :]))
            for t in range(NT):
                ch.do(nc.vector.tensor_scalar(dest[:, t, :], source[:, t, :], mv[:, t, 0:1], rstd[:, t:t + 1],
                                              ALU.subtract, ALU.mult))
            ch.wait()
            if w is not None:
                wide = [P, NT, D]
                ch.link(nc.vector.tensor_tensor(dest[:, :, :], dest[:, :, :], w[:, :].unsqueeze(1).to_broadcast(wide),
                                                ALU.mult))
                ch.link(nc.vector.tensor_tensor(dest[:, :, :], dest[:, :, :], b[:, :].unsqueeze(1).to_broadcast(wide),
                                                ALU.add))

        def root(act, temps):
            stats, mv, rstd, var_ready, std_ready = temps
            act.wait_ge(var_ready, 1)
            nc.scalar.activation(rstd[:, :], rstd[:, :], ACT.Sqrt).then_inc(std_ready, 1)

        def norm_temps(ctx, name):
            return (sb(f"{name}_stats", [P, NT, 12], F32, ctx), sb(f"{name}_mv", [P, NT, 2], F32, ctx),
                    sb(f"{name}_rstd", [P, NT], F32, ctx), sem(f"{name}_var_ready"), sem(f"{name}_std_ready"))

        def turn_pe(pe, source, bank, turned, taken):
            k = 0
            for c in range(KC):
                for t0, n in GROUPS:
                    if k >= len(bank):
                        pe.wait_ge(taken, k - len(bank) + 1)
                    for t in range(n):
                        ins = nc.tensor.transpose(bank[k % len(bank)][:, t * P:t * P + P],
                                                  source[:, t0 + t, c * 128:c * 128 + 128], ident[0:P, 0:P])
                    ins.then_inc(turned, 1)
                    k += 1

        def turn_act(act, dest, bank, turned, taken):
            k = 0
            for c in range(KC):
                for t0, n in GROUPS:
                    act.wait_ge(turned, k + 1)
                    nc.scalar.copy(dest[:, c, t0 * P:(t0 + n) * P], bank[k % len(bank)][:, 0:n * P]).then_inc(taken, 1)
                    k += 1

        TURNS = KC * len(GROUPS)

        with ExitStack() as ctx:
            rows_a = sb("rows_a", [128, 128], I32, ctx)
            rows_b = sb("rows_b", [32, 128], I32, ctx)
            drows_a = sb("drows_a", [128, 128], I32, ctx)
            drows_b = sb("drows_b", [32, 128], I32, ctx)
            fa = sb("fa", [128, 4, 128], F32, ctx)
            dst_f = sb("dst_f", [128, ETP], F32, ctx)
            first = sb("first", [128, ETP], F32, ctx)
            win_f = sb("win_f", [128, ETP], F32, ctx)
            junk = sb("junk", [128, ETP], F32, ctx)
            below = sb("below", [128, NT - 1], F32, ctx)
            cut = sb("cut", [128, NT - 1], F32, ctx)
            cut_i = sb("cut_i", [128, NT - 1], I32, ctx)
            cut_tf = sb("cut_tf", [128, NT - 1], F32, ctx)
            even = sb("even", [128, NT - 1], F32, ctx)
            dc_i = sb("dc_i", [128, CE], I32, ctx)
            pair = sb("pair", [128, 2], F32, ctx)
            pairs8 = sb("pairs8", [GH, 2 * CH], F32, ctx)
            zero = sb("zero", [120, D], F32, ctx)
            temps = norm_temps(ctx, "ln0")
            turned_p = ps("turned_p", [128, 512], ctx)
            first_p = ps("first_p", [128, 512], ctx)
            cut_p = ps("cut_p", [128, 512], ctx)

            x_in, src_in, dst_in, dc_in = sem("x_in"), sem("src_in"), sem("dst_in"), sem("dc_in")
            padded, consts, iota_done = sem("padded"), sem("consts"), sem("iota_done")
            v0, src_turned, dst_turned = sem("v0"), sem("src_turned"), sem("dst_turned")
            floats, dst_f_ready, first_ready, below_ready, cut_ready = (
                sem("floats"), sem("dst_f_ready"), sem("first_ready"), sem("below_ready"), sem("cut_ready"))
            pair_ready, pair_out, pair_in, zeroed = sem("pair_ready"), sem("pair_out"), sem("pair_in"), sem("zeroed")
            full = ET - 1 - 128

            with nc.Block() as block:
                @block.sync
                def _(sp):
                    sp.dma_start(x[:, :, :], rows(a["x"])).then_inc(x_in, 16)
                    sp.wait_ge(padded, 2)
                    for name, ra, rb, s in (("src", rows_a, rows_b, src_in), ("dst", drows_a, drows_b, dst_in)):
                        v = a[name]
                        sp.dma_start(ra[:, :], v[0:128 * EP].rearrange("(t e) -> t e", e=EP)).then_inc(s, 16)
                        sp.dma_start(rb[0:full, :], v[128 * EP:(128 + full) * EP].rearrange("(t e) -> t e", e=EP)
                                     ).then_inc(s, 16)
                        sp.dma_start(rb[full:full + 1, 0:E - (ET - 1) * EP],
                                     v[(ET - 1) * EP:E].rearrange("(a e) -> a e", a=1)).then_inc(s, 16)
                    for g in range(GH):
                        sp.dma_start(dc_i[g * CH:(g + 1) * CH, :], a["dst"].rearrange("(c e) -> c e", e=CE)
                                     ).then_inc(dc_in, 16)
                    sp.wait_ge(pair_ready, 1)
                    sp.dma_start(pair_dram, pair[:, :]).then_inc(pair_out, 16)
                    sp.wait_ge(pair_out, 16)
                    sp.dma_start(pairs8[:, :], pair_dram.rearrange("(h c) k -> h (c k)", h=GH)).then_inc(pair_in, 16)

                @block.scalar
                def _(act):
                    act.wait_ge(consts, 3)
                    act.dma_start(slot_in[0:SLOTS, :].rearrange("(p r) d -> p r d", p=120),
                                  zero[:, :].unsqueeze(1).to_broadcast([120, SLOTS // 120, D])).then_inc(zeroed, 16)
                    root(act, temps)
                    act.wait_ge(zeroed, 16)

                @block.gpsimd
                def _(pool):
                    nc.gpsimd.memset(rows_b[:, :], 0).then_inc(padded, 1)
                    nc.gpsimd.memset(drows_b[:, :], int(FAR)).then_inc(padded, 1)
                    nc.gpsimd.memset(ident[:, :], 0.0).then_inc(consts, 1)
                    nc.gpsimd.memset(ones[:, :], 1.0).then_inc(consts, 1)
                    nc.gpsimd.memset(zero[:, :], 0.0).then_inc(consts, 1)
                    pool.wait_ge(consts, 3)
                    nc.gpsimd.affine_select(out=ident[:, :], in_=ident[:, :], compare_op=ALU.not_equal, fill=1.0,
                                            base=0, pattern=[[-1, 128]], channel_multiplier=1).then_inc(consts, 1)
                    nc.gpsimd.iota(lanes[:, :], [[1, P]], base=0, channel_multiplier=0,
                                   allow_small_or_imprecise_dtypes=True).then_inc(iota_done, 1)
                    pool.wait_ge(iota_done, 1)

                @block.tensor
                def _(pe):
                    pe.wait_ge(consts, 4)
                    pe.wait_ge(floats, 2)
                    nc.tensor.transpose(turned_p[:, 0:128], fa[:, 0, :], ident[:, :]).then_inc(src_turned, 1)
                    nc.tensor.transpose(turned_p[:, 128:160], fa[0:32, 1, :], ident[0:32, 0:32]).then_inc(src_turned, 1)
                    pe.wait_ge(floats, 4)
                    nc.tensor.transpose(turned_p[:, 160:288], fa[:, 2, :], ident[:, :]).then_inc(dst_turned, 1)
                    nc.tensor.transpose(turned_p[:, 288:320], fa[0:32, 3, :], ident[0:32, 0:32]).then_inc(dst_turned, 1)
                    pe.wait_ge(dst_f_ready, 1)
                    nc.tensor.matmul(first_p[:, 0:ETP], ones[0:1, :], dst_f[0:1, :], start=True, stop=True
                                     ).then_inc(first_ready, 1)
                    pe.wait_ge(below_ready, NT - 1)
                    nc.tensor.matmul(cut_p[:, 0:NT - 1], ones[:, :], below[:, :], start=True, stop=True
                                     ).then_inc(cut_ready, 1)

                @block.vector
                def _(dve):
                    ch = Chain(dve, v0)
                    dve.wait_ge(src_in, 48)
                    nc.vector.tensor_copy(fa[:, 0, :], rows_a[:, :]).then_inc(floats, 1)
                    nc.vector.tensor_copy(fa[0:32, 1, :], rows_b[:, :]).then_inc(floats, 1)
                    dve.wait_ge(dst_in, 48)
                    nc.vector.tensor_copy(fa[:, 2, :], drows_a[:, :]).then_inc(floats, 1)
                    nc.vector.tensor_copy(fa[0:32, 3, :], drows_b[:, :]).then_inc(floats, 1)
                    ch.do(nc.vector.memset(src_item[:, ETP:], 0))
                    ch.do(nc.vector.memset(dst_rel[:, ETP:], FAR))
                    ch.do(nc.vector.memset(win[:, ETP:], 0))
                    ch.do(nc.vector.memset(win_f[:, :], 0.0))
                    dve.wait_ge(src_turned, 2)
                    dve.wait_ge(dst_turned, 2)
                    nc.vector.tensor_copy(dst_f[:, :], turned_p[:, ETP:2 * ETP]).then_inc(dst_f_ready, 1)
                    ch.do(nc.vector.tensor_copy(src_item[:, 0:ETP], turned_p[:, 0:ETP]))
                    dve.wait_ge(dst_f_ready, 1)
                    ch.do(nc.vector.tensor_scalar(dst_idx[:, :], dst_f[:, :], float(N - 1), None, ALU.min))
                    for k in range(1, NT):
                        nc.vector.tensor_scalar(junk[:, :], dst_f[:, :], float(P * k), 0.0, ALU.is_lt, ALU.add,
                                                accum_out=below[:, k - 1:k]).then_inc(below_ready, 1)
                        dve.wait_ge(below_ready, k)
                    dve.wait_ge(first_ready, 1)
                    ch.link(nc.vector.tensor_copy(first[:, :], first_p[:, 0:ETP]))
                    for k in range(1, NT):
                        ch.link(nc.vector.scalar_tensor_tensor(out=win_f[:, :], in0=first[:, :], scalar=float(P * k),
                                                               in1=win_f[:, :], op0=ALU.is_ge, op1=ALU.add))
                    ch.do(nc.vector.tensor_copy(win[:, 0:ETP], win_f[0:1, :]))
                    ch.do(nc.vector.scalar_tensor_tensor(out=dst_rel[:, 0:ETP], in0=win_f[:, :], scalar=-float(P),
                                                         in1=dst_f[:, :], op0=ALU.mult, op1=ALU.add))
                    dve.wait_ge(cut_ready, 1)
                    ch.do(nc.vector.tensor_copy(cut[:, :], cut_p[:, 0:NT - 1]))
                    ch.link(nc.vector.tensor_copy(cut_i[:, :], cut_p[:, 0:NT - 1]))
                    ch.link(nc.vector.tensor_scalar(cut_tile[:, :], cut_i[:, :], 7, None, ALU.arith_shift_right))
                    ch.link(nc.vector.tensor_copy(cut_tf[:, :], cut_tile[:, :]))
                    ch.link(nc.vector.scalar_tensor_tensor(out=even[:, :], in0=cut_tf[:, :], scalar=-float(EP),
                                                           in1=cut[:, :], op0=ALU.mult, op1=ALU.add))
                    ch.link(nc.vector.tensor_scalar(even[:, :], even[:, :], 0.0, FAR, ALU.is_equal, ALU.mult))
                    for k in range(1, NT):
                        t = nc.vector.value_load(cut_tile[0:1, k - 1:k], min_val=0, max_val=ETP - 1)
                        ch.do(nc.vector.tensor_copy(src_item[:, ETP + k - 1:ETP + k], src_item[:, bass.ds(t, 1)]))
                        ch.do(nc.vector.tensor_scalar(dst_rel[:, ETP + k - 1:ETP + k], dst_f[:, bass.ds(t, 1)],
                                                      -float(P * k), even[:, k - 1:k], ALU.add, ALU.add))
                        ch.do(nc.vector.memset(win[:, ETP + k - 1:ETP + k], k))
                    dve.wait_ge(dc_in, 16 * GH)
                    ch.do(nc.vector.tensor_copy(dstc[:, :], dc_i[:, :]))
                    ch.do(nc.vector.memset(change[:, :], -BIG))
                    ch.do(nc.vector.memset(change2[:, :], -BIG))
                    ch.wait()
                    ch.do(nc.vector.tensor_tensor(change[:, 1:CE], dstc[:, 1:CE], dstc[:, 0:CE - 1], ALU.not_equal))
                    ch.do(nc.vector.tensor_copy(pair[:, 0:1], dstc[:, 0:1]))
                    ch.do(nc.vector.tensor_copy(pair[:, 1:2], dstc[:, CE - 1:CE]))
                    ch.wait()
                    dve.sem_inc(pair_ready, 1)
                    ch.do(nc.vector.tensor_scalar(change[:, 1:CE], change[:, 1:CE], -BIG, None, ALU.mult))
                    dve.wait_ge(pair_in, 16)
                    ch.link(nc.vector.tensor_tensor(change2[:, 1:2 * CH], pairs8[:, 1:2 * CH], pairs8[:, 0:2 * CH - 1],
                                                    ALU.not_equal))
                    ch.link(nc.vector.tensor_scalar(change2[:, 1:2 * CH], change2[:, 1:2 * CH], -BIG, None, ALU.mult))
                    dve.wait_ge(x_in, 16)
                    layer_norm(ch, x, h, temps)
            end_stage()

        with nc.Fori(0, L) as l:

            with ExitStack() as ctx:
                hT = sb("hT", [128, KC, N], F32, ctx)
                w = [sb(f"w{k}_", [128, KC, D], F32, ctx) for k in range(2)]
                bias = sb("gbias", [P, 2, D], F32, ctx)
                att = sb("att", [P, D], F32, ctx)
                rowx = [sb(f"rowx{k}_", [P, DX], F32, ctx) for k in range(2)]
                prod = sb("prod", [P, D], F32, ctx)
                bank = [ps(f"lin{k}_", [128, 512], ctx) for k in range(8)]
                w_in, b_in, turned, taken = sem("w_in"), sem("b_in"), sem("turned"), sem("taken")
                lin_done, v1 = sem("lin_done"), sem("v1_")
                stored = [sem(f"stored{k}_") for k in range(2)]
                PER = 3

                with nc.Block() as block:
                    @block.sync
                    def _(sp):
                        for k, name in enumerate(("Wsrc", "Wdst")):
                            sp.dma_start(w[k][:, :, :], a[f"L0_gnn_{name}"][bass.ds(l, 1)].rearrange("a (c p) n -> p (a c) n", p=128)
                                         ).then_inc(w_in, 16)
                        for k, name in enumerate(("bsrc", "bdst")):
                            sp.dma_start(bias[:, k, :], spread(a[f"L0_gnn_{name}"][bass.ds(l, 1)].rearrange("a d -> (a d)"), P)).then_inc(b_in, 16)
                        sp.dma_start(att[:, :], spread(a["L0_gnn_attn"][bass.ds(l, 1)].rearrange("a h d -> (a h d)"), P)
                                     ).then_inc(b_in, 16)
                        for t in range(NT):
                            for k, table in enumerate((hs_dram, hd_dram)):
                                sp.wait_ge(v1, PER * (2 * t + k + 1) + 1)
                                sp.dma_start(table[t * P:t * P + P, :], rowx[k][:, :]).then_inc(stored[k], 16)
                        for k in range(2):
                            sp.wait_ge(stored[k], 16 * NT)

                    @block.tensor
                    def _(pe):
                        turn_pe(pe, h, bank, turned, taken)
                        pe.wait_ge(taken, TURNS)
                        pe.wait_ge(w_in, 32)
                        for m in range(2 * NT):
                            t, k = m // 2, m % 2
                            if m >= 4:
                                pe.wait_ge(v1, PER * (m - 4) + 2)
                            for half in range(2):
                                for c in range(KC):
                                    ins = nc.tensor.matmul(bank[2 * (m % 4) + half][0:P, 0:384],
                                                           hT[:, c, t * P:t * P + P],
                                                           w[k][:, c, 384 * half:384 * half + 384],
                                                           start=(c == 0), stop=(c == KC - 1))
                            ins.then_inc(lin_done, 1)

                    @block.scalar
                    def _(act):
                        turn_act(act, hT, bank, turned, taken)

                    @block.vector
                    def _(dve):
                        ch = Chain(dve, v1)
                        dve.wait_ge(b_in, 48)
                        ch.link(nc.vector.tensor_scalar(att[:, :], att[:, :], SLOPE, None, ALU.mult))
                        for m in range(2 * NT):
                            t, k = m // 2, m % 2
                            r = rowx[k]
                            dve.wait_ge(lin_done, m + 1)
                            if t:
                                dve.wait_ge(stored[k], 16 * t)
                            nc.vector.tensor_tensor(r[:, 0:384], bank[2 * (m % 4)][0:P, 0:384], bias[:, k, 0:384],
                                                    ALU.add)
                            ch.link(nc.vector.tensor_tensor(r[:, 384:D], bank[2 * (m % 4) + 1][0:P, 0:384],
                                                            bias[:, k, 384:D], ALU.add))
                            ch.link(nc.vector.tensor_tensor(prod[:, :], r[:, 0:D], att[:, :], ALU.mult))
                            ch.link(nc.vector.tensor_reduce(r[:, D:DX], prod[:, :].rearrange("p (h d) -> p h d", h=GH),
                                                            AX.X, ALU.add))
                end_stage()

            with ExitStack() as ctx:
                R = 4
                LAPS = ETP // R
                gs = sb("gs", [128, R, DX], F32, ctx)
                gd = sb("gd", [128, R, DX], F32, ctx)
                cur = sb("cur", [128, R, 2], I32, ctx)
                rz = sb("rz", [128, 2, D], F32, ctx)
                acol = sb("acol", [128, KC], F32, ctx)
                arow = sb("arow", [KC, 128], F32, ctx)
                a8 = sb("a8", [128, KC, GH], F32, ctx)
                lg = sb("lg", [GH, R * EP], F32, ctx)
                zt = [ps(f"zt{k}_", [128, 1024], ctx) for k in range(2)]
                lp = ps("lp", [128, 512], ctx)
                ap_ = ps("ap_", [128, 512], ctx)
                a_in, a_turned, mask0, a8_ready, v2 = (sem("a_in"), sem("a_turned"), sem("mask0_"),
                                                       sem("a8_ready"), sem("v2_"))
                picked, handed = sem("picked"), sem("handed")
                got = [sem(f"got{k}_") for k in range(R)]
                z_ready, z_turned, relu_done, l_done, l_taken, l_out = (
                    sem("z_ready"), sem("z_turned"), sem("relu_done"), sem("l_done"),
                    sem("l_taken"), sem("l_out"))

                with nc.Block() as block:
                    @block.sync
                    def _(sp):
                        sp.dma_start(arow[:, :], a["L0_gnn_attn"][bass.ds(l, 1)].rearrange("a h d -> (a h d)")
                                     .rearrange("(c p) -> c p", p=128)).then_inc(a_in, 16)

                        sp.sem_inc(l_out, 16)

                        def lap(i):
                            sp.wait_ge(l_taken, i + 1)
                            sp.dma_start(logit_dram[:, bass.ds(i * (R * EP), R * EP)], lg[:, :]).then_inc(l_out, 16)
                        laps(sp, LAPS, lap)
                        sp.wait_ge(l_out, 16 * (LAPS + 1))

                    @block.gpsimd
                    def _(pool):
                        nc.gpsimd.memset(a8[:, :, :], 1.0 - SLOPE).then_inc(mask0, 1)
                        pool.wait_ge(mask0, 1)
                        nc.gpsimd.affine_select(out=a8[:, :, :], in_=a8[:, :, :], compare_op=ALU.is_ge, fill=0.0, base=0,
                                                pattern=[[128, KC], [-GD, GH]], channel_multiplier=1).then_inc(mask0, 1)
                        pool.wait_ge(mask0, 2)
                        nc.gpsimd.affine_select(out=a8[:, :, :], in_=a8[:, :, :], compare_op=ALU.is_ge, fill=0.0,
                                                base=GD - 1, pattern=[[-128, KC], [GD, GH]], channel_multiplier=-1
                                                ).then_inc(mask0, 1)

                        def lap(i):
                            for j in range(R):
                                t = R * i + j
                                if past(t, R):
                                    pool.wait_ge(l_done, t - R + 1)
                                nc.gpsimd.tensor_copy(cur[:, j, 0:1], src_item[:, bass.ds(t, 1)]).then_inc(picked, 1)
                                nc.gpsimd.tensor_copy(cur[:, j, 1:2], dst_idx[:, bass.ds(t, 1)]).then_inc(picked, 1)
                                pool.wait_ge(picked, 2 * t + 2)
                                pool.sem_inc(handed, 1)
                                for k, (g, table) in enumerate(((gs, hs_dram), (gd, hd_dram))):
                                    nc.gpsimd.indirect_dma_start(
                                        out=g[:, j, :], out_offset=None, in_=table,
                                        in_offset=bass.IndirectOffsetOnAxis(ap=cur[:, j, k:k + 1], axis=0)
                                    ).then_inc(got[j], 16)
                        laps(pool, LAPS, lap)

                    @block.vector
                    def _(dve):
                        dve.wait_ge(a_turned, 1)
                        nc.vector.tensor_copy(acol[:, :], ap_[:, 0:KC]).then_inc(v2, 1)
                        dve.wait_ge(v2, 1)
                        dve.wait_ge(mask0, 3)
                        nc.vector.tensor_tensor(a8[:, :, :], a8[:, :, :],
                                                acol[:, :].unsqueeze(2).to_broadcast([128, KC, GH]), ALU.mult
                                                ).then_inc(a8_ready, 1)

                        def take(laps_done):
                            dve.wait_ge(l_done, R * laps_done)
                            dve.wait_ge(l_out, 16 * laps_done)
                            nc.vector.tensor_copy(lg[:, :], lp[0:GH, 0:R * EP]).then_inc(l_taken, 1)

                        def lap(i):
                            for j in range(R):
                                dve.wait_ge(got[j], 32 * (i + 1))
                                nc.vector.tensor_tensor(gs[:, j, :], gs[:, j, :], gd[:, j, :], ALU.add
                                                        ).then_inc(z_ready, 1)
                                if j == 1 and past(i, 1):
                                    take(i)
                        laps(dve, LAPS, lap)
                        take(LAPS)

                    @block.tensor
                    def _(pe):
                        pe.wait_ge(a_in, 16)
                        nc.tensor.transpose(ap_[:, 0:KC], arow[:, :], ident[0:KC, 0:KC]).then_inc(a_turned, 1)
                        pe.wait_ge(a8_ready, 1)

                        def turn(t, j):
                            pe.wait_ge(z_ready, t + 1)
                            if past(t, 2):
                                pe.wait_ge(relu_done, t - 1)
                            for c in range(KC):
                                ins = nc.tensor.transpose(zt[j % 2][:, c * 128:c * 128 + 128],
                                                          gs[:, j, c * 128:c * 128 + 128], ident[:, :])
                            ins.then_inc(z_turned, 1)

                        def logits(t, i, j):
                            pe.wait_ge(relu_done, t + 1)
                            if j == 0 and past(i, 1):
                                pe.wait_ge(l_taken, i)
                            at = lp[0:GH, j * EP:j * EP + EP]
                            for c in range(KC):
                                nc.tensor.matmul(at, a8[:, c, :], rz[:, j % 2, c * 128:c * 128 + 128],
                                                 start=(c == 0), stop=False)
                            nc.tensor.matmul(at, gs[:, j, D:DX], ident[:, :], start=False, stop=True
                                             ).then_inc(l_done, 1)

                        def lap(i):
                            for j in range(R):
                                turn(R * i + j, j)
                                if j:
                                    logits(R * i + j - 1, i, j - 1)
                            logits(R * i + R - 1, i, R - 1)
                        laps(pe, LAPS, lap)

                    @block.scalar
                    def _(act):
                        def lap(i):
                            for j in range(R):
                                t = R * i + j
                                act.wait_ge(z_turned, t + 1)
                                if past(t, 2):
                                    act.wait_ge(l_done, t - 1)
                                nc.scalar.activation(rz[:, j % 2, 0:512], zt[j % 2][:, 0:512], ACT.Relu)
                                nc.scalar.activation(rz[:, j % 2, 512:D], zt[j % 2][:, 512:D], ACT.Relu
                                                     ).then_inc(relu_done, 1)
                        laps(act, LAPS, lap)
                end_stage()

            with ExitStack() as ctx:
                lt = sb("lt", [128, CE], F32, ctx)
                fwd = sb("fwd", [128, CE], F32, ctx)
                bwd = sb("bwd", [128, CE], F32, ctx)
                pen = sb("pen", [128, CE], F32, ctx)
                ends = sb("ends", [128, 2], F32, ctx)
                ends8 = sb("ends8_", [GH, 2 * CH], F32, ctx)
                fwd8 = sb("fwd8_", [GH, 2 * CH], F32, ctx)
                bwd8 = sb("bwd8_", [GH, 2 * CH], F32, ctx)
                tops = sb("tops", [128, 2], F32, ctx)
                blank = sb("blank", [GH, ETP * EP - E], F32, ctx)
                lt_in, v3, ends_ready, ends_out, ends_in, tops_ready, tops_out, tops_in = (
                    sem(n) for n in ("lt_in", "v3_", "ends_ready", "ends_out", "ends_in", "tops_ready",
                                          "tops_out", "tops_in"))
                less_ready, ex_ready, ex_out, blank_ready = (
                    sem("less_ready"), sem("ex_ready"), sem("ex_out"), sem("blank_ready"))

                with nc.Block() as block:
                    @block.sync
                    def _(sp):
                        for g in range(GH):
                            sp.dma_start(lt[g * CH:g * CH + CH, :],
                                         logit_dram[g, 0:E].rearrange("(c e) -> c e", e=CE)).then_inc(lt_in, 16)
                        sp.wait_ge(ends_ready, 1)
                        sp.dma_start(pair_dram, ends[:, :]).then_inc(ends_out, 16)
                        sp.wait_ge(ends_out, 16)
                        sp.dma_start(ends8[:, :], pair_dram.rearrange("(h c) k -> h (c k)", h=GH)).then_inc(ends_in, 16)
                        sp.wait_ge(tops_ready, 1)
                        sp.dma_start(top_dram.rearrange("(h c) k -> h (c k)", h=GH), fwd8[:, :]).then_inc(tops_out, 16)
                        sp.wait_ge(tops_out, 16)
                        sp.dma_start(tops[:, :], top_dram).then_inc(tops_in, 16)
                        sp.wait_ge(blank_ready, 1)
                        sp.dma_start(ex_dram[:, E:], blank[:, :]).then_inc(ex_out, 16)
                        sp.wait_ge(ex_ready, 1)
                        for g in range(GH):
                            sp.dma_start(ex_dram[g, 0:E].rearrange("(c e) -> c e", e=CE),
                                         bwd[g * CH:g * CH + CH, :]).then_inc(ex_out, 16)
                        sp.wait_ge(ex_out, 16 * (GH + 1))

                    @block.scalar
                    def _(act):
                        act.wait_ge(less_ready, 1)
                        nc.scalar.activation(bwd[:, :], fwd[:, :], ACT.Exp).then_inc(ex_ready, 1)

                    @block.vector
                    def _(dve):
                        ch = Chain(dve, v3)
                        nc.vector.memset(blank[:, :], 0.0).then_inc(blank_ready, 1)
                        dve.wait_ge(lt_in, 16 * GH)
                        ch.do(nc.vector.tensor_tensor_scan(fwd[:, :], change[:, 0:CE], lt[:, :], -BIG, ALU.add, ALU.max))
                        ch.do(nc.vector.tensor_tensor_scan(bwd[:, ::-1], change[:, CE:0:-1], lt[:, ::-1], -BIG,
                                                           ALU.add, ALU.max))
                        ch.wait()
                        ch.link(nc.vector.tensor_tensor(fwd[:, :], fwd[:, :], bwd[:, :], ALU.max))
                        ch.do(nc.vector.tensor_copy(ends[:, 0:1], fwd[:, 0:1]))
                        ch.do(nc.vector.tensor_copy(ends[:, 1:2], fwd[:, CE - 1:CE]))
                        ch.wait()
                        dve.sem_inc(ends_ready, 1)
                        dve.wait_ge(ends_in, 16)
                        ch.do(nc.vector.tensor_tensor_scan(fwd8[:, :], change2[:, 0:2 * CH], ends8[:, :], -BIG,
                                                           ALU.add, ALU.max))
                        ch.do(nc.vector.tensor_tensor_scan(bwd8[:, ::-1], change2[:, 2 * CH:0:-1], ends8[:, ::-1], -BIG,
                                                           ALU.add, ALU.max))
                        ch.wait()
                        nc.vector.tensor_tensor(fwd8[:, :], fwd8[:, :], bwd8[:, :], ALU.max).then_inc(tops_ready, 1)
                        dve.wait_ge(tops_in, 16)
                        for k, e in enumerate((0, CE - 1)):
                            ch.link(nc.vector.tensor_scalar(pen[:, :], dstc[:, :], dstc[:, e:e + 1], -BIG,
                                                            ALU.not_equal, ALU.mult))
                            ch.link(nc.vector.scalar_tensor_tensor(out=fwd[:, :], in0=pen[:, :], scalar=tops[:, k:k + 1],
                                                                   in1=fwd[:, :], op0=ALU.add, op1=ALU.max))
                        ch.link(nc.vector.tensor_tensor(fwd[:, :], lt[:, :], fwd[:, :], ALU.subtract))
                        dve.sem_inc(less_ready, 1)
                end_stage()

            with ExitStack() as ctx:
                R = 4
                LAPS = ITEMS // R
                Q = ETP // 4
                acc = sb("acc", [P, NT, DX], F32, ctx)
                gr = sb("gr", [128, R, DX], F32, ctx)
                cur = sb("curb", [128, R], I32, ctx)
                oh = sb("oh", [128, R, P], F32, ctx)
                exr = sb("exr", [GH, 2, Q * EP], F32, ctx)
                exT = sb("exT", [128, ITEMS, GH], F32, ctx)
                sinv = sb("sinv", [P, NT, GH], F32, ctx)
                neg = sb("neg", [P, 2, D], F32, ctx)
                lnw = sb("lnw", [P, D], F32, ctx)
                lnb = sb("lnb", [P, D], F32, ctx)
                temps = norm_temps(ctx, "lng")
                sums = [ps(f"sums{k}_", [128, 2, 512], ctx) for k in range(R)]
                ex_in = [sem(f"ex_in{k}_") for k in range(2)]
                ln_in, ex_turned, ex_taken, v4, v5 = (sem(n) for n in ("ln_in", "ex_turned", "ex_taken", "v4_",
                                                                            "v5_"))
                picked, handed = sem("picked2_"), sem("handed2_")
                got = [sem(f"got2{k}_") for k in range(R)]
                weighed, summed, added, neg_ready, exp_done = (
                    sem(n) for n in ("weighed", "summed", "added", "neg_ready", "exp_done"))

                with nc.Block() as block:
                    @block.sync
                    def _(sp):
                        sp.dma_start(lnw[:, :], spread(a["L0_gnn_ln_w"][bass.ds(l, 1)].rearrange("a d -> (a d)"), P)).then_inc(ln_in, 16)
                        sp.dma_start(lnb[:, :], spread(a["L0_gnn_ln_b"][bass.ds(l, 1)].rearrange("a d -> (a d)"), P)).then_inc(ln_in, 16)
                        for q in range(4):
                            if q >= 2:
                                sp.wait_ge(ex_turned, q - 1)
                            sp.dma_start(exr[:, q % 2, :], ex_dram[:, q * Q * EP:(q + 1) * Q * EP]
                                         ).then_inc(ex_in[q % 2], 16)

                    @block.gpsimd
                    def _(pool):
                        def lap(i):
                            for j in range(R):
                                t = R * i + j
                                if past(t, R):
                                    pool.wait_ge(summed, t - R + 1)
                                nc.gpsimd.tensor_copy(cur[:, j:j + 1], src_item[:, bass.ds(t, 1)]).then_inc(picked, 1)
                                pool.wait_ge(picked, t + 1)
                                pool.sem_inc(handed, 1)
                                nc.gpsimd.indirect_dma_start(
                                    out=gr[:, j, :], out_offset=None, in_=hs_dram,
                                    in_offset=bass.IndirectOffsetOnAxis(ap=cur[:, j:j + 1], axis=0)
                                ).then_inc(got[j], 16)
                        laps(pool, LAPS, lap)

                    @block.tensor
                    def _(pe):
                        for q in range(4):
                            pe.wait_ge(ex_in[q % 2], 16 * (q // 2 + 1))
                            for t in range(Q):
                                ins = nc.tensor.transpose(sums[q][:, 0, t * GH:t * GH + GH],
                                                          exr[:, q % 2, t * EP:t * EP + EP], ident[0:GH, 0:GH])
                            ins.then_inc(ex_turned, 1)
                        pe.wait_ge(ex_taken, 4)

                        def lap(i):
                            for j in range(R):
                                t = R * i + j
                                pe.wait_ge(weighed, 3 * t + 3)
                                if past(t, R):
                                    pe.wait_ge(added, t - R + 1)
                                for k in range(2):
                                    ins = nc.tensor.matmul(sums[j][0:P, k, 0:DX // 2], oh[:, j, :],
                                                           gr[:, j, k * (DX // 2):(k + 1) * (DX // 2)],
                                                           start=True, stop=True)
                                ins.then_inc(summed, 1)
                        laps(pe, LAPS, lap)

                    @block.scalar
                    def _(act):
                        for t in range(NT):
                            act.wait_ge(neg_ready, t + 1)
                            nc.scalar.activation(neg[:, t % 2, :], neg[:, t % 2, :], ACT.Exp).then_inc(exp_done, 1)
                        root(act, temps)

                    @block.vector
                    def _(dve):
                        ch = Chain(dve, v4)
                        ch.do(nc.vector.memset(acc[:, :, :], 0.0))
                        ch.do(nc.vector.memset(exT[:, ETP + NT - 1:, :], 0.0))
                        for q in range(4):
                            dve.wait_ge(ex_turned, q + 1)
                            nc.vector.tensor_copy(exT[:, q * Q:(q + 1) * Q, :],
                                                  sums[q][:, 0, 0:Q * GH].rearrange("p (t h) -> p t h", h=GH)
                                                  ).then_inc(ex_taken, 1)
                        dve.wait_ge(ex_taken, 4)
                        for k in range(NT - 1):
                            t = nc.vector.value_load(cut_tile[0:1, k:k + 1], min_val=0, max_val=ETP - 1)
                            ch.do(nc.vector.tensor_copy(exT[:, ETP + k:ETP + k + 1, :], exT[:, bass.ds(t, 1), :]))
                        ch.wait()

                        def weigh(t, i, j):
                            e = exT[:, bass.ds(t, 1), :]
                            dve.wait_ge(got[j], 16 * (i + 1))
                            g3 = gr[:, j, 0:D].rearrange("p (h d) -> p h d", h=GH)
                            nc.vector.tensor_tensor(
                                g3, g3, e.rearrange("p a h -> p h a").to_broadcast([128, GH, GD]), ALU.mult
                            ).then_inc(weighed, 1)
                            nc.vector.tensor_copy(gr[:, j, D:DX], e.rearrange("p a h -> p (a h)")).then_inc(weighed, 1)
                            nc.vector.tensor_scalar(oh[:, j, :], lanes[:, :], dst_rel[:, bass.ds(t, 1)], None,
                                                    ALU.is_equal).then_inc(weighed, 1)

                        def add(t, j):
                            w = nc.vector.value_load(win[0:1, bass.ds(t, 1)], min_val=0, max_val=NT - 1)
                            dve.wait_ge(summed, t + 1)
                            if past(t, 1):
                                dve.wait_ge(added, t)
                            to = acc[:, bass.ds(w, 1), :].rearrange("p a (k n) -> p (a k) n", k=2)
                            nc.vector.tensor_tensor(to, to, sums[j][0:P, :, 0:DX // 2], ALU.add).then_inc(added, 1)

                        def lap(i):
                            for j in range(R):
                                t = R * i + j
                                weigh(t, i, j)
                                if past(t, 1):
                                    add(t - 1, (j - 1) % R)
                        laps(dve, LAPS, lap)
                        add(ITEMS - 1, R - 1)
                        dve.wait_ge(added, ITEMS)

                        ch = Chain(dve, v5)
                        ch.link(nc.vector.tensor_scalar(sinv[:, :, :], acc[:, :, D:DX], 1e-30, None, ALU.max))
                        ch.link(nc.vector.reciprocal(sinv[:, :, :], sinv[:, :, :]))
                        for t in range(NT):
                            o3 = acc[:, t, 0:D].rearrange("p (h d) -> p h d", h=GH)
                            ch.do(nc.vector.tensor_tensor(o3, o3, sinv[:, t, :].unsqueeze(2).to_broadcast([P, GH, GD]),
                                                          ALU.mult))
                        ch.wait()

                        def elu_tail(t):
                            dve.wait_ge(exp_done, t + 1)
                            ch.link(nc.vector.scalar_tensor_tensor(out=acc[:, t, 0:D], in0=acc[:, t, 0:D], scalar=0.0,
                                                                   in1=neg[:, t % 2, :], op0=ALU.max, op1=ALU.add))
                            ch.do(nc.vector.scalar_tensor_tensor(out=h[:, t, :], in0=acc[:, t, 0:D], scalar=-1.0,
                                                                 in1=h[:, t, :], op0=ALU.add, op1=ALU.add))
                        for t in range(NT):
                            nc.vector.tensor_scalar(neg[:, t % 2, :], acc[:, t, 0:D], 0.0, None, ALU.min
                                                    ).then_inc(neg_ready, 1)
                            if t:
                                elu_tail(t - 1)
                        elu_tail(NT - 1)
                        ch.wait()
                        dve.wait_ge(ln_in, 32)
                        layer_norm(ch, h, h, temps, w=lnw, b=lnb)
                end_stage()

        edge.close()

        with ExitStack() as ctx:
            onw = sb("onw", [P, D], F32, ctx)
            onb = sb("onb", [P, D], F32, ctx)
            temps = norm_temps(ctx, "lno")
            temps2 = norm_temps(ctx, "lny")
            on_in, v6 = sem("on_in"), sem("v6")
            with nc.Block() as block:
                @block.sync
                def _(sp):
                    sp.dma_start(onw[:, :], spread(a["L0_gnn_on_w"], P)).then_inc(on_in, 16)
                    sp.dma_start(onb[:, :], spread(a["L0_gnn_on_b"], P)).then_inc(on_in, 16)

                @block.scalar
                def _(act):
                    root(act, temps)
                    root(act, temps2)

                @block.vector
                def _(dve):
                    ch = Chain(dve, v6)
                    dve.wait_ge(on_in, 32)
                    layer_norm(ch, h, h, temps, w=onw, b=onb)
                    ch.link(nc.vector.tensor_tensor(x[:, :, :], x[:, :, :], h[:, :, :], ALU.add))
                    layer_norm(ch, x, h, temps2)
                    ch.link(nc.vector.tensor_tensor(x[:, :, :], x[:, :, :], h[:, :, :], ALU.add))
            end_stage()

        o = sb("o", [P, NT, D], F32, mid)
        with ExitStack() as ctx:
            w1 = sb("ln1w", [P, D], F32, ctx)
            b1 = sb("ln1b", [P, D], F32, ctx)
            temps = norm_temps(ctx, "ln1")
            tT = sb("tT", [128, KC, N], F32, ctx)
            wp = sb("wp", [128, KC, 3, 128], F32, ctx)
            brow = sb("brow", [3 * KC, 128], F32, ctx)
            bcol = sb("bcol", [128, 3 * KC], F32, ctx)
            bv = sb("bv", [P, D], F32, ctx)
            qT = sb("qT", [128, N], F32, ctx)
            kT = sb("kT", [128, N], F32, ctx)
            v = sb("v", [P, NT, 128], F32, ctx)
            prob = sb("prob", [P, 2, N], F32, ctx)
            pT = sb("pT", [P, 2, 3, 4 * P], F32, ctx)
            bank_high = sb("bank_high", [P, 2, 3], F32, ctx)
            high = sb("high", [P, 2], F32, ctx)
            low = sb("low", [P, 2], F32, ctx)
            part = sb("part", [P, 2, 3], F32, ctx)
            total = sb("total", [P, 2], F32, ctx)
            tinv = sb("tinv", [P, 2], F32, ctx)
            ident_h = sb("ident_h", [P, P], BF16, ctx)
            causal = sb("causal", [P, P], BF16, ctx)
            S = [ps(f"S{k}_", [128, 3, 512], ctx) for k in range(2)]
            O = [ps(f"O{k}_", [128, 512], ctx) for k in range(2)]
            banks = [S[k][:, b, :] for k in range(2) for b in range(3)]
            (ln1_in, v7, normed, turned, taken, brow_in, b_turned, b_taken, bv_in, masks, w_in, qk_done, v_done,
             qk_taken, v_taken, s_done, low_ready, p_ready, p_turned, pt_act, pt_dve, o_done, o_taken, v8) = (
                sem(n) for n in ("ln1_in", "v7", "t_normed", "t_turned", "t_taken", "brow_in", "b_turned",
                                 "b_taken", "bv_in", "masks", "wp_in", "qk_done", "v_done", "qk_taken",
                                 "v_taken", "s_done", "low_ready", "p_ready", "p_turned", "pt_act", "pt_dve",
                                 "o_done", "o_taken", "v8"))
            IT = 2 * NT
            CHUNKS = [(0, 500), (500, 500), (1000, 250)]
            qkv_w = a["L0_ffn_attn_qkv_w"].rearrange("(c p) (k n) -> p c k n", p=128, k=3)

            def groups(n):
                qi = n % NT
                return [(b, min(4, qi + 1 - 4 * b)) for b in range((qi + 4) // 4)]

            SMALL = sum(len(groups(n)) + 2 for n in range(IT))

            with nc.Block() as block:
                @block.sync
                def _(sp):
                    sp.dma_start(w1[:, :], spread(a["L0_ffn_ln1_w"], P)).then_inc(ln1_in, 16)
                    sp.dma_start(b1[:, :], spread(a["L0_ffn_ln1_b"], P)).then_inc(ln1_in, 16)
                    sp.dma_start(brow[:, :], a["L0_ffn_attn_qkv_b"].rearrange("(c p) -> c p", p=128)
                                 ).then_inc(brow_in, 16)
                    sp.dma_start(bv[:, :], spread(a["L0_ffn_attn_qkv_b"][2 * D:3 * D], P)).then_inc(bv_in, 16)

                    def lap(i):
                        if past(i, 1):
                            sp.wait_ge(v_done, 3 * i)
                        for k in range(3):
                            sp.dma_start(wp[:, :, k, :], qkv_w[:, :, k, bass.ds(i * 128, 128)]).then_inc(w_in, 16)
                    laps(sp, PAIRS, lap)

                @block.gpsimd
                def _(pool):
                    nc.gpsimd.memset(ident_h[:, :], 0.0).then_inc(masks, 1)
                    nc.gpsimd.memset(causal[:, :], 0.0).then_inc(masks, 1)
                    pool.wait_ge(masks, 2)
                    nc.gpsimd.affine_select(out=ident_h[:, :], in_=ident_h[:, :], compare_op=ALU.not_equal, fill=1.0,
                                            base=0, pattern=[[-1, P]], channel_multiplier=1).then_inc(masks, 1)
                    nc.gpsimd.affine_select(out=causal[:, :], in_=causal[:, :], compare_op=ALU.is_ge, fill=-BIG,
                                            base=0, pattern=[[-1, P]], channel_multiplier=1).then_inc(masks, 1)

                @block.tensor
                def _(pe):
                    pe.wait_ge(normed, 1)
                    turn_pe(pe, o, banks, turned, taken)
                    pe.wait_ge(taken, TURNS)
                    pe.wait_ge(brow_in, 16)
                    nc.tensor.transpose(O[0][:, 0:3 * KC], brow[:, :], ident[0:3 * KC, 0:3 * KC]).then_inc(b_turned, 1)
                    pe.wait_ge(masks, 4)
                    pe.wait_ge(b_taken, 1)

                    def scores(n):
                        r, qi = 64 * (n // NT), n % NT
                        for b, m in groups(n):
                            nc.tensor.matmul(S[n % 2][0:P, b, 0:m * P], qT[r:r + 64, qi * P:qi * P + P],
                                             kT[r:r + 64, 4 * b * P:(4 * b + m) * P], start=True,
                                             stop=(b != qi // 4))
                        nc.tensor.matmul(S[n % 2][0:P, qi // 4, (qi % 4) * P:(qi % 4) * P + P], ident_h[:, :],
                                         causal[:, :], start=False, stop=True).then_inc(s_done, 1)

                    def lap(i):
                        pe.wait_ge(w_in, 48 * (i + 1))
                        for k in range(2):
                            for b, (s, m) in enumerate(CHUNKS):
                                for c in range(KC):
                                    ins = nc.tensor.matmul(S[k][:, b, 0:m], wp[:, c, k, :], tT[:, c, s:s + m],
                                                           start=(c == 0), stop=(c == KC - 1))
                            ins.then_inc(qk_done, 1)
                        pe.wait_ge(qk_taken, 6 * i + 3)
                        for b, (t0, m) in enumerate(GROUPS):
                            for t in range(m):
                                for c in range(KC):
                                    ins = nc.tensor.matmul(S[0][0:P, b, t * 128:t * 128 + 128],
                                                           tT[:, c, (t0 + t) * P:(t0 + t) * P + P], wp[:, c, 2, :],
                                                           start=(c == 0), stop=(c == KC - 1))
                            ins.then_inc(v_done, 1)
                        pe.wait_ge(qk_taken, 6 * i + 6)
                        pe.wait_ge(v_taken, 3 * i + 3)
                        scores(0)
                        for n in range(IT + 1):
                            if n + 1 < IT:
                                if n >= 1:
                                    pe.wait_ge(pt_act, IT * i + n)
                                    pe.wait_ge(pt_dve, IT * i + n)
                                scores(n + 1)
                            if n < IT:
                                pe.wait_ge(p_ready, IT * i + n + 1)
                                for b, m in groups(n):
                                    for t in range(m):
                                        ins = nc.tensor.transpose(
                                            S[n % 2][0:P, b, t * P:t * P + P],
                                            prob[:, n % 2, (4 * b + t) * P:(4 * b + t + 1) * P], ident[0:P, 0:P])
                                ins.then_inc(p_turned, 1)
                            if n >= 1:
                                m = n - 1
                                hh, qi = m // NT, m % NT
                                pe.wait_ge(pt_act, IT * i + m + 1)
                                pe.wait_ge(pt_dve, IT * i + m + 1)
                                if m >= 2 or past(i, 1):
                                    pe.wait_ge(o_taken, IT * i + m - 1)
                                for t in range(qi + 1):
                                    ins = nc.tensor.matmul(O[m % 2][0:P, 0:HD],
                                                           pT[:, m % 2, t // 4, (t % 4) * P:(t % 4) * P + P],
                                                           v[:, t, HD * hh:HD * hh + HD], start=(t == 0),
                                                           stop=(t == qi))
                                ins.then_inc(o_done, 1)
                    laps(pe, PAIRS, lap)

                @block.scalar
                def _(act):
                    root(act, temps)
                    turn_act(act, tT, banks, turned, taken)
                    act.wait_ge(b_taken, 1)

                    def lap(i):
                        for k, to in enumerate((qT, kT)):
                            act.wait_ge(qk_done, 2 * i + k + 1)
                            for b, (s, m) in enumerate(CHUNKS):
                                nc.scalar.activation(to[:, s:s + m], S[k][:, b, 0:m], ACT.Identity,
                                                     bias=bcol[:, bass.ds(i + k * KC, 1)]).then_inc(qk_taken, 1)
                        for n in range(IT + 1):
                            if n < IT:
                                act.wait_ge(low_ready, IT * i + n + 1)
                                if n >= 2 or past(i, 1):
                                    act.wait_ge(p_turned, IT * i + n - 1)
                                    act.wait_ge(pt_dve, IT * i + n - 1)
                                for b, m in groups(n):
                                    ins = nc.scalar.activation(prob[:, n % 2, 4 * b * P:(4 * b + m) * P],
                                                               S[n % 2][0:P, b, 0:m * P], ACT.Exp,
                                                               bias=low[:, n % 2:n % 2 + 1], scale=HD ** -0.5,
                                                               accum_out=part[:, n % 2, b:b + 1])
                                ins.then_inc(p_ready, 1)
                            if n >= 1:
                                m = n - 1
                                act.wait_ge(p_turned, IT * i + m + 1)
                                if m >= 2 or past(i, 1):
                                    act.wait_ge(o_done, IT * i + m - 1)
                                k = groups(m)[0][1] * P
                                nc.scalar.copy(pT[:, m % 2, 0, 0:k], S[m % 2][0:P, 0, 0:k]).then_inc(pt_act, 1)
                    laps(act, PAIRS, lap)

                @block.vector
                def _(dve):
                    ch = Chain(dve, v7)
                    dve.wait_ge(ln1_in, 32)
                    layer_norm(ch, h, o, temps, w=w1, b=b1)
                    dve.sem_inc(normed, 1)
                    dve.wait_ge(b_turned, 1)
                    nc.vector.tensor_copy(bcol[:, :], O[0][:, 0:3 * KC]).then_inc(b_taken, 1)
                    dve.wait_ge(bv_in, 16)

                    def lap(i):
                        for b, (t0, m) in enumerate(GROUPS):
                            dve.wait_ge(v_done, 3 * i + b + 1)
                            nc.vector.tensor_tensor(
                                v[:, t0:t0 + m, :], S[0][0:P, b, 0:m * 128].rearrange("p (t n) -> p t n", n=128),
                                bv[:, bass.ds(i * 128, 128)].unsqueeze(1).to_broadcast([P, m, 128]), ALU.add
                            ).then_inc(v_taken, 1)
                        small = Chain(dve, v8, base=SMALL * i)
                        for n in range(IT + 2):
                            if n < IT:
                                k = n % 2
                                dve.wait_ge(s_done, IT * i + n + 1)
                                for b, m in groups(n):
                                    small.do(nc.vector.tensor_reduce(bank_high[:, k, b:b + 1],
                                                                     S[k][0:P, b, 0:m * P], AX.X, ALU.max))
                                small.wait()
                                small.link(nc.vector.tensor_reduce(high[:, k:k + 1],
                                                                   bank_high[:, k, 0:len(groups(n))], AX.X, ALU.max))
                                if n >= 2 or past(i, 1):
                                    dve.wait_ge(p_ready, IT * i + n - 1)
                                nc.vector.tensor_scalar(low[:, k:k + 1], high[:, k:k + 1], -HD ** -0.5, None,
                                                        ALU.mult).then_inc(low_ready, 1)
                            if 1 <= n <= IT:
                                m, k = n - 1, (n - 1) % 2
                                dve.wait_ge(p_turned, IT * i + m + 1)
                                if m >= 2 or past(i, 1):
                                    dve.wait_ge(o_done, IT * i + m - 1)
                                for b, c in groups(m)[1:]:
                                    nc.vector.tensor_copy(pT[:, k, b, 0:c * P], S[k][0:P, b, 0:c * P])
                                nc.vector.tensor_reduce(total[:, k:k + 1], part[:, k, 0:len(groups(m))], AX.X,
                                                        ALU.add).then_inc(pt_dve, 1)
                            if n >= 2:
                                m, k = n - 2, n % 2
                                dve.wait_ge(pt_dve, IT * i + m + 1)
                                small.link(nc.vector.reciprocal(tinv[:, k:k + 1], total[:, k:k + 1]))
                                dve.wait_ge(o_done, IT * i + m + 1)
                                nc.vector.tensor_scalar(o[:, m % NT, bass.ds(i * 128 + HD * (m // NT), HD)],
                                                        O[k][0:P, 0:HD], tinv[:, k:k + 1], None,
                                                        ALU.mult).then_inc(o_taken, 1)
                        assert small.n == SMALL
                    laps(dve, PAIRS, lap)
            end_stage()

        with ExitStack() as ctx:
            oT = sb("oT", [128, KC, N], F32, ctx)
            wo = sb("wo", [128, KC, D], F32, ctx)
            bo = sb("bo", [P, D], F32, ctx)
            w2 = sb("ln2w", [P, D], F32, ctx)
            b2 = sb("ln2b", [P, D], F32, ctx)
            row = sb("row", [P, D], F32, ctx)
            temps = norm_temps(ctx, "ln2")
            bank = [ps(f"pr{k}_", [128, 512], ctx) for k in range(8)]
            wo_in, b_in, turned, taken, done, v9 = (
                sem(n) for n in ("wo_in", "bo_in", "o_turned", "oT_taken", "proj_done", "v9"))
            with nc.Block() as block:
                @block.sync
                def _(sp):
                    sp.dma_start(wo[:, :, :], a["L0_ffn_attn_proj_w"].rearrange("(c p) n -> p c n", p=128)
                                 ).then_inc(wo_in, 16)
                    sp.dma_start(bo[:, :], spread(a["L0_ffn_attn_proj_b"], P)).then_inc(b_in, 16)
                    sp.dma_start(w2[:, :], spread(a["L0_ffn_ln2_w"], P)).then_inc(b_in, 16)
                    sp.dma_start(b2[:, :], spread(a["L0_ffn_ln2_b"], P)).then_inc(b_in, 16)

                @block.tensor
                def _(pe):
                    turn_pe(pe, o, bank, turned, taken)
                    pe.wait_ge(taken, TURNS)
                    pe.wait_ge(wo_in, 16)
                    for t in range(NT):
                        if t >= 4:
                            pe.wait_ge(v9, 3 * (t - 4) + 1)
                        for k in range(2):
                            for c in range(KC):
                                ins = nc.tensor.matmul(bank[2 * (t % 4) + k][0:P, 0:384], oT[:, c, t * P:t * P + P],
                                                       wo[:, c, 384 * k:384 * k + 384], start=(c == 0),
                                                       stop=(c == KC - 1))
                        ins.then_inc(done, 1)

                @block.scalar
                def _(act):
                    turn_act(act, oT, bank, turned, taken)
                    root(act, temps)

                @block.vector
                def _(dve):
                    ch = Chain(dve, v9)
                    dve.wait_ge(b_in, 48)
                    for t in range(NT):
                        dve.wait_ge(done, t + 1)
                        nc.vector.tensor_tensor(row[:, 0:384], bank[2 * (t % 4)][0:P, 0:384], bo[:, 0:384], ALU.add)
                        ch.link(nc.vector.tensor_tensor(row[:, 384:D], bank[2 * (t % 4) + 1][0:P, 0:384],
                                                        bo[:, 384:D], ALU.add))
                        ch.do(nc.vector.tensor_tensor(h[:, t, :], h[:, t, :], row[:, :], ALU.add))
                        ch.do(nc.vector.tensor_tensor(x[:, t, :], x[:, t, :], row[:, :], ALU.add))
                        ch.wait()
                    dve.wait_ge(turned, TURNS)
                    layer_norm(ch, h, o, temps, w=w2, b=b2)
            end_stage()

        with ExitStack() as ctx:
            uT = sb("uT", [128, KC, N], F32, ctx)
            wg = sb("wg", [128, KC, NX], F32, ctx)
            tri = sb("tri", [P, P], F32, ctx)
            expert = sb("expert", [P, NX], F32, ctx)
            spare = sb("spare", [P, 2 * NT], F32, ctx)
            lgt = sb("lgt", [P, NT, NX], F32, ctx)
            best = sb("best", [P, NT, NX], F32, ctx)
            which = sb("which", [P, NT, NX], U32, ctx)
            which_f = sb("which_f", [P, 2, NT], F32, ctx)
            gap = sb("gap", [P, NT], F32, ctx)
            prob0 = sb("prob0", [P, 2, NT], F32, ctx)
            hot = sb("hot", [P, 2, NT, NX], F32, ctx)
            base = sb("base", [P, 2 * NT, NX], F32, ctx)
            tot = sb("tot", [P, 2 * NT, NX], F32, ctx)
            rank = sb("rank", [P, 2 * NT], F32, ctx)
            keep = sb("keep", [P, 2 * NT], F32, ctx)
            slot = sb("slot", [P, 2 * NT], F32, ctx)
            slot_write = sb("slot_write", [P, 2 * NT], I32, ctx)
            bank = [ps(f"ro{k}_", [128, 512], ctx) for k in range(4)]
            lg_p = ps("lg_p", [128, 512], ctx)
            cum_p = ps("cum_p", [128, 512], ctx)
            tot_p = ps("tot_p", [128, 512], ctx)
            turned, taken, wg_in, made, lg_done, gap_ready, exp_done, hot_ready, counted, v10, slots_ready, sent = (
                sem(n) for n in ("u_turned", "uT_taken", "wg_in", "made", "lg_done", "gap_ready", "gap_exp",
                                 "hot_ready", "counted", "v10", "slots_ready", "sent"))
            with nc.Block() as block:
                @block.sync
                def _(sp):
                    sp.dma_start(wg[:, :, :], a["L0_ffn_w_g"].rearrange("(c p) e -> p c e", p=128)).then_inc(wg_in, 16)

                @block.gpsimd
                def _(pool):
                    nc.gpsimd.memset(tri[:, :], 1.0).then_inc(made, 1)
                    nc.gpsimd.iota(expert[:, :], [[1, NX]], base=0, channel_multiplier=0,
                                   allow_small_or_imprecise_dtypes=True).then_inc(made, 1)
                    nc.gpsimd.iota(spare[:, :], [[P, 2 * NT]], base=SLOTS, channel_multiplier=1,
                                   allow_small_or_imprecise_dtypes=True).then_inc(made, 1)
                    pool.wait_ge(made, 3)
                    nc.gpsimd.affine_select(out=tri[:, :], in_=tri[:, :], compare_op=ALU.is_ge, fill=0.0, base=0,
                                            pattern=[[1, P]], channel_multiplier=-1).then_inc(made, 1)
                    pool.wait_ge(slots_ready, 1)
                    for k in range(2):
                        for t in range(NT):
                            b = k * NT + t
                            nc.gpsimd.indirect_dma_start(
                                out=slot_in, in_=o[:, t, :], in_offset=None,
                                out_offset=bass.IndirectOffsetOnAxis(ap=slot_write[:, b:b + 1], axis=0)
                            ).then_inc(sent, 16)
                    pool.wait_ge(sent, 32 * NT)

                @block.tensor
                def _(pe):
                    turn_pe(pe, o, bank, turned, taken)
                    pe.wait_ge(taken, TURNS)
                    pe.wait_ge(wg_in, 16)
                    for t in range(NT):
                        for c in range(KC):
                            ins = nc.tensor.matmul(lg_p[0:P, t * NX:t * NX + NX], uT[:, c, t * P:t * P + P],
                                                   wg[:, c, :], start=(c == 0), stop=(c == KC - 1))
                    ins.then_inc(lg_done, 1)
                    pe.wait_ge(made, 4)
                    pe.wait_ge(hot_ready, 2)
                    all_hot = hot[:, :, :, :].rearrange("p k t e -> p (k t e)")
                    nc.tensor.matmul(cum_p[0:P, 0:2 * NT * NX], tri[:, :], all_hot, start=True, stop=True
                                     ).then_inc(counted, 1)
                    nc.tensor.matmul(tot_p[0:P, 0:2 * NT * NX], ones[0:P, 0:P], all_hot, start=True, stop=True
                                     ).then_inc(counted, 1)

                @block.scalar
                def _(act):
                    turn_act(act, uT, bank, turned, taken)
                    act.wait_ge(gap_ready, 1)
                    nc.scalar.activation(gap[:, :], gap[:, :], ACT.Exp).then_inc(exp_done, 1)

                @block.vector
                def _(dve):
                    ch = Chain(dve, v10)
                    dve.wait_ge(lg_done, 1)
                    ch.link(nc.vector.tensor_copy(lgt[:, :, :], lg_p[0:P, 0:NT * NX].rearrange("p (t e) -> p t e", e=NX)))
                    for t in range(NT):
                        ch.do(nc.vector.max(best[:, t, :], lgt[:, t, :]))
                    ch.wait()
                    for t in range(NT):
                        ch.do(nc.vector.max_index(which[:, t, :], best[:, t, :], lgt[:, t, :]))
                    ch.wait()
                    nc.vector.tensor_tensor(gap[:, :], best[:, :, 1], best[:, :, 0], ALU.subtract).then_inc(gap_ready, 1)
                    for k in range(2):
                        ch.do(nc.vector.tensor_copy(which_f[:, k, :], which[:, :, k]))
                    ch.wait()
                    dve.wait_ge(made, 3)
                    for k in range(2):
                        nc.vector.tensor_tensor(hot[:, k, :, :], expert[:, :].unsqueeze(1).to_broadcast([P, NT, NX]),
                                                which_f[:, k, :].unsqueeze(2).to_broadcast([P, NT, NX]),
                                                ALU.is_equal).then_inc(hot_ready, 1)
                    dve.wait_ge(exp_done, 1)
                    ch.link(nc.vector.tensor_scalar(prob0[:, 0, :], gap[:, :], 1.0, None, ALU.add))
                    ch.link(nc.vector.reciprocal(prob0[:, 0, :], prob0[:, 0, :]))
                    ch.link(nc.vector.tensor_tensor(prob0[:, 1, :], prob0[:, 0, :], gap[:, :], ALU.mult))
                    dve.wait_ge(counted, 2)
                    ch.do(nc.vector.tensor_copy(tot[:, :, :], tot_p[0:P, 0:2 * NT * NX]
                                                .rearrange("p (b e) -> p b e", e=NX)))
                    ch.do(nc.vector.memset(base[:, 0, :], 0.0))
                    ch.wait()
                    for b in range(1, 2 * NT):
                        ch.link(nc.vector.tensor_tensor(base[:, b, :], base[:, b - 1, :], tot[:, b - 1, :], ALU.add))
                    ch.link(nc.vector.tensor_tensor(base[:, :, :], base[:, :, :], cum_p[0:P, 0:2 * NT * NX]
                                                    .rearrange("p (b e) -> p b e", e=NX), ALU.add))
                    ch.link(nc.vector.tensor_tensor(base[:, :, :], base[:, :, :],
                                                    hot[:, :, :, :].rearrange("p k t e -> p (k t) e"), ALU.mult))
                    ch.link(nc.vector.tensor_reduce(rank[:, :], base[:, :, :], AX.X, ALU.add))
                    ch.link(nc.vector.tensor_scalar(keep[:, :], rank[:, :], float(CAP), None, ALU.is_le))
                    ch.link(nc.vector.scalar_tensor_tensor(out=slot[:, :], scalar=float(CAP), in1=rank[:, :],
                                                           in0=which_f[:, :, :].rearrange("p k t -> p (k t)"),
                                                           op0=ALU.mult, op1=ALU.add))
                    ch.link(nc.vector.tensor_scalar(slot[:, :], slot[:, :], -1.0, None, ALU.add))
                    ch.link(nc.vector.tensor_tensor(rank[:, :], slot[:, :], keep[:, :], ALU.mult))
                    ch.do(nc.vector.tensor_copy(slot_read[:, :], rank[:, :]))
                    ch.do(nc.vector.tensor_tensor(wgt[:, :], prob0[:, :, :].rearrange("p k t -> p (k t)"),
                                                  keep[:, :], ALU.mult))
                    ch.do(nc.vector.tensor_tensor(slot[:, :], slot[:, :], spare[:, :], ALU.subtract))
                    ch.wait()
                    ch.link(nc.vector.tensor_tensor(slot[:, :], slot[:, :], keep[:, :], ALU.mult))
                    ch.link(nc.vector.tensor_tensor(slot[:, :], slot[:, :], spare[:, :], ALU.add))
                    nc.vector.tensor_copy(slot_write[:, :], slot[:, :]).then_inc(slots_ready, 1)
            end_stage()

        mid.close()

        with ExitStack() as ctx:
            R = 3
            FW = FJ * 128
            TILES = FG * FJ
            wf = sb("wf", [128, R, KC, FW], F32, ctx)
            wj = sb("wj", [128, R, FJ, D], F32, ctx)
            wf_part = [sb(f"wf_{n}", [128, 2, KC, FW], F32R, ctx) for n in ("high", "low")]
            wj_part = [sb(f"wj_{n}", [128, 2, FJ, D], F32R, ctx) for n in ("high", "low")]
            xT_part = [sb(f"xT_{n}", [128, KC, CAP], F32R, ctx) for n in ("high", "low")]
            hid_part = [sb(f"hid_{n}", [128, 2, FJ, CAP], F32R, ctx) for n in ("high", "low")]
            hid = sb("hid", [128, 2, CAP], F32, ctx)
            xs = sb("xs", [128, 3, D], F32, ctx)
            xs3 = sb("xs3", [6, D], F32, ctx)
            yT = sb("yT", [128, KC, CAP], F32, ctx)
            ys = sb("ys", [128, 3, D], F32, ctx)
            ys3 = sb("ys3", [6, D], F32, ctx)
            fb_rows = sb("fb_rows", [96, 2, 128], F32, ctx)
            jb_rows = sb("jb_rows", [48, 128], F32, ctx)
            fb = sb("fb", [128, NX * TILES], F32, ctx)
            jb = sb("jb", [128, NX * KC], F32, ctx)
            ring = [ps(f"ring{k}_", [128, 512], ctx) for k in range(2)]
            accu = [ps(f"accu{k}_", [128, 512], ctx) for k in range(KC)]
            wf_in = [sem(f"wf_in{k}") for k in range(R)]
            wj_in = [sem(f"wj_in{k}") for k in range(R)]
            (bias_in, bias_turned, bias_taken, xs_in, loads, stores, wf_high, wf_split, wj_high, wj_split, x_turned,
             x_high, x_split, up_done, up_taken, hid_high, hid_split, pj_done, y_taken, y_turned, y_rows, stored) = (
                sem(n) for n in ("bias_in", "bias_turned", "bias_taken", "xs_in", "loads", "stores", "wf_high",
                                 "wf_split", "wj_high", "wj_split", "x_turned", "x_high", "x_split", "up_done",
                                 "up_taken", "hid_high", "hid_split", "pj_done", "y_taken", "y_turned", "y_rows",
                                 "stored"))
            YU = 2 * len(ROWS)
            LAP = ([("up", i) for i in range(2 * FJ)] + [("y", i) for i in range(YU // 2)]
                   + [("up", i) for i in range(2 * FJ, 3 * FJ)] + [("y", i) for i in range(YU // 2, YU)]
                   + [("up", i) for i in range(3 * FJ, TILES)] + [("x", i) for i in range(KC)])
            fc_w = a["L0_ffn_exp_fc_w"].rearrange("e (c p) f -> p (e c) f", p=128)
            pj_w = a["L0_ffn_exp_proj_w"].rearrange("e (j p) d -> p (e j) d", p=128)

            def rows_of(big, small, s0, n):
                return big[:, s0 // 128, :] if n == 128 else small[:, :]

            def expert_laps(eng, body):
                body(0, False)
                with eng.Fori(1, NX - 1) as e:
                    body(e, False)
                body(NX - 1, True)

            with nc.Block() as block:
                @block.sync
                def _(sp):
                    fbr = a["L0_ffn_exp_fc_b"].rearrange("e a (g p) -> (e a g) p", p=128)
                    for k in range(2):
                        sp.dma_start(fb_rows[:, k, :], fbr[96 * k:96 * k + 96, :]).then_inc(bias_in, 16)
                    sp.dma_start(jb_rows[:, :], a["L0_ffn_exp_proj_b"].rearrange("e a (c p) -> (e a c) p", p=128)
                                 ).then_inc(bias_in, 16)

                    def lap(e):
                        for g in range(FG):
                            if g >= R or past(e, 1):
                                sp.wait_ge(wf_split, FG * e + g - R + 1)
                            sp.dma_start(wf[:, g % R, :, :], fc_w[:, bass.ds(e * KC, KC), g * FW:(g + 1) * FW]
                                         ).then_inc(wf_in[g % R], 16)
                            if g >= R or past(e, 1):
                                sp.wait_ge(wj_split, FG * e + g - R + 1)
                            sp.dma_start(wj[:, g % R, :, :], pj_w[:, bass.ds(e * TILES + g * FJ, FJ), :]
                                         ).then_inc(wj_in[g % R], 16)
                    laps(sp, NX, lap)

                @block.gpsimd
                def _(pool):
                    def load(e):
                        pool.dma_start(xs[:, :, :], slot_in[bass.ds(e * CAP, 384), :]
                                       .rearrange("(k p) d -> p k d", p=128)).then_inc(xs_in, 16)
                        pool.dma_start(xs3[:, :], slot_in[bass.ds(e * CAP + 384, 6), :]).then_inc(xs_in, 16)

                    def store(e):
                        pool.wait_ge(y_rows, YU * e + YU)
                        pool.sem_inc(stores, 1)
                        pool.dma_start(slot_out[bass.ds(e * CAP, 384), :].rearrange("(k p) d -> p k d", p=128),
                                       ys[:, :, :]).then_inc(stored, 16)
                        pool.dma_start(slot_out[bass.ds(e * CAP + 384, 6), :], ys3[:, :]).then_inc(stored, 16)

                    load(0)
                    pool.wait_ge(x_turned, KC)
                    pool.sem_inc(loads, 1)
                    load(1)
                    with pool.Fori(1, NX - 1) as e:
                        store(e - 1)
                        pool.wait_ge(x_turned, KC * e + KC)
                        pool.sem_inc(loads, 1)
                        load(e + 1)
                    store(NX - 2)
                    store(NX - 1)
                    pool.wait_ge(stored, 32 * NX)

                @block.tensor
                def _(pe):
                    pe.wait_ge(bias_in, 48)
                    for k in range(2):
                        nc.tensor.transpose(accu[k][:, 0:96], fb_rows[:, k, :], ident[0:96, 0:96]
                                            ).then_inc(bias_turned, 1)
                    nc.tensor.transpose(accu[2][:, 0:48], jb_rows[:, :], ident[0:48, 0:48]).then_inc(bias_turned, 1)
                    pe.wait_ge(bias_taken, 3)

                    def product(bank, weights, moving, start, stop):
                        for k, (p, q) in enumerate(((0, 0), (0, 1), (1, 0))):
                            ins = nc.tensor.matmul(bank, weights[p], moving[q], start=(start and k == 0),
                                                   stop=(stop and k == 2))
                        return ins

                    def turn_in(e, c, bank):
                        pe.wait_ge(xs_in, 32 * (e + 1))
                        for s0, n in ROWS:
                            ins = nc.tensor.transpose(bank[:, s0:s0 + n],
                                                      rows_of(xs, xs3, s0, n)[:, c * 128:c * 128 + 128],
                                                      ident[0:n, 0:n])
                        ins.then_inc(x_turned, 1)

                    def turn_out(i, bank):
                        s0, n = ROWS[i // 2]
                        for c in range(3):
                            ins = nc.tensor.transpose(bank[0:n, c * 128:c * 128 + 128],
                                                      yT[:, 3 * (i % 2) + c, s0:s0 + n], ident[:, :])
                        ins.then_inc(y_turned, 1)

                    def lap(e, last):
                        first = not past(e, 1)
                        uses = [use for use in LAP if not (first and use[0] == "y") and not (last and use[0] == "x")]
                        taken_by = {"up": (up_taken, TILES * e), "y": (y_rows, YU * e - YU),
                                    "x": (x_split, KC * e + KC)}
                        step = iter(range(len(uses)))

                        def claim():
                            u = next(step)
                            if u >= 2:
                                kind, i = uses[u - 2]
                                signal, base = taken_by[kind]
                                pe.wait_ge(signal, base + i + 1)
                            return ring[u % 2]

                        def up(g):
                            pe.wait_ge(wf_split, FG * e + g + 1)
                            for j in range(FJ):
                                bank = claim()
                                for c in range(KC):
                                    ins = product(bank[:, 0:CAP],
                                                  [w[:, g % 2, c, j * 128:j * 128 + 128] for w in wf_part],
                                                  [xT[:, c, :] for xT in xT_part], c == 0, c == KC - 1)
                                ins.then_inc(up_done, 1)

                        def down(g, turns):
                            pe.wait_ge(wj_split, FG * e + g + 1)
                            pe.wait_ge(hid_split, TILES * e + (g + 1) * FJ)
                            if g == 0 and past(e, 1):
                                pe.wait_ge(y_taken, KC * e)
                            for j in range(FJ):
                                for c in range(KC):
                                    ins = product(accu[c][:, 0:CAP],
                                                  [w[:, g % 2, j, c * 128:c * 128 + 128] for w in wj_part],
                                                  [part[:, g % 2, j, :] for part in hid_part],
                                                  g == 0 and j == 0, g == FG - 1 and j == FJ - 1)
                                    if j == FJ - 1 and c == KC - 1:
                                        ins.then_inc(pj_done, 1)
                                    if c % 2 == 1 and turns:
                                        turns.pop(0)()
                            assert not turns

                        pe.wait_ge(x_split, KC * e + KC)
                        for g in range(FG):
                            up(g)
                            if g in (1, 2) and not first:
                                down(g - 1, [lambda i=i: turn_out(i, claim())
                                             for i in range((g - 1) * YU // 2, g * YU // 2)])
                            elif g:
                                down(g - 1, [])
                        down(FG - 1, [] if last else [lambda c=c: turn_in(e + 1, c, claim()) for c in range(KC)])

                    for c in range(KC):
                        if c >= 2:
                            pe.wait_ge(x_split, c - 1)
                        turn_in(0, c, ring[c % 2])
                    expert_laps(pe, lap)
                    pe.wait_ge(y_taken, KC * NX)
                    pe.wait_ge(up_taken, TILES * NX)
                    for i in range(YU):
                        if i >= 2:
                            pe.wait_ge(y_rows, YU * (NX - 1) + i - 1)
                        turn_out(i, ring[i % 2])

                @block.scalar
                def _(act):
                    act.wait_ge(bias_taken, 3)

                    def lap(e, last):
                        def high_fc(g):
                            act.wait_ge(wf_in[g % R], 16 * (FG // R * e + g // R + 1))
                            if g >= 2 or past(e, 1):
                                act.wait_ge(up_done, TILES * e + (g - 1) * FJ)
                            nc.scalar.activation(wf_part[0][:, g % 2, :, :], wf[:, g % R, :, :], ACT.Copy
                                                 ).then_inc(wf_high, 1)

                        if not past(e, 1):
                            high_fc(0)
                        for g in range(FG):
                            if not (last and g == FG - 1):
                                high_fc(g + 1)
                            act.wait_ge(wj_in[g % R], 16 * (FG // R * e + g // R + 1))
                            if g >= 2 or past(e, 1):
                                act.wait_ge(pj_done, FG * e + g - 1)
                            nc.scalar.activation(wj_part[0][:, g % 2, :, :], wj[:, g % R, :, :], ACT.Copy
                                                 ).then_inc(wj_high, 1)
                            for j in range(FJ):
                                i = g * FJ + j
                                act.wait_ge(up_done, TILES * e + i + 1)
                                if i >= 2 or past(e, 1):
                                    act.wait_ge(hid_split, TILES * e + i - 1)
                                nc.scalar.activation(hid[:, i % 2, :], ring[i % 2][:, 0:CAP], ACT.Gelu,
                                                     bias=fb[:, bass.ds(e * TILES + i, 1)]).then_inc(up_taken, 1)
                    expert_laps(act, lap)

                @block.vector
                def _(dve):
                    dve.wait_ge(bias_turned, 3)
                    for k in range(2):
                        nc.vector.tensor_copy(fb[:, 96 * k:96 * k + 96], accu[k][:, 0:96]).then_inc(bias_taken, 1)
                    nc.vector.tensor_copy(jb[:, :], accu[2][:, 0:48]).then_inc(bias_taken, 1)
                    dve.wait_ge(bias_taken, 3)

                    def low(dest, source, high):
                        return nc.vector.tensor_tensor(dest, source, high.bitcast(F32), ALU.subtract)

                    def split_slots(e, c):
                        dve.wait_ge(x_turned, KC * e + c + 1)
                        nc.vector.tensor_copy(xT_part[0][:, c, :], ring[c % 2][:, 0:CAP]).then_inc(x_high, 1)
                        dve.wait_ge(x_high, KC * e + c + 1)
                        low(xT_part[1][:, c, :], ring[c % 2][:, 0:CAP], xT_part[0][:, c, :]).then_inc(x_split, 1)

                    def take_sums(e):
                        dve.wait_ge(pj_done, FG * e + FG)
                        for c in range(KC):
                            nc.vector.tensor_scalar(yT[:, c, :], accu[c][:, 0:CAP], jb[:, bass.ds(e * KC + c, 1)],
                                                    None, ALU.add).then_inc(y_taken, 1)

                    def take_rows(e, i):
                        s0, n = ROWS[i // 2]
                        dve.wait_ge(y_turned, YU * e + i + 1)
                        nc.vector.tensor_copy(rows_of(ys, ys3, s0, n)[:, 384 * (i % 2):384 * (i % 2) + 384],
                                              ring[i % 2][0:n, 0:384]).then_inc(y_rows, 1)

                    def lap(e, last):
                        def low_fc(g):
                            dve.wait_ge(wf_high, FG * e + g + 1)
                            low(wf_part[1][:, g % 2, :, :], wf[:, g % R, :, :], wf_part[0][:, g % 2, :, :]
                                ).then_inc(wf_split, 1)

                        if not past(e, 1):
                            low_fc(0)
                        for g in range(FG):
                            if not (last and g == FG - 1):
                                low_fc(g + 1)
                            dve.wait_ge(wj_high, FG * e + g + 1)
                            low(wj_part[1][:, g % 2, :, :], wj[:, g % R, :, :], wj_part[0][:, g % 2, :, :]
                                ).then_inc(wj_split, 1)
                            if g == 0 and past(e, 1):
                                take_sums(e - 1)
                            for j in range(FJ):
                                i = g * FJ + j
                                dve.wait_ge(up_taken, TILES * e + i + 1)
                                if j == 0 and (g >= 2 or past(e, 1)):
                                    dve.wait_ge(pj_done, FG * e + g - 1)
                                nc.vector.tensor_copy(hid_part[0][:, g % 2, j, :], hid[:, i % 2, :]
                                                      ).then_inc(hid_high, 1)
                                dve.wait_ge(hid_high, TILES * e + i + 1)
                                low(hid_part[1][:, g % 2, j, :], hid[:, i % 2, :], hid_part[0][:, g % 2, j, :]
                                    ).then_inc(hid_split, 1)
                            if g in (1, 2) and past(e, 1):
                                if g == 1:
                                    dve.wait_ge(stored, 32 * (e - 1))
                                for i in range((g - 1) * YU // 2, g * YU // 2):
                                    take_rows(e - 1, i)
                        if not last:
                            for c in range(KC):
                                split_slots(e + 1, c)

                    for c in range(KC):
                        split_slots(0, c)
                    expert_laps(dve, lap)
                    take_sums(NX - 1)
                    dve.wait_ge(stored, 32 * (NX - 1))
                    for i in range(YU):
                        take_rows(NX - 1, i)
            end_stage()

        with ExitStack() as ctx:
            got_row = sb("got_row", [P, 4, 2, D], F32, ctx)
            got = [sem(f"got_row{k}") for k in range(4)]
            v11, summed, stored = sem("v11"), sem("out_summed"), sem("out_stored")
            with nc.Block() as block:
                @block.gpsimd
                def _(pool):
                    for t in range(NT):
                        if t >= 4:
                            pool.wait_ge(summed, t - 3)
                        for k in range(2):
                            nc.gpsimd.indirect_dma_start(
                                out=got_row[:, t % 4, k, :], out_offset=None, in_=slot_out,
                                in_offset=bass.IndirectOffsetOnAxis(
                                    ap=slot_read[:, k * NT + t:k * NT + t + 1], axis=0)
                            ).then_inc(got[t % 4], 16)

                @block.vector
                def _(dve):
                    for t in range(NT):
                        dve.wait_ge(got[t % 4], 32 * (t // 4 + 1))
                        for k, s in ((0, v11), (1, summed)):
                            nc.vector.scalar_tensor_tensor(
                                out=x[:, t, :], in0=got_row[:, t % 4, k, :],
                                scalar=wgt[:, k * NT + t:k * NT + t + 1], in1=x[:, t, :],
                                op0=ALU.mult, op1=ALU.add).then_inc(s, 1)
                            if k == 0:
                                dve.wait_ge(v11, t + 1)

                @block.sync
                def _(sp):
                    for t in range(NT):
                        sp.wait_ge(summed, t + 1)
                        sp.dma_start(out[t * P:t * P + P, :], x[:, t, :]).then_inc(stored, 16)
                    sp.wait_ge(stored, 16 * NT)
            end_stage()


_INS = ["x", "src", "dst"] + ["L0_gnn_" + n for n in
                              ("Wsrc", "bsrc", "Wdst", "bdst", "attn", "ln_w", "ln_b", "on_w", "on_b")] + [
    "L0_ffn_" + n for n in ("ln1_w", "ln1_b", "ln2_w", "ln2_b", "attn_qkv_w", "attn_qkv_b", "attn_proj_w",
                            "attn_proj_b", "w_g", "exp_fc_w", "exp_fc_b", "exp_proj_w", "exp_proj_b")]


def kernel(**inputs):
    import numpy as _np
    import concourse.bacc as _bacc
    from concourse import mybir as _mybir
    from concourse.bass_utils import run_bass_kernel_spmd as _run

    nc = _bacc.Bacc("TRN2", target_bir_lowering=False, num_devices=1)
    arrays, args = {}, {}
    for name in _INS:
        v = _np.ascontiguousarray(inputs[name])
        arrays[f"in_{name}_dram"] = v
        args[name] = nc.dram_tensor(f"in_{name}_dram", v.shape, _mybir.dt.from_np(v.dtype), kind="ExternalInput").ap()
    out = nc.dram_tensor("out_0_dram", (N, D), _mybir.dt.float32, kind="ExternalOutput").ap()
    build(nc, args, out)
    r = _run(nc, [arrays], core_ids=[0])
    return r.results[0]["out_0_dram"]
```

```python
from contextlib import ExitStack

import concourse.bass as bass
from concourse import mybir

ALU = mybir.AluOpType
ACT = mybir.ActivationFunctionType
AX = mybir.AxisListType
F32 = mybir.dt.float32
F32R = mybir.dt.float32r
BF16 = mybir.dt.bfloat16
I32 = mybir.dt.int32
U32 = mybir.dt.uint32

N, D = 1250, 768
P, NT = 125, 10
KC = D // 128
E, EP = 20000, 128
ET = -(-E // EP)
ETP = 160
ITEMS = 174
GH, GD = 8, D // 8
DX = D + GH
L = 2
CH = 16
CE = E // CH
NH, HD = 12, 64
PAIRS = NH // 2
NX, F = 8, 4 * D
CAP = 390
SLOTS = NX * CAP
FG = 12
FJ = F // 128 // FG
ROWS = [(0, 128), (128, 128), (256, 128), (384, 6)]
LN_EPS = 1e-5
SLOPE = 0.2
BIG = 1e30
FAR = 1e6
GROUPS = [(0, 4), (4, 4), (8, 2)]


def past(t, n):
    return not isinstance(t, int) or t >= n


class Chain:

    def __init__(self, eng, sem, base=0):
        self.eng, self.sem, self.base, self.n = eng, sem, base, 0

    def do(self, ins):
        ins.then_inc(self.sem, 1)
        self.n += 1

    def wait(self):
        self.eng.wait_ge(self.sem, self.base + self.n)

    def link(self, ins):
        self.do(ins)
        self.wait()


def laps(eng, n, body):
    body(0)
    with eng.Fori(1, n) as i:
        body(i)


def build(nc, a, out):
    with ExitStack() as top:
        def sb(name, shape, dt=F32, ctx=top):
            return ctx.enter_context(nc.sbuf_tensor(name, shape, dt))

        def ps(name, shape, ctx, dt=F32):
            return ctx.enter_context(nc.psum_tensor(name, shape, dt))

        live = []

        def sem(name):
            live.append(nc.alloc_semaphore(name=name))
            return live[-1]

        def end_stage():
            nc.clear_and_free_semaphores(live)
            live.clear()
            nc.all_engine_barrier()

        def dram(name, shape, dt=F32):
            return nc.dram_tensor(name, shape, dt, kind="Internal").ap()

        def spread(row, parts):
            return row.partition_broadcast(parts)

        def rows(t):
            return t.rearrange("(t p) d -> p t d", p=P)

        hs_dram = dram("hs_dram", (N, DX))
        hd_dram = dram("hd_dram", (N, DX))
        logit_dram = dram("logit_dram", (GH, ETP * EP))
        ex_dram = dram("ex_dram", (GH, ETP * EP))
        pair_dram = dram("pair_dram", (128, 2))
        top_dram = dram("top_dram", (128, 2))
        slot_in = dram("slot_in", (SLOTS + 2 * N, D))
        slot_out = dram("slot_out", (SLOTS, D))

        x = sb("x", [P, NT, D])
        wgt = sb("wgt", [P, 2 * NT])
        slot_read = sb("slot_read", [P, 2 * NT], I32)
        ident = sb("ident", [128, 128])
        mid = top.enter_context(ExitStack())
        h = sb("h", [P, NT, D], F32, mid)
        ones = sb("ones", [128, 128], F32, mid)
        edge = mid.enter_context(ExitStack())
        lanes = sb("lanes", [128, P], F32, edge)
        src_item = sb("src_item", [128, ITEMS], I32, edge)
        dst_idx = sb("dst_idx", [128, ETP], I32, edge)
        dst_rel = sb("dst_rel", [128, ITEMS], F32, edge)
        win = sb("win", [1, ITEMS], I32, edge)
        cut_tile = sb("cut_tile", [128, NT - 1], I32, edge)
        dstc = sb("dstc", [128, CE], F32, edge)
        change = sb("change", [128, CE + 1], F32, edge)
        change2 = sb("change2", [GH, 2 * CH + 1], F32, edge)

        def layer_norm(ch, source, dest, temps, w=None, b=None):
            stats, mv, rstd, var_ready, std_ready = temps
            for t in range(NT):
                for k in range(2):
                    ch.do(nc.vector.bn_stats(stats[:, t, 6 * k:6 * k + 6], source[:, t, 384 * k:384 * k + 384]))
            ch.wait()
            for t in range(NT):
                ch.do(nc.vector.bn_aggr(mv[:, t, :], stats[:, t, :]))
            ch.wait()
            nc.vector.tensor_scalar(rstd[:, :], mv[:, :, 1], LN_EPS, None, ALU.add).then_inc(var_ready, 1)
            ch.eng.wait_ge(std_ready, 1)
            ch.link(nc.vector.reciprocal(rstd[:, :], rstd[:, :]))
            for t in range(NT):
                ch.do(nc.vector.tensor_scalar(dest[:, t, :], source[:, t, :], mv[:, t, 0:1], rstd[:, t:t + 1],
                                              ALU.subtract, ALU.mult))
            ch.wait()
            if w is not None:
                wide = [P, NT, D]
                ch.link(nc.vector.tensor_tensor(dest[:, :, :], dest[:, :, :], w[:, :].unsqueeze(1).to_broadcast(wide),
                                                ALU.mult))
                ch.link(nc.vector.tensor_tensor(dest[:, :, :], dest[:, :, :], b[:, :].unsqueeze(1).to_broadcast(wide),
                                                ALU.add))

        def root(act, temps):
            stats, mv, rstd, var_ready, std_ready = temps
            act.wait_ge(var_ready, 1)
            nc.scalar.activation(rstd[:, :], rstd[:, :], ACT.Sqrt).then_inc(std_ready, 1)

        def norm_temps(ctx, name):
            return (sb(f"{name}_stats", [P, NT, 12], F32, ctx), sb(f"{name}_mv", [P, NT, 2], F32, ctx),
                    sb(f"{name}_rstd", [P, NT], F32, ctx), sem(f"{name}_var_ready"), sem(f"{name}_std_ready"))

        def turn_pe(pe, source, bank, turned, taken):
            k = 0
            for c in range(KC):
                for t0, n in GROUPS:
                    if k >= len(bank):
                        pe.wait_ge(taken, k - len(bank) + 1)
                    for t in range(n):
                        ins = nc.tensor.transpose(bank[k % len(bank)][:, t * P:t * P + P],
                                                  source[:, t0 + t, c * 128:c * 128 + 128], ident[0:P, 0:P])
                    ins.then_inc(turned, 1)
                    k += 1

        def turn_act(act, dest, bank, turned, taken):
            k = 0
            for c in range(KC):
                for t0, n in GROUPS:
                    act.wait_ge(turned, k + 1)
                    nc.scalar.copy(dest[:, c, t0 * P:(t0 + n) * P], bank[k % len(bank)][:, 0:n * P]).then_inc(taken, 1)
                    k += 1

        TURNS = KC * len(GROUPS)

        with ExitStack() as ctx:
            rows_a = sb("rows_a", [128, 128], I32, ctx)
            rows_b = sb("rows_b", [32, 128], I32, ctx)
            drows_a = sb("drows_a", [128, 128], I32, ctx)
            drows_b = sb("drows_b", [32, 128], I32, ctx)
            fa = sb("fa", [128, 4, 128], F32, ctx)
            dst_f = sb("dst_f", [128, ETP], F32, ctx)
            first = sb("first", [128, ETP], F32, ctx)
            win_f = sb("win_f", [128, ETP], F32, ctx)
            junk = sb("junk", [128, ETP], F32, ctx)
            below = sb("below", [128, NT - 1], F32, ctx)
            cut = sb("cut", [128, NT - 1], F32, ctx)
            cut_i = sb("cut_i", [128, NT - 1], I32, ctx)
            cut_tf = sb("cut_tf", [128, NT - 1], F32, ctx)
            even = sb("even", [128, NT - 1], F32, ctx)
            dc_i = sb("dc_i", [128, CE], I32, ctx)
            pair = sb("pair", [128, 2], F32, ctx)
            pairs8 = sb("pairs8", [GH, 2 * CH], F32, ctx)
            zero = sb("zero", [120, D], F32, ctx)
            temps = norm_temps(ctx, "ln0")
            turned_p = ps("turned_p", [128, 512], ctx)
            first_p = ps("first_p", [128, 512], ctx)
            cut_p = ps("cut_p", [128, 512], ctx)

            x_in, src_in, dst_in, dc_in = sem("x_in"), sem("src_in"), sem("dst_in"), sem("dc_in")
            padded, consts, iota_done = sem("padded"), sem("consts"), sem("iota_done")
            v0, src_turned, dst_turned = sem("v0"), sem("src_turned"), sem("dst_turned")
            floats, dst_f_ready, first_ready, below_ready, cut_ready = (
                sem("floats"), sem("dst_f_ready"), sem("first_ready"), sem("below_ready"), sem("cut_ready"))
            pair_ready, pair_out, pair_in, zeroed = sem("pair_ready"), sem("pair_out"), sem("pair_in"), sem("zeroed")
            full = ET - 1 - 128

            with nc.Block() as block:
                @block.sync
                def _(sp):
                    sp.dma_start(x[:, :, :], rows(a["x"])).then_inc(x_in, 16)
                    sp.wait_ge(padded, 2)
                    for name, ra, rb, s in (("src", rows_a, rows_b, src_in), ("dst", drows_a, drows_b, dst_in)):
                        v = a[name]
                        sp.dma_start(ra[:, :], v[0:128 * EP].rearrange("(t e) -> t e", e=EP)).then_inc(s, 16)
                        sp.dma_start(rb[0:full, :], v[128 * EP:(128 + full) * EP].rearrange("(t e) -> t e", e=EP)
                                     ).then_inc(s, 16)
                        sp.dma_start(rb[full:full + 1, 0:E - (ET - 1) * EP],
                                     v[(ET - 1) * EP:E].rearrange("(a e) -> a e", a=1)).then_inc(s, 16)
                    for g in range(GH):
                        sp.dma_start(dc_i[g * CH:(g + 1) * CH, :], a["dst"].rearrange("(c e) -> c e", e=CE)
                                     ).then_inc(dc_in, 16)
                    sp.wait_ge(pair_ready, 1)
                    sp.dma_start(pair_dram, pair[:, :]).then_inc(pair_out, 16)
                    sp.wait_ge(pair_out, 16)
                    sp.dma_start(pairs8[:, :], pair_dram.rearrange("(h c) k -> h (c k)", h=GH)).then_inc(pair_in, 16)

                @block.scalar
                def _(act):
                    act.wait_ge(consts, 3)
                    act.dma_start(slot_in[0:SLOTS, :].rearrange("(p r) d -> p r d", p=120),
                                  zero[:, :].unsqueeze(1).to_broadcast([120, SLOTS // 120, D])).then_inc(zeroed, 16)
                    root(act, temps)
                    act.wait_ge(zeroed, 16)

                @block.gpsimd
                def _(pool):
                    nc.gpsimd.memset(rows_b[:, :], 0).then_inc(padded, 1)
                    nc.gpsimd.memset(drows_b[:, :], int(FAR)).then_inc(padded, 1)
                    nc.gpsimd.memset(ident[:, :], 0.0).then_inc(consts, 1)
                    nc.gpsimd.memset(ones[:, :], 1.0).then_inc(consts, 1)
                    nc.gpsimd.memset(zero[:, :], 0.0).then_inc(consts, 1)
                    pool.wait_ge(consts, 3)
                    nc.gpsimd.affine_select(out=ident[:, :], in_=ident[:, :], compare_op=ALU.not_equal, fill=1.0,
                                            base=0, pattern=[[-1, 128]], channel_multiplier=1).then_inc(consts, 1)
                    nc.gpsimd.iota(lanes[:, :], [[1, P]], base=0, channel_multiplier=0,
                                   allow_small_or_imprecise_dtypes=True).then_inc(iota_done, 1)
                    pool.wait_ge(iota_done, 1)

                @block.tensor
                def _(pe):
                    pe.wait_ge(consts, 4)
                    pe.wait_ge(floats, 2)
                    nc.tensor.transpose(turned_p[:, 0:128], fa[:, 0, :], ident[:, :]).then_inc(src_turned, 1)
                    nc.tensor.transpose(turned_p[:, 128:160], fa[0:32, 1, :], ident[0:32, 0:32]).then_inc(src_turned, 1)
                    pe.wait_ge(floats, 4)
                    nc.tensor.transpose(turned_p[:, 160:288], fa[:, 2, :], ident[:, :]).then_inc(dst_turned, 1)
                    nc.tensor.transpose(turned_p[:, 288:320], fa[0:32, 3, :], ident[0:32, 0:32]).then_inc(dst_turned, 1)
                    pe.wait_ge(dst_f_ready, 1)
                    nc.tensor.matmul(first_p[:, 0:ETP], ones[0:1, :], dst_f[0:1, :], start=True, stop=True
                                     ).then_inc(first_ready, 1)
                    pe.wait_ge(below_ready, NT - 1)
                    nc.tensor.matmul(cut_p[:, 0:NT - 1], ones[:, :], below[:, :], start=True, stop=True
                                     ).then_inc(cut_ready, 1)

                @block.vector
                def _(dve):
                    ch = Chain(dve, v0)
                    dve.wait_ge(src_in, 48)
                    nc.vector.tensor_copy(fa[:, 0, :], rows_a[:, :]).then_inc(floats, 1)
                    nc.vector.tensor_copy(fa[0:32, 1, :], rows_b[:, :]).then_inc(floats, 1)
                    dve.wait_ge(dst_in, 48)
                    nc.vector.tensor_copy(fa[:, 2, :], drows_a[:, :]).then_inc(floats, 1)
                    nc.vector.tensor_copy(fa[0:32, 3, :], drows_b[:, :]).then_inc(floats, 1)
                    ch.do(nc.vector.memset(src_item[:, ETP:], 0))
                    ch.do(nc.vector.memset(dst_rel[:, ETP:], FAR))
                    ch.do(nc.vector.memset(win[:, ETP:], 0))
                    ch.do(nc.vector.memset(win_f[:, :], 0.0))
                    dve.wait_ge(src_turned, 2)
                    dve.wait_ge(dst_turned, 2)
                    nc.vector.tensor_copy(dst_f[:, :], turned_p[:, ETP:2 * ETP]).then_inc(dst_f_ready, 1)
                    ch.do(nc.vector.tensor_copy(src_item[:, 0:ETP], turned_p[:, 0:ETP]))
                    dve.wait_ge(dst_f_ready, 1)
                    ch.do(nc.vector.tensor_scalar(dst_idx[:, :], dst_f[:, :], float(N - 1), None, ALU.min))
                    for k in range(1, NT):
                        nc.vector.tensor_scalar(junk[:, :], dst_f[:, :], float(P * k), 0.0, ALU.is_lt, ALU.add,
                                                accum_out=below[:, k - 1:k]).then_inc(below_ready, 1)
                        dve.wait_ge(below_ready, k)
                    dve.wait_ge(first_ready, 1)
                    ch.link(nc.vector.tensor_copy(first[:, :], first_p[:, 0:ETP]))
                    for k in range(1, NT):
                        ch.link(nc.vector.scalar_tensor_tensor(out=win_f[:, :], in0=first[:, :], scalar=float(P * k),
                                                               in1=win_f[:, :], op0=ALU.is_ge, op1=ALU.add))
                    ch.do(nc.vector.tensor_copy(win[:, 0:ETP], win_f[0:1, :]))
                    ch.do(nc.vector.scalar_tensor_tensor(out=dst_rel[:, 0:ETP], in0=win_f[:, :], scalar=-float(P),
                                                         in1=dst_f[:, :], op0=ALU.mult, op1=ALU.add))
                    dve.wait_ge(cut_ready, 1)
                    ch.do(nc.vector.tensor_copy(cut[:, :], cut_p[:, 0:NT - 1]))
                    ch.link(nc.vector.tensor_copy(cut_i[:, :], cut_p[:, 0:NT - 1]))
                    ch.link(nc.vector.tensor_scalar(cut_tile[:, :], cut_i[:, :], 7, None, ALU.arith_shift_right))
                    ch.link(nc.vector.tensor_copy(cut_tf[:, :], cut_tile[:, :]))
                    ch.link(nc.vector.scalar_tensor_tensor(out=even[:, :], in0=cut_tf[:, :], scalar=-float(EP),
                                                           in1=cut[:, :], op0=ALU.mult, op1=ALU.add))
                    ch.link(nc.vector.tensor_scalar(even[:, :], even[:, :], 0.0, FAR, ALU.is_equal, ALU.mult))
                    for k in range(1, NT):
                        t = nc.vector.value_load(cut_tile[0:1, k - 1:k], min_val=0, max_val=ETP - 1)
                        ch.do(nc.vector.tensor_copy(src_item[:, ETP + k - 1:ETP + k], src_item[:, bass.ds(t, 1)]))
                        ch.do(nc.vector.tensor_scalar(dst_rel[:, ETP + k - 1:ETP + k], dst_f[:, bass.ds(t, 1)],
                                                      -float(P * k), even[:, k - 1:k], ALU.add, ALU.add))
                        ch.do(nc.vector.memset(win[:, ETP + k - 1:ETP + k], k))
                    dve.wait_ge(dc_in, 16 * GH)
                    ch.do(nc.vector.tensor_copy(dstc[:, :], dc_i[:, :]))
                    ch.do(nc.vector.memset(change[:, :], -BIG))
                    ch.do(nc.vector.memset(change2[:, :], -BIG))
                    ch.wait()
                    ch.do(nc.vector.tensor_tensor(change[:, 1:CE], dstc[:, 1:CE], dstc[:, 0:CE - 1], ALU.not_equal))
                    ch.do(nc.vector.tensor_copy(pair[:, 0:1], dstc[:, 0:1]))
                    ch.do(nc.vector.tensor_copy(pair[:, 1:2], dstc[:, CE - 1:CE]))
                    ch.wait()
                    dve.sem_inc(pair_ready, 1)
                    ch.do(nc.vector.tensor_scalar(change[:, 1:CE], change[:, 1:CE], -BIG, None, ALU.mult))
                    dve.wait_ge(pair_in, 16)
                    ch.link(nc.vector.tensor_tensor(change2[:, 1:2 * CH], pairs8[:, 1:2 * CH], pairs8[:, 0:2 * CH - 1],
                                                    ALU.not_equal))
                    ch.link(nc.vector.tensor_scalar(change2[:, 1:2 * CH], change2[:, 1:2 * CH], -BIG, None, ALU.mult))
                    dve.wait_ge(x_in, 16)
                    layer_norm(ch, x, h, temps)
            end_stage()

        with nc.Fori(0, L) as l:

            with ExitStack() as ctx:
                hT = sb("hT", [128, KC, N], F32, ctx)
                w = [sb(f"w{k}_", [128, KC, D], F32, ctx) for k in range(2)]
                bias = sb("gbias", [P, 2, D], F32, ctx)
                att = sb("att", [P, D], F32, ctx)
                rowx = [sb(f"rowx{k}_", [P, DX], F32, ctx) for k in range(2)]
                prod = sb("prod", [P, D], F32, ctx)
                bank = [ps(f"lin{k}_", [128, 512], ctx) for k in range(8)]
                w_in, b_in, turned, taken = sem("w_in"), sem("b_in"), sem("turned"), sem("taken")
                lin_done, v1 = sem("lin_done"), sem("v1_")
                stored = [sem(f"stored{k}_") for k in range(2)]
                PER = 3

                with nc.Block() as block:
                    @block.sync
                    def _(sp):
                        for k, name in enumerate(("Wsrc", "Wdst")):
                            sp.dma_start(w[k][:, :, :], a[f"L0_gnn_{name}"][bass.ds(l, 1)].rearrange("a (c p) n -> p (a c) n", p=128)
                                         ).then_inc(w_in, 16)
                        for k, name in enumerate(("bsrc", "bdst")):
                            sp.dma_start(bias[:, k, :], spread(a[f"L0_gnn_{name}"][bass.ds(l, 1)].rearrange("a d -> (a d)"), P)).then_inc(b_in, 16)
                        sp.dma_start(att[:, :], spread(a["L0_gnn_attn"][bass.ds(l, 1)].rearrange("a h d -> (a h d)"), P)
                                     ).then_inc(b_in, 16)
                        for t in range(NT):
                            for k, table in enumerate((hs_dram, hd_dram)):
                                sp.wait_ge(v1, PER * (2 * t + k + 1) + 1)
                                sp.dma_start(table[t * P:t * P + P, :], rowx[k][:, :]).then_inc(stored[k], 16)
                        for k in range(2):
                            sp.wait_ge(stored[k], 16 * NT)

                    @block.tensor
                    def _(pe):
                        turn_pe(pe, h, bank, turned, taken)
                        pe.wait_ge(taken, TURNS)
                        pe.wait_ge(w_in, 32)
                        for m in range(2 * NT):
                            t, k = m // 2, m % 2
                            if m >= 4:
                                pe.wait_ge(v1, PER * (m - 4) + 2)
                            for half in range(2):
                                for c in range(KC):
                                    ins = nc.tensor.matmul(bank[2 * (m % 4) + half][0:P, 0:384],
                                                           hT[:, c, t * P:t * P + P],
                                                           w[k][:, c, 384 * half:384 * half + 384],
                                                           start=(c == 0), stop=(c == KC - 1))
                            ins.then_inc(lin_done, 1)

                    @block.scalar
                    def _(act):
                        turn_act(act, hT, bank, turned, taken)

                    @block.vector
                    def _(dve):
                        ch = Chain(dve, v1)
                        dve.wait_ge(b_in, 48)
                        ch.link(nc.vector.tensor_scalar(att[:, :], att[:, :], SLOPE, None, ALU.mult))
                        for m in range(2 * NT):
                            t, k = m // 2, m % 2
                            r = rowx[k]
                            dve.wait_ge(lin_done, m + 1)
                            if t:
                                dve.wait_ge(stored[k], 16 * t)
                            nc.vector.tensor_tensor(r[:, 0:384], bank[2 * (m % 4)][0:P, 0:384], bias[:, k, 0:384],
                                                    ALU.add)
                            ch.link(nc.vector.tensor_tensor(r[:, 384:D], bank[2 * (m % 4) + 1][0:P, 0:384],
                                                            bias[:, k, 384:D], ALU.add))
                            ch.link(nc.vector.tensor_tensor(prod[:, :], r[:, 0:D], att[:, :], ALU.mult))
                            ch.link(nc.vector.tensor_reduce(r[:, D:DX], prod[:, :].rearrange("p (h d) -> p h d", h=GH),
                                                            AX.X, ALU.add))
                end_stage()

            with ExitStack() as ctx:
                R = 8
                HALF = R // 2
                LAPS = ETP // R
                gs = sb("gs", [128, R, DX], F32, ctx)
                gd = sb("gd", [128, R, DX], F32, ctx)
                cur = sb("cur", [128, 2, R], I32, ctx)
                rz = sb("rz", [128, 2, D], F32, ctx)
                acol = sb("acol", [128, KC], F32, ctx)
                arow = sb("arow", [KC, 128], F32, ctx)
                a8 = sb("a8", [128, KC, GH], F32, ctx)
                lg = sb("lg", [GH, 2, HALF * EP], F32, ctx)
                zt = [ps(f"zt{k}_", [128, 1024], ctx) for k in range(2)]
                lp = [ps(f"lp{k}_", [128, HALF * EP], ctx) for k in range(2)]
                ap_ = ps("ap_", [128, 512], ctx)
                a_in, a_turned, mask0, a8_ready, v2 = (sem("a_in"), sem("a_turned"), sem("mask0_"),
                                                       sem("a8_ready"), sem("v2_"))
                picked, handed = sem("picked"), sem("handed")
                got = [sem(f"got{k}_") for k in range(R)]
                z_ready, z_turned, relu_done, l_done, l_taken = (
                    sem("z_ready"), sem("z_turned"), sem("relu_done"), sem("l_done"), sem("l_taken"))
                l_out = [sem(f"l_out{half}_") for half in range(2)]

                with nc.Block() as block:
                    @block.sync
                    def _(sp):
                        sp.dma_start(arow[:, :], a["L0_gnn_attn"][bass.ds(l, 1)].rearrange("a h d -> (a h d)")
                                     .rearrange("(c p) -> c p", p=128)).then_inc(a_in, 16)

                        for half in range(2):
                            sp.sem_inc(l_out[half], 16)

                        def lap(i):
                            for half in range(2):
                                sp.wait_ge(l_taken, 2 * i + half + 1)
                                sp.dma_start(logit_dram[:, bass.ds(i * (R * EP) + half * (HALF * EP), HALF * EP)],
                                             lg[:, half, :]).then_inc(l_out[half], 16)
                        laps(sp, LAPS, lap)
                        for half in range(2):
                            sp.wait_ge(l_out[half], 16 * (LAPS + 1))

                    @block.gpsimd
                    def _(pool):
                        nc.gpsimd.memset(a8[:, :, :], 1.0 - SLOPE).then_inc(mask0, 1)
                        pool.wait_ge(mask0, 1)
                        nc.gpsimd.affine_select(out=a8[:, :, :], in_=a8[:, :, :], compare_op=ALU.is_ge, fill=0.0, base=0,
                                                pattern=[[128, KC], [-GD, GH]], channel_multiplier=1).then_inc(mask0, 1)
                        pool.wait_ge(mask0, 2)
                        nc.gpsimd.affine_select(out=a8[:, :, :], in_=a8[:, :, :], compare_op=ALU.is_ge, fill=0.0,
                                                base=GD - 1, pattern=[[-128, KC], [GD, GH]], channel_multiplier=-1
                                                ).then_inc(mask0, 1)

                        def lap(i):
                            for half in range(2):
                                t0 = R * i + half * HALF
                                if past(i, 1):
                                    pool.wait_ge(z_ready, t0 - R + HALF)
                                at = slice(half * HALF, half * HALF + HALF)
                                nc.gpsimd.tensor_copy(cur[:, 0, at], src_item[:, bass.ds(t0, HALF)]).then_inc(picked, 1)
                                nc.gpsimd.tensor_copy(cur[:, 1, at], dst_idx[:, bass.ds(t0, HALF)]).then_inc(picked, 1)
                                pool.wait_ge(picked, 4 * i + 2 * half + 2)
                                for j in range(half * HALF, half * HALF + HALF):
                                    if past(i, 1):
                                        pool.wait_ge(l_done, R * i + j - R + 1)
                                    pool.sem_inc(handed, 1)
                                    for k, (g, table) in enumerate(((gs, hs_dram), (gd, hd_dram))):
                                        nc.gpsimd.indirect_dma_start(
                                            out=g[:, j, :], out_offset=None, in_=table,
                                            in_offset=bass.IndirectOffsetOnAxis(ap=cur[:, k, j:j + 1], axis=0)
                                        ).then_inc(got[j], 16)
                        laps(pool, LAPS, lap)

                    @block.vector
                    def _(dve):
                        dve.wait_ge(a_turned, 1)
                        nc.vector.tensor_copy(acol[:, :], ap_[:, 0:KC]).then_inc(v2, 1)
                        dve.wait_ge(v2, 1)
                        dve.wait_ge(mask0, 3)
                        nc.vector.tensor_tensor(a8[:, :, :], a8[:, :, :],
                                                acol[:, :].unsqueeze(2).to_broadcast([128, KC, GH]), ALU.mult
                                                ).then_inc(a8_ready, 1)

                        def take(i, half):
                            dve.wait_ge(l_done, R * i + (half + 1) * HALF)
                            dve.wait_ge(l_out[half], 16 * (i + 1))
                            nc.vector.tensor_copy(lg[:, half, :], lp[half][0:GH, :]).then_inc(l_taken, 1)

                        def lap(i):
                            for j in range(R):
                                dve.wait_ge(got[j], 32 * (i + 1))
                                nc.vector.tensor_tensor(gs[:, j, :], gs[:, j, :], gd[:, j, :], ALU.add
                                                        ).then_inc(z_ready, 1)
                                if j == 2 and past(i, 1):
                                    take(i - 1, 1)
                                if j == 2 + HALF:
                                    take(i, 0)
                        laps(dve, LAPS, lap)
                        take(LAPS - 1, 1)

                    @block.tensor
                    def _(pe):
                        pe.wait_ge(a_in, 16)
                        nc.tensor.transpose(ap_[:, 0:KC], arow[:, :], ident[0:KC, 0:KC]).then_inc(a_turned, 1)
                        pe.wait_ge(a8_ready, 1)

                        def turn(t, j):
                            pe.wait_ge(z_ready, t + 1)
                            if past(t, 2):
                                pe.wait_ge(relu_done, t - 1)
                            for c in range(KC):
                                ins = nc.tensor.transpose(zt[j % 2][:, c * 128:c * 128 + 128],
                                                          gs[:, j, c * 128:c * 128 + 128], ident[:, :])
                            ins.then_inc(z_turned, 1)

                        def logits(t, i, j):
                            pe.wait_ge(relu_done, t + 1)
                            if j % HALF == 0 and past(i, 1):
                                pe.wait_ge(l_taken, 2 * i + j // HALF - 1)
                            at = lp[j // HALF][0:GH, j % HALF * EP:j % HALF * EP + EP]
                            for c in range(KC):
                                nc.tensor.matmul(at, a8[:, c, :], rz[:, j % 2, c * 128:c * 128 + 128],
                                                 start=(c == 0), stop=False)
                            nc.tensor.matmul(at, gs[:, j, D:DX], ident[:, :], start=False, stop=True
                                             ).then_inc(l_done, 1)

                        def lap(i):
                            for j in range(R):
                                turn(R * i + j, j)
                                if j:
                                    logits(R * i + j - 1, i, j - 1)
                            logits(R * i + R - 1, i, R - 1)
                        laps(pe, LAPS, lap)

                    @block.scalar
                    def _(act):
                        def lap(i):
                            for j in range(R):
                                t = R * i + j
                                act.wait_ge(z_turned, t + 1)
                                if past(t, 2):
                                    act.wait_ge(l_done, t - 1)
                                nc.scalar.activation(rz[:, j % 2, 0:512], zt[j % 2][:, 0:512], ACT.Relu)
                                nc.scalar.activation(rz[:, j % 2, 512:D], zt[j % 2][:, 512:D], ACT.Relu
                                                     ).then_inc(relu_done, 1)
                        laps(act, LAPS, lap)
                end_stage()

            with ExitStack() as ctx:
                lt = sb("lt", [128, CE], F32, ctx)
                fwd = sb("fwd", [128, CE], F32, ctx)
                bwd = sb("bwd", [128, CE], F32, ctx)
                pen = sb("pen", [128, CE], F32, ctx)
                ends = sb("ends", [128, 2], F32, ctx)
                ends8 = sb("ends8_", [GH, 2 * CH], F32, ctx)
                fwd8 = sb("fwd8_", [GH, 2 * CH], F32, ctx)
                bwd8 = sb("bwd8_", [GH, 2 * CH], F32, ctx)
                tops = sb("tops", [128, 2], F32, ctx)
                blank = sb("blank", [GH, ETP * EP - E], F32, ctx)
                lt_in, v3, ends_ready, ends_out, ends_in, tops_ready, tops_out, tops_in = (
                    sem(n) for n in ("lt_in", "v3_", "ends_ready", "ends_out", "ends_in", "tops_ready",
                                          "tops_out", "tops_in"))
                less_ready, ex_ready, ex_out, blank_ready = (
                    sem("less_ready"), sem("ex_ready"), sem("ex_out"), sem("blank_ready"))

                with nc.Block() as block:
                    @block.sync
                    def _(sp):
                        for g in range(GH):
                            sp.dma_start(lt[g * CH:g * CH + CH, :],
                                         logit_dram[g, 0:E].rearrange("(c e) -> c e", e=CE)).then_inc(lt_in, 16)
                        sp.wait_ge(ends_ready, 1)
                        sp.dma_start(pair_dram, ends[:, :]).then_inc(ends_out, 16)
                        sp.wait_ge(ends_out, 16)
                        sp.dma_start(ends8[:, :], pair_dram.rearrange("(h c) k -> h (c k)", h=GH)).then_inc(ends_in, 16)
                        sp.wait_ge(tops_ready, 1)
                        sp.dma_start(top_dram.rearrange("(h c) k -> h (c k)", h=GH), fwd8[:, :]).then_inc(tops_out, 16)
                        sp.wait_ge(tops_out, 16)
                        sp.dma_start(tops[:, :], top_dram).then_inc(tops_in, 16)
                        sp.wait_ge(blank_ready, 1)
                        sp.dma_start(ex_dram[:, E:], blank[:, :]).then_inc(ex_out, 16)
                        sp.wait_ge(ex_ready, 1)
                        for g in range(GH):
                            sp.dma_start(ex_dram[g, 0:E].rearrange("(c e) -> c e", e=CE),
                                         bwd[g * CH:g * CH + CH, :]).then_inc(ex_out, 16)
                        sp.wait_ge(ex_out, 16 * (GH + 1))

                    @block.scalar
                    def _(act):
                        act.wait_ge(less_ready, 1)
                        nc.scalar.activation(bwd[:, :], fwd[:, :], ACT.Exp).then_inc(ex_ready, 1)

                    @block.vector
                    def _(dve):
                        ch = Chain(dve, v3)
                        nc.vector.memset(blank[:, :], 0.0).then_inc(blank_ready, 1)
                        dve.wait_ge(lt_in, 16 * GH)
                        ch.do(nc.vector.tensor_tensor_scan(fwd[:, :], change[:, 0:CE], lt[:, :], -BIG, ALU.add, ALU.max))
                        ch.do(nc.vector.tensor_tensor_scan(bwd[:, ::-1], change[:, CE:0:-1], lt[:, ::-1], -BIG,
                                                           ALU.add, ALU.max))
                        ch.wait()
                        ch.link(nc.vector.tensor_tensor(fwd[:, :], fwd[:, :], bwd[:, :], ALU.max))
                        ch.do(nc.vector.tensor_copy(ends[:, 0:1], fwd[:, 0:1]))
                        ch.do(nc.vector.tensor_copy(ends[:, 1:2], fwd[:, CE - 1:CE]))
                        ch.wait()
                        dve.sem_inc(ends_ready, 1)
                        dve.wait_ge(ends_in, 16)
                        ch.do(nc.vector.tensor_tensor_scan(fwd8[:, :], change2[:, 0:2 * CH], ends8[:, :], -BIG,
                                                           ALU.add, ALU.max))
                        ch.do(nc.vector.tensor_tensor_scan(bwd8[:, ::-1], change2[:, 2 * CH:0:-1], ends8[:, ::-1], -BIG,
                                                           ALU.add, ALU.max))
                        ch.wait()
                        nc.vector.tensor_tensor(fwd8[:, :], fwd8[:, :], bwd8[:, :], ALU.max).then_inc(tops_ready, 1)
                        dve.wait_ge(tops_in, 16)
                        for k, e in enumerate((0, CE - 1)):
                            ch.link(nc.vector.tensor_scalar(pen[:, :], dstc[:, :], dstc[:, e:e + 1], -BIG,
                                                            ALU.not_equal, ALU.mult))
                            ch.link(nc.vector.scalar_tensor_tensor(out=fwd[:, :], in0=pen[:, :], scalar=tops[:, k:k + 1],
                                                                   in1=fwd[:, :], op0=ALU.add, op1=ALU.max))
                        ch.link(nc.vector.tensor_tensor(fwd[:, :], lt[:, :], fwd[:, :], ALU.subtract))
                        dve.sem_inc(less_ready, 1)
                end_stage()

            with ExitStack() as ctx:
                R = 6
                HALF = R // 2
                LAPS = ITEMS // R
                ACT_HEADS = 4
                DVE_HEADS = GH - ACT_HEADS
                Q = ETP // 4
                acc = sb("acc", [P, NT, DX], F32, ctx)
                gr = sb("gr", [128, R, DX], F32, ctx)
                cur = sb("curb", [128, R], I32, ctx)
                oh = sb("oh", [128, R, P], F32, ctx)
                exr = sb("exr", [GH, 2, Q * EP], F32, ctx)
                exT = sb("exT", [128, ITEMS, GH], F32, ctx)
                sinv = sb("sinv", [P, NT, GH], F32, ctx)
                neg = sb("neg", [P, 2, D], F32, ctx)
                lnw = sb("lnw", [P, D], F32, ctx)
                lnb = sb("lnb", [P, D], F32, ctx)
                temps = norm_temps(ctx, "lng")
                SUMS = 3
                sums = [ps(f"sums{k}_", [128, 2, 512], ctx) for k in range(SUMS)]
                turned_ex = [sums[0][:, 0, :], sums[0][:, 1, :], sums[1][:, 0, :], sums[1][:, 1, :]]
                ex_in = [sem(f"ex_in{k}_") for k in range(2)]
                ln_in, ex_turned, ex_taken, v4, v5 = (sem(n) for n in ("ln_in", "ex_turned", "ex_taken", "v4_",
                                                                            "v5_"))
                picked, handed = sem("picked2_"), sem("handed2_")
                got = [sem(f"got2{k}_") for k in range(R)]
                weighed, weighed_act, summed, added, neg_ready, exp_done, exT_ready = (
                    sem(n) for n in ("weighed", "weighed_act", "summed", "added", "neg_ready", "exp_done",
                                     "exT_ready"))

                with nc.Block() as block:
                    @block.sync
                    def _(sp):
                        sp.dma_start(lnw[:, :], spread(a["L0_gnn_ln_w"][bass.ds(l, 1)].rearrange("a d -> (a d)"), P)).then_inc(ln_in, 16)
                        sp.dma_start(lnb[:, :], spread(a["L0_gnn_ln_b"][bass.ds(l, 1)].rearrange("a d -> (a d)"), P)).then_inc(ln_in, 16)
                        for q in range(4):
                            if q >= 2:
                                sp.wait_ge(ex_turned, q - 1)
                            sp.dma_start(exr[:, q % 2, :], ex_dram[:, q * Q * EP:(q + 1) * Q * EP]
                                         ).then_inc(ex_in[q % 2], 16)

                    @block.gpsimd
                    def _(pool):
                        def lap(i):
                            for half in range(2):
                                t0 = R * i + half * HALF
                                if past(i, 1):
                                    pool.wait_ge(weighed, t0 - R + HALF)
                                at = slice(half * HALF, half * HALF + HALF)
                                nc.gpsimd.tensor_copy(cur[:, at], src_item[:, bass.ds(t0, HALF)]).then_inc(picked, 1)
                                pool.wait_ge(picked, 2 * i + half + 1)
                                for j in range(half * HALF, half * HALF + HALF):
                                    if past(i, 1):
                                        pool.wait_ge(summed, R * i + j - R + 1)
                                    pool.sem_inc(handed, 1)
                                    nc.gpsimd.indirect_dma_start(
                                        out=gr[:, j, :], out_offset=None, in_=hs_dram,
                                        in_offset=bass.IndirectOffsetOnAxis(ap=cur[:, j:j + 1], axis=0)
                                    ).then_inc(got[j], 16)
                        laps(pool, LAPS, lap)

                    @block.tensor
                    def _(pe):
                        for q in range(4):
                            pe.wait_ge(ex_in[q % 2], 16 * (q // 2 + 1))
                            for t in range(Q):
                                ins = nc.tensor.transpose(turned_ex[q][:, t * GH:t * GH + GH],
                                                          exr[:, q % 2, t * EP:t * EP + EP], ident[0:GH, 0:GH])
                            ins.then_inc(ex_turned, 1)
                        pe.wait_ge(ex_taken, 4)

                        def lap(i):
                            for j in range(R):
                                t = R * i + j
                                pe.wait_ge(weighed, t + 1)
                                pe.wait_ge(weighed_act, t + 1)
                                if past(t, SUMS):
                                    pe.wait_ge(added, t - SUMS + 1)
                                for k in range(2):
                                    ins = nc.tensor.matmul(sums[j % SUMS][0:P, k, 0:DX // 2], oh[:, j, :],
                                                           gr[:, j, k * (DX // 2):(k + 1) * (DX // 2)],
                                                           start=True, stop=True)
                                ins.then_inc(summed, 1)
                        laps(pe, LAPS, lap)

                    @block.scalar
                    def _(act):
                        act.wait_ge(exT_ready, 1)

                        def lap(i):
                            for j in range(R):
                                t = R * i + j
                                act.wait_ge(got[j], 16 * (i + 1))
                                for g in range(DVE_HEADS, GH):
                                    part = gr[:, j, g * GD:(g + 1) * GD]
                                    nc.scalar.activation(part, part, ACT.Copy,
                                                         scale=exT[:, bass.ds(t, 1), g:g + 1]
                                                         .rearrange("p a h -> p (a h)"))
                                nc.scalar.copy(gr[:, j, D:DX], exT[:, bass.ds(t, 1), :].rearrange("p a h -> p (a h)")
                                               ).then_inc(weighed_act, 1)
                        laps(act, LAPS, lap)
                        for t in range(NT):
                            act.wait_ge(neg_ready, t + 1)
                            nc.scalar.activation(neg[:, t % 2, :], neg[:, t % 2, :], ACT.Exp).then_inc(exp_done, 1)
                        root(act, temps)

                    @block.vector
                    def _(dve):
                        ch = Chain(dve, v4)
                        ch.do(nc.vector.memset(acc[:, :, :], 0.0))
                        ch.do(nc.vector.memset(exT[:, ETP + NT - 1:, :], 0.0))
                        for q in range(4):
                            dve.wait_ge(ex_turned, q + 1)
                            nc.vector.tensor_copy(exT[:, q * Q:(q + 1) * Q, :],
                                                  turned_ex[q][:, 0:Q * GH].rearrange("p (t h) -> p t h", h=GH)
                                                  ).then_inc(ex_taken, 1)
                        dve.wait_ge(ex_taken, 4)
                        for k in range(NT - 1):
                            t = nc.vector.value_load(cut_tile[0:1, k:k + 1], min_val=0, max_val=ETP - 1)
                            ch.do(nc.vector.tensor_copy(exT[:, ETP + k:ETP + k + 1, :], exT[:, bass.ds(t, 1), :]))
                        ch.wait()
                        dve.sem_inc(exT_ready, 1)

                        def weigh(t, i, j):
                            e = exT[:, bass.ds(t, 1), 0:DVE_HEADS]
                            dve.wait_ge(got[j], 16 * (i + 1))
                            g3 = gr[:, j, 0:DVE_HEADS * GD].rearrange("p (h d) -> p h d", h=DVE_HEADS)
                            nc.vector.tensor_tensor(
                                g3, g3, e.rearrange("p a h -> p h a").to_broadcast([128, DVE_HEADS, GD]), ALU.mult)
                            nc.vector.tensor_scalar(oh[:, j, :], lanes[:, :], dst_rel[:, bass.ds(t, 1)], None,
                                                    ALU.is_equal).then_inc(weighed, 1)

                        def add(t, j):
                            w = nc.vector.value_load(win[0:1, bass.ds(t, 1)], min_val=0, max_val=NT - 1)
                            dve.wait_ge(summed, t + 1)
                            if past(t, 1):
                                dve.wait_ge(added, t)
                            to = acc[:, bass.ds(w, 1), :].rearrange("p a (k n) -> p (a k) n", k=2)
                            nc.vector.tensor_tensor(to, to, sums[j % SUMS][0:P, :, 0:DX // 2], ALU.add).then_inc(added, 1)

                        def lap(i):
                            for j in range(R):
                                t = R * i + j
                                weigh(t, i, j)
                                if past(t, 2):
                                    add(t - 2, (j - 2) % R)
                        laps(dve, LAPS, lap)
                        add(ITEMS - 2, R - 2)
                        add(ITEMS - 1, R - 1)
                        dve.wait_ge(added, ITEMS)

                        ch = Chain(dve, v5)
                        ch.link(nc.vector.tensor_scalar(sinv[:, :, :], acc[:, :, D:DX], 1e-30, None, ALU.max))
                        ch.link(nc.vector.reciprocal(sinv[:, :, :], sinv[:, :, :]))
                        for t in range(NT):
                            o3 = acc[:, t, 0:D].rearrange("p (h d) -> p h d", h=GH)
                            ch.do(nc.vector.tensor_tensor(o3, o3, sinv[:, t, :].unsqueeze(2).to_broadcast([P, GH, GD]),
                                                          ALU.mult))
                        ch.wait()

                        def elu_tail(t):
                            dve.wait_ge(exp_done, t + 1)
                            ch.link(nc.vector.scalar_tensor_tensor(out=acc[:, t, 0:D], in0=acc[:, t, 0:D], scalar=0.0,
                                                                   in1=neg[:, t % 2, :], op0=ALU.max, op1=ALU.add))
                            ch.do(nc.vector.scalar_tensor_tensor(out=h[:, t, :], in0=acc[:, t, 0:D], scalar=-1.0,
                                                                 in1=h[:, t, :], op0=ALU.add, op1=ALU.add))
                        for t in range(NT):
                            nc.vector.tensor_scalar(neg[:, t % 2, :], acc[:, t, 0:D], 0.0, None, ALU.min
                                                    ).then_inc(neg_ready, 1)
                            if t:
                                elu_tail(t - 1)
                        elu_tail(NT - 1)
                        ch.wait()
                        dve.wait_ge(ln_in, 32)
                        layer_norm(ch, h, h, temps, w=lnw, b=lnb)
                end_stage()

        edge.close()

        with ExitStack() as ctx:
            onw = sb("onw", [P, D], F32, ctx)
            onb = sb("onb", [P, D], F32, ctx)
            temps = norm_temps(ctx, "lno")
            temps2 = norm_temps(ctx, "lny")
            on_in, v6 = sem("on_in"), sem("v6")
            with nc.Block() as block:
                @block.sync
                def _(sp):
                    sp.dma_start(onw[:, :], spread(a["L0_gnn_on_w"], P)).then_inc(on_in, 16)
                    sp.dma_start(onb[:, :], spread(a["L0_gnn_on_b"], P)).then_inc(on_in, 16)

                @block.scalar
                def _(act):
                    root(act, temps)
                    root(act, temps2)

                @block.vector
                def _(dve):
                    ch = Chain(dve, v6)
                    dve.wait_ge(on_in, 32)
                    layer_norm(ch, h, h, temps, w=onw, b=onb)
                    ch.link(nc.vector.tensor_tensor(x[:, :, :], x[:, :, :], h[:, :, :], ALU.add))
                    layer_norm(ch, x, h, temps2)
                    ch.link(nc.vector.tensor_tensor(x[:, :, :], x[:, :, :], h[:, :, :], ALU.add))
            end_stage()

        o_full = sb("o", [128, NT, D], F32, mid)
        o = o_full[0:P, :, :]
        oT = (o_full[:, :, :].rearrange("p t d -> p (t d)")[:, 0:KC * N].rearrange("p (c n) -> p c n", c=KC))
        with ExitStack() as ctx:
            w1 = sb("ln1w", [P, D], F32, ctx)
            b1 = sb("ln1b", [P, D], F32, ctx)
            temps = norm_temps(ctx, "ln1")
            tT = sb("tT", [128, KC, N], F32, ctx)
            wp = [sb(f"wp{k}_", [128, KC, 3, 128], F32, ctx) for k in range(2)]
            brow = sb("brow", [3 * KC, 128], F32, ctx)
            bcol = sb("bcol", [128, 3 * KC], F32, ctx)
            bv = sb("bv", [P, D], F32, ctx)
            qT = sb("qT", [128, N], F32, ctx)
            kT = sb("kT", [128, N], F32, ctx)
            v = sb("v", [P, NT, 128], F32, ctx)
            prob = sb("prob", [P, 2, N], F32, ctx)
            pT = sb("pT", [P, 2, 3, 4 * P], F32, ctx)
            bank_high = sb("bank_high", [P, 2, 3], F32, ctx)
            high = sb("high", [P, 2], F32, ctx)
            low = sb("low", [P, 2], F32, ctx)
            part = sb("part", [P, 2, 3], F32, ctx)
            total = sb("total", [P, 2], F32, ctx)
            tinv = sb("tinv", [P, 2], F32, ctx)
            ident_h = sb("ident_h", [P, P], BF16, ctx)
            causal = sb("causal", [P, P], BF16, ctx)
            S = [ps(f"S{k}_", [128, 3, 512], ctx) for k in range(2)]
            O = [ps(f"O{k}_", [128, 512], ctx) for k in range(2)]
            banks = [S[k][:, b, :] for k in range(2) for b in range(3)]
            (ln1_in, v7, normed, turned, taken, brow_in, b_turned, b_taken, bv_in, masks, qk_done, v_done,
             qk_taken, v_taken, s_done, low_ready, exp_done, p_ready, p_turned, pt_act, pt_dve, o_done, o_taken, v8) = (
                sem(n) for n in ("ln1_in", "v7", "t_normed", "t_turned", "t_taken", "brow_in", "b_turned",
                                 "b_taken", "bv_in", "masks", "qk_done", "v_done", "qk_taken",
                                 "v_taken", "s_done", "low_ready", "exps_in", "p_ready", "p_turned", "pt_act", "pt_dve",
                                 "o_done", "o_taken", "v8"))
            w_in = [sem(f"wp_in{k}") for k in range(2)]

            def pair_laps(eng, body):
                def two(i):
                    for k in range(2):
                        body(2 * i + k, k, i)
                laps(eng, PAIRS // 2, two)

            IT = 2 * NT
            ORDER = [9, 0, 8, 1, 7, 2, 6, 3, 5, 4]
            BANKS = len(banks)
            CHUNKS = [(0, 500), (500, 500), (1000, 250)]
            qkv_w = a["L0_ffn_attn_qkv_w"].rearrange("(c p) (k n) -> p c k n", p=128, k=3)

            def groups(n):
                qi = ORDER[n % NT]
                return [(b, min(4, qi + 1 - 4 * b)) for b in range((qi + 4) // 4)]

            home = [sum(len(groups(m)) for m in range(n)) for n in range(IT)]
            owner = [n for n in range(IT) for _ in groups(n)]
            assert len(owner) % BANKS == 0

            def bank_of(n, b):
                return banks[(home[n] + b) % BANKS]

            def held_by(n):
                g = home[n] + len(groups(n)) - 1 - BANKS
                return owner[g] if g >= 0 else -1

            assert all(held_by(n) <= max(n - 2, -1) for n in range(IT))

            AHEAD = 3
            early, made_items = [], 0
            for n in range(-1, IT):
                early.append([])
                while made_items < min(IT, n + AHEAD + 1) and held_by(made_items) < max(n, 0):
                    early[-1].append(made_items)
                    made_items += 1

            SMALL = sum(len(groups(n)) + 3 for n in range(IT))

            with nc.Block() as block:
                @block.sync
                def _(sp):
                    sp.dma_start(w1[:, :], spread(a["L0_ffn_ln1_w"], P)).then_inc(ln1_in, 16)
                    sp.dma_start(b1[:, :], spread(a["L0_ffn_ln1_b"], P)).then_inc(ln1_in, 16)
                    sp.dma_start(brow[:, :], a["L0_ffn_attn_qkv_b"].rearrange("(c p) -> c p", p=128)
                                 ).then_inc(brow_in, 16)
                    sp.dma_start(bv[:, :], spread(a["L0_ffn_attn_qkv_b"][2 * D:3 * D], P)).then_inc(bv_in, 16)

                    def lap(i, w, lap_i):
                        if past(i, 2):
                            sp.wait_ge(v_done, 3 * i - 3)
                        for k in range(3):
                            sp.dma_start(wp[w][:, :, k, :], qkv_w[:, :, k, bass.ds(i * 128, 128)]
                                         ).then_inc(w_in[w], 16)
                    pair_laps(sp, lap)

                @block.gpsimd
                def _(pool):
                    nc.gpsimd.memset(ident_h[:, :], 0.0).then_inc(masks, 1)
                    nc.gpsimd.memset(causal[:, :], 0.0).then_inc(masks, 1)
                    pool.wait_ge(masks, 2)
                    nc.gpsimd.affine_select(out=ident_h[:, :], in_=ident_h[:, :], compare_op=ALU.not_equal, fill=1.0,
                                            base=0, pattern=[[-1, P]], channel_multiplier=1).then_inc(masks, 1)
                    nc.gpsimd.affine_select(out=causal[:, :], in_=causal[:, :], compare_op=ALU.is_ge, fill=-BIG,
                                            base=0, pattern=[[-1, P]], channel_multiplier=1).then_inc(masks, 1)

                @block.tensor
                def _(pe):
                    pe.wait_ge(normed, 1)
                    turn_pe(pe, o, banks, turned, taken)
                    pe.wait_ge(taken, TURNS)
                    pe.wait_ge(brow_in, 16)
                    nc.tensor.transpose(O[0][:, 0:3 * KC], brow[:, :], ident[0:3 * KC, 0:3 * KC]).then_inc(b_turned, 1)
                    pe.wait_ge(masks, 4)
                    pe.wait_ge(b_taken, 1)

                    def scores(n):
                        r, qi = 64 * (n // NT), ORDER[n % NT]
                        for b, m in groups(n):
                            nc.tensor.matmul(bank_of(n, b)[0:P, 0:m * P], qT[r:r + 64, qi * P:qi * P + P],
                                             kT[r:r + 64, 4 * b * P:(4 * b + m) * P], start=True,
                                             stop=(b != qi // 4))
                        nc.tensor.matmul(bank_of(n, qi // 4)[0:P, (qi % 4) * P:(qi % 4) * P + P], ident_h[:, :],
                                         causal[:, :], start=False, stop=True).then_inc(s_done, 1)

                    def lap(i, w, lap_i):
                        pe.wait_ge(w_in[w], 48 * (lap_i + 1))
                        for k in range(2):
                            for b, (s, m) in enumerate(CHUNKS):
                                for c in range(KC):
                                    ins = nc.tensor.matmul(S[k][:, b, 0:m], wp[w][:, c, k, :], tT[:, c, s:s + m],
                                                           start=(c == 0), stop=(c == KC - 1))
                            ins.then_inc(qk_done, 1)
                        pe.wait_ge(qk_taken, 6 * i + 3)
                        for b, (t0, m) in enumerate(GROUPS):
                            for t in range(m):
                                for c in range(KC):
                                    ins = nc.tensor.matmul(S[0][0:P, b, t * 128:t * 128 + 128],
                                                           tT[:, c, (t0 + t) * P:(t0 + t) * P + P], wp[w][:, c, 2, :],
                                                           start=(c == 0), stop=(c == KC - 1))
                            ins.then_inc(v_done, 1)
                        pe.wait_ge(qk_taken, 6 * i + 6)
                        pe.wait_ge(v_taken, 3 * i + 3)
                        for n in range(-1, IT + 1):
                            for m in early[n + 1] if n < IT else ():
                                if held_by(m) >= 0:
                                    pe.wait_ge(pt_act, IT * i + held_by(m) + 1)
                                    pe.wait_ge(pt_dve, IT * i + held_by(m) + 1)
                                scores(m)
                            if n < 0:
                                continue
                            if n < IT:
                                pe.wait_ge(p_ready, IT * i + n + 1)
                                for b, m in groups(n):
                                    for t in range(m):
                                        ins = nc.tensor.transpose(
                                            bank_of(n, b)[0:P, t * P:t * P + P],
                                            prob[:, n % 2, (4 * b + t) * P:(4 * b + t + 1) * P], ident[0:P, 0:P])
                                ins.then_inc(p_turned, 1)
                            if n >= 1:
                                m = n - 1
                                hh, qi = m // NT, ORDER[m % NT]
                                pe.wait_ge(pt_act, IT * i + m + 1)
                                pe.wait_ge(pt_dve, IT * i + m + 1)
                                if m >= 2 or past(i, 1):
                                    pe.wait_ge(o_taken, IT * i + m - 1)
                                for t in range(qi + 1):
                                    ins = nc.tensor.matmul(O[m % 2][0:HD, 0:P], v[:, t, HD * hh:HD * hh + HD],
                                                           pT[:, m % 2, t // 4, (t % 4) * P:(t % 4) * P + P],
                                                           start=(t == 0), stop=(t == qi))
                                ins.then_inc(o_done, 1)
                    pair_laps(pe, lap)

                @block.scalar
                def _(act):
                    root(act, temps)
                    turn_act(act, tT, banks, turned, taken)
                    act.wait_ge(b_taken, 1)

                    def lap(i, *_):
                        for k, to in enumerate((qT, kT)):
                            act.wait_ge(qk_done, 2 * i + k + 1)
                            for b, (s, m) in enumerate(CHUNKS):
                                nc.scalar.activation(to[:, s:s + m], S[k][:, b, 0:m], ACT.Identity,
                                                     bias=bcol[:, bass.ds(i + k * KC, 1)]).then_inc(qk_taken, 1)
                        for n in range(IT + 3):
                            if 2 <= n < IT + 2:
                                m = n - 2
                                act.wait_ge(p_turned, IT * i + m + 1)
                                if m >= 2 or past(i, 1):
                                    act.wait_ge(o_done, IT * i + m - 1)
                                k = groups(m)[0][1] * P
                                nc.scalar.copy(pT[:, m % 2, 0, 0:k], bank_of(m, 0)[0:P, 0:k]).then_inc(pt_act, 1)
                            if n < IT:
                                act.wait_ge(low_ready, IT * i + n + 1)
                                if n >= 2 or past(i, 1):
                                    act.wait_ge(p_turned, IT * i + n - 1)
                                for b, m in groups(n):
                                    ins = nc.scalar.activation(prob[:, n % 2, 4 * b * P:(4 * b + m) * P],
                                                               bank_of(n, b)[0:P, 0:m * P], ACT.Exp,
                                                               bias=low[:, n % 2:n % 2 + 1], scale=HD ** -0.5,
                                                               accum_out=part[:, n % 2, b:b + 1])
                                ins.then_inc(exp_done, 1)
                            if n >= 3:
                                m = n - 3
                                r, q = HD * (m // NT), ORDER[m % NT] * P
                                act.wait_ge(o_done, IT * i + m + 1)
                                nc.scalar.copy(oT[r:r + HD, bass.ds(i, 1), q:q + P].rearrange("p a n -> p (a n)"),
                                               O[m % 2][0:HD, 0:P]).then_inc(o_taken, 1)
                    pair_laps(act, lap)

                @block.vector
                def _(dve):
                    ch = Chain(dve, v7)
                    dve.wait_ge(ln1_in, 32)
                    layer_norm(ch, h, o, temps, w=w1, b=b1)
                    dve.sem_inc(normed, 1)
                    dve.wait_ge(b_turned, 1)
                    nc.vector.tensor_copy(bcol[:, :], O[0][:, 0:3 * KC]).then_inc(b_taken, 1)
                    dve.wait_ge(bv_in, 16)

                    def lap(i, *_):
                        for b, (t0, m) in enumerate(GROUPS):
                            dve.wait_ge(v_done, 3 * i + b + 1)
                            nc.vector.tensor_tensor(
                                v[:, t0:t0 + m, :], S[0][0:P, b, 0:m * 128].rearrange("p (t n) -> p t n", n=128),
                                bv[:, bass.ds(i * 128, 128)].unsqueeze(1).to_broadcast([P, m, 128]), ALU.add
                            ).then_inc(v_taken, 1)
                        small = Chain(dve, v8, base=SMALL * i)
                        for n in range(IT + 2):
                            if n >= 2:
                                m, k = n - 2, n % 2
                                dve.wait_ge(p_turned, IT * i + m + 1)
                                if m >= 2 or past(i, 1):
                                    dve.wait_ge(o_done, IT * i + m - 1)
                                for b, c in groups(m)[1:]:
                                    ins = nc.vector.tensor_copy(pT[:, k, b, 0:c * P], bank_of(m, b)[0:P, 0:c * P])
                                if len(groups(m)) > 1:
                                    ins.then_inc(pt_dve, 1)
                                else:
                                    dve.sem_inc(pt_dve, 1)
                            if n < IT:
                                k = n % 2
                                dve.wait_ge(s_done, IT * i + n + 1)
                                for b, m in groups(n):
                                    small.do(nc.vector.tensor_reduce(bank_high[:, k, b:b + 1],
                                                                     bank_of(n, b)[0:P, 0:m * P], AX.X, ALU.max))
                                small.wait()
                                small.link(nc.vector.tensor_reduce(high[:, k:k + 1],
                                                                   bank_high[:, k, 0:len(groups(n))], AX.X, ALU.max))
                                nc.vector.tensor_scalar(low[:, k:k + 1], high[:, k:k + 1], -HD ** -0.5, None,
                                                        ALU.mult).then_inc(low_ready, 1)
                            if 1 <= n <= IT:
                                m, k = n - 1, (n - 1) % 2
                                dve.wait_ge(exp_done, IT * i + m + 1)
                                small.link(nc.vector.tensor_reduce(total[:, k:k + 1], part[:, k, 0:len(groups(m))],
                                                                   AX.X, ALU.add))
                                small.link(nc.vector.reciprocal(tinv[:, k:k + 1], total[:, k:k + 1]))
                                keys = prob[:, k, 0:(ORDER[m % NT] + 1) * P]
                                nc.vector.tensor_scalar(keys, keys, tinv[:, k:k + 1], None, ALU.mult
                                                        ).then_inc(p_ready, 1)
                        assert small.n == SMALL
                    pair_laps(dve, lap)
            end_stage()

        with ExitStack() as ctx:
            wo = sb("wo", [128, KC, D], F32, ctx)
            bo = sb("bo", [P, D], F32, ctx)
            w2 = sb("ln2w", [P, D], F32, ctx)
            b2 = sb("ln2b", [P, D], F32, ctx)
            row = sb("row", [P, D], F32, ctx)
            temps = norm_temps(ctx, "ln2")
            bank = [ps(f"pr{k}_", [128, 512], ctx) for k in range(8)]
            wo_in, b_in, done, v9 = (sem(n) for n in ("wo_in", "bo_in", "proj_done", "v9"))
            with nc.Block() as block:
                @block.sync
                def _(sp):
                    sp.dma_start(wo[:, :, :], a["L0_ffn_attn_proj_w"].rearrange("(c p) n -> p c n", p=128)
                                 ).then_inc(wo_in, 16)
                    sp.dma_start(bo[:, :], spread(a["L0_ffn_attn_proj_b"], P)).then_inc(b_in, 16)
                    sp.dma_start(w2[:, :], spread(a["L0_ffn_ln2_w"], P)).then_inc(b_in, 16)
                    sp.dma_start(b2[:, :], spread(a["L0_ffn_ln2_b"], P)).then_inc(b_in, 16)

                @block.tensor
                def _(pe):
                    pe.wait_ge(wo_in, 16)
                    for t in range(NT):
                        if t >= 4:
                            pe.wait_ge(v9, 3 * (t - 4) + 1)
                        for k in range(2):
                            for c in range(KC):
                                ins = nc.tensor.matmul(bank[2 * (t % 4) + k][0:P, 0:384], oT[:, c, t * P:t * P + P],
                                                       wo[:, c, 384 * k:384 * k + 384], start=(c == 0),
                                                       stop=(c == KC - 1))
                        ins.then_inc(done, 1)

                @block.scalar
                def _(act):
                    root(act, temps)

                @block.vector
                def _(dve):
                    ch = Chain(dve, v9)
                    dve.wait_ge(b_in, 48)
                    for t in range(NT):
                        dve.wait_ge(done, t + 1)
                        nc.vector.tensor_tensor(row[:, 0:384], bank[2 * (t % 4)][0:P, 0:384], bo[:, 0:384], ALU.add)
                        ch.link(nc.vector.tensor_tensor(row[:, 384:D], bank[2 * (t % 4) + 1][0:P, 0:384],
                                                        bo[:, 384:D], ALU.add))
                        ch.do(nc.vector.tensor_tensor(h[:, t, :], h[:, t, :], row[:, :], ALU.add))
                        ch.do(nc.vector.tensor_tensor(x[:, t, :], x[:, t, :], row[:, :], ALU.add))
                        ch.wait()
                    layer_norm(ch, h, o, temps, w=w2, b=b2)
            end_stage()

        with ExitStack() as ctx:
            uT = sb("uT", [128, KC, N], F32, ctx)
            wg = sb("wg", [128, KC, NX], F32, ctx)
            tri = sb("tri", [P, P], F32, ctx)
            expert = sb("expert", [P, NX], F32, ctx)
            spare = sb("spare", [P, 2 * NT], F32, ctx)
            lgt = sb("lgt", [P, NT, NX], F32, ctx)
            best = sb("best", [P, NT, NX], F32, ctx)
            which = sb("which", [P, NT, NX], U32, ctx)
            which_f = sb("which_f", [P, 2, NT], F32, ctx)
            gap = sb("gap", [P, NT], F32, ctx)
            prob0 = sb("prob0", [P, 2, NT], F32, ctx)
            hot = sb("hot", [P, 2, NT, NX], F32, ctx)
            base = sb("base", [P, 2 * NT, NX], F32, ctx)
            tot = sb("tot", [P, 2 * NT, NX], F32, ctx)
            rank = sb("rank", [P, 2 * NT], F32, ctx)
            keep = sb("keep", [P, 2 * NT], F32, ctx)
            slot = sb("slot", [P, 2 * NT], F32, ctx)
            slot_write = sb("slot_write", [P, 2 * NT], I32, ctx)
            bank = [ps(f"ro{k}_", [128, 512], ctx) for k in range(4)]
            lg_p = ps("lg_p", [128, 512], ctx)
            cum_p = ps("cum_p", [128, 512], ctx)
            tot_p = ps("tot_p", [128, 512], ctx)
            turned, taken, wg_in, made, lg_done, gap_ready, exp_done, hot_ready, counted, v10, slots_ready, sent = (
                sem(n) for n in ("u_turned", "uT_taken", "wg_in", "made", "lg_done", "gap_ready", "gap_exp",
                                 "hot_ready", "counted", "v10", "slots_ready", "sent"))
            with nc.Block() as block:
                @block.sync
                def _(sp):
                    sp.dma_start(wg[:, :, :], a["L0_ffn_w_g"].rearrange("(c p) e -> p c e", p=128)).then_inc(wg_in, 16)

                @block.gpsimd
                def _(pool):
                    nc.gpsimd.memset(tri[:, :], 1.0).then_inc(made, 1)
                    nc.gpsimd.iota(expert[:, :], [[1, NX]], base=0, channel_multiplier=0,
                                   allow_small_or_imprecise_dtypes=True).then_inc(made, 1)
                    nc.gpsimd.iota(spare[:, :], [[P, 2 * NT]], base=SLOTS, channel_multiplier=1,
                                   allow_small_or_imprecise_dtypes=True).then_inc(made, 1)
                    pool.wait_ge(made, 3)
                    nc.gpsimd.affine_select(out=tri[:, :], in_=tri[:, :], compare_op=ALU.is_ge, fill=0.0, base=0,
                                            pattern=[[1, P]], channel_multiplier=-1).then_inc(made, 1)
                    pool.wait_ge(slots_ready, 1)
                    for k in range(2):
                        for t in range(NT):
                            b = k * NT + t
                            nc.gpsimd.indirect_dma_start(
                                out=slot_in, in_=o[:, t, :], in_offset=None,
                                out_offset=bass.IndirectOffsetOnAxis(ap=slot_write[:, b:b + 1], axis=0)
                            ).then_inc(sent, 16)
                    pool.wait_ge(sent, 32 * NT)

                @block.tensor
                def _(pe):
                    turn_pe(pe, o, bank, turned, taken)
                    pe.wait_ge(taken, TURNS)
                    pe.wait_ge(wg_in, 16)
                    for t in range(NT):
                        for c in range(KC):
                            ins = nc.tensor.matmul(lg_p[0:P, t * NX:t * NX + NX], uT[:, c, t * P:t * P + P],
                                                   wg[:, c, :], start=(c == 0), stop=(c == KC - 1))
                    ins.then_inc(lg_done, 1)
                    pe.wait_ge(made, 4)
                    pe.wait_ge(hot_ready, 2)
                    all_hot = hot[:, :, :, :].rearrange("p k t e -> p (k t e)")
                    nc.tensor.matmul(cum_p[0:P, 0:2 * NT * NX], tri[:, :], all_hot, start=True, stop=True
                                     ).then_inc(counted, 1)
                    nc.tensor.matmul(tot_p[0:P, 0:2 * NT * NX], ones[0:P, 0:P], all_hot, start=True, stop=True
                                     ).then_inc(counted, 1)

                @block.scalar
                def _(act):
                    turn_act(act, uT, bank, turned, taken)
                    act.wait_ge(gap_ready, 1)
                    nc.scalar.activation(gap[:, :], gap[:, :], ACT.Exp).then_inc(exp_done, 1)

                @block.vector
                def _(dve):
                    ch = Chain(dve, v10)
                    dve.wait_ge(lg_done, 1)
                    ch.link(nc.vector.tensor_copy(lgt[:, :, :], lg_p[0:P, 0:NT * NX].rearrange("p (t e) -> p t e", e=NX)))
                    for t in range(NT):
                        ch.do(nc.vector.max(best[:, t, :], lgt[:, t, :]))
                    ch.wait()
                    for t in range(NT):
                        ch.do(nc.vector.max_index(which[:, t, :], best[:, t, :], lgt[:, t, :]))
                    ch.wait()
                    nc.vector.tensor_tensor(gap[:, :], best[:, :, 1], best[:, :, 0], ALU.subtract).then_inc(gap_ready, 1)
                    for k in range(2):
                        ch.do(nc.vector.tensor_copy(which_f[:, k, :], which[:, :, k]))
                    ch.wait()
                    dve.wait_ge(made, 3)
                    for k in range(2):
                        nc.vector.tensor_tensor(hot[:, k, :, :], expert[:, :].unsqueeze(1).to_broadcast([P, NT, NX]),
                                                which_f[:, k, :].unsqueeze(2).to_broadcast([P, NT, NX]),
                                                ALU.is_equal).then_inc(hot_ready, 1)
                    dve.wait_ge(exp_done, 1)
                    ch.link(nc.vector.tensor_scalar(prob0[:, 0, :], gap[:, :], 1.0, None, ALU.add))
                    ch.link(nc.vector.reciprocal(prob0[:, 0, :], prob0[:, 0, :]))
                    ch.link(nc.vector.tensor_tensor(prob0[:, 1, :], prob0[:, 0, :], gap[:, :], ALU.mult))
                    dve.wait_ge(counted, 2)
                    ch.do(nc.vector.tensor_copy(tot[:, :, :], tot_p[0:P, 0:2 * NT * NX]
                                                .rearrange("p (b e) -> p b e", e=NX)))
                    ch.do(nc.vector.memset(base[:, 0, :], 0.0))
                    ch.wait()
                    for b in range(1, 2 * NT):
                        ch.link(nc.vector.tensor_tensor(base[:, b, :], base[:, b - 1, :], tot[:, b - 1, :], ALU.add))
                    ch.link(nc.vector.tensor_tensor(base[:, :, :], base[:, :, :], cum_p[0:P, 0:2 * NT * NX]
                                                    .rearrange("p (b e) -> p b e", e=NX), ALU.add))
                    ch.link(nc.vector.tensor_tensor(base[:, :, :], base[:, :, :],
                                                    hot[:, :, :, :].rearrange("p k t e -> p (k t) e"), ALU.mult))
                    ch.link(nc.vector.tensor_reduce(rank[:, :], base[:, :, :], AX.X, ALU.add))
                    ch.link(nc.vector.tensor_scalar(keep[:, :], rank[:, :], float(CAP), None, ALU.is_le))
                    ch.link(nc.vector.scalar_tensor_tensor(out=slot[:, :], scalar=float(CAP), in1=rank[:, :],
                                                           in0=which_f[:, :, :].rearrange("p k t -> p (k t)"),
                                                           op0=ALU.mult, op1=ALU.add))
                    ch.link(nc.vector.tensor_scalar(slot[:, :], slot[:, :], -1.0, None, ALU.add))
                    ch.link(nc.vector.tensor_tensor(rank[:, :], slot[:, :], keep[:, :], ALU.mult))
                    ch.do(nc.vector.tensor_copy(slot_read[:, :], rank[:, :]))
                    ch.do(nc.vector.tensor_tensor(wgt[:, :], prob0[:, :, :].rearrange("p k t -> p (k t)"),
                                                  keep[:, :], ALU.mult))
                    ch.do(nc.vector.tensor_tensor(slot[:, :], slot[:, :], spare[:, :], ALU.subtract))
                    ch.wait()
                    ch.link(nc.vector.tensor_tensor(slot[:, :], slot[:, :], keep[:, :], ALU.mult))
                    ch.link(nc.vector.tensor_tensor(slot[:, :], slot[:, :], spare[:, :], ALU.add))
                    nc.vector.tensor_copy(slot_write[:, :], slot[:, :]).then_inc(slots_ready, 1)
            end_stage()

        mid.close()

        with ExitStack() as ctx:
            R = 3
            FW = FJ * 128
            TILES = FG * FJ
            wf = sb("wf", [128, R, KC, FW], F32, ctx)
            wj = sb("wj", [128, R, FJ, D], F32, ctx)
            wf_part = [sb(f"wf_{n}", [128, 2, KC, FW], F32R, ctx) for n in ("high", "low")]
            wj_part = [sb(f"wj_{n}", [128, 2, FJ, D], F32R, ctx) for n in ("high", "low")]
            xT_part = [sb(f"xT_{n}", [128, KC, CAP], F32R, ctx) for n in ("high", "low")]
            hid_part = [sb(f"hid_{n}", [128, 2, FJ, CAP], F32R, ctx) for n in ("high", "low")]
            hid = sb("hid", [128, 2, CAP], F32, ctx)
            xs = sb("xs", [128, 3, D], F32, ctx)
            xs3 = sb("xs3", [6, D], F32, ctx)
            yT = sb("yT", [128, KC, CAP], F32, ctx)
            ys = sb("ys", [128, 3, D], F32, ctx)
            ys3 = sb("ys3", [6, D], F32, ctx)
            fb_rows = sb("fb_rows", [96, 2, 128], F32, ctx)
            jb_rows = sb("jb_rows", [48, 128], F32, ctx)
            fb = sb("fb", [128, NX * TILES], F32, ctx)
            jb = sb("jb", [128, NX * KC], F32, ctx)
            ring = [ps(f"ring{k}_", [128, 512], ctx) for k in range(2)]
            accu = [ps(f"accu{k}_", [128, 512], ctx) for k in range(KC)]
            wf_in = [sem(f"wf_in{k}") for k in range(R)]
            wj_in = [sem(f"wj_in{k}") for k in range(R)]
            (bias_in, bias_turned, bias_taken, xs_in, loads, stores, wf_high, wf_split, wj_high, wj_split, x_turned,
             x_high, x_split, up_done, up_taken, hid_high, hid_split, pj_done, y_taken, y_turned, y_rows, stored) = (
                sem(n) for n in ("bias_in", "bias_turned", "bias_taken", "xs_in", "loads", "stores", "wf_high",
                                 "wf_split", "wj_high", "wj_split", "x_turned", "x_high", "x_split", "up_done",
                                 "up_taken", "hid_high", "hid_split", "pj_done", "y_taken", "y_turned", "y_rows",
                                 "stored"))
            YU = 2 * len(ROWS)
            LAP = ([("up", i) for i in range(2 * FJ)] + [("y", i) for i in range(YU // 2)]
                   + [("up", i) for i in range(2 * FJ, 3 * FJ)] + [("y", i) for i in range(YU // 2, YU)]
                   + [("up", i) for i in range(3 * FJ, TILES)] + [("x", i) for i in range(KC)])
            fc_w = a["L0_ffn_exp_fc_w"].rearrange("e (c p) f -> p (e c) f", p=128)
            pj_w = a["L0_ffn_exp_proj_w"].rearrange("e (j p) d -> p (e j) d", p=128)

            def rows_of(big, small, s0, n):
                return big[:, s0 // 128, :] if n == 128 else small[:, :]

            def expert_laps(eng, body, peeled=1):
                for e in range(peeled):
                    body(e, False)
                with eng.Fori(peeled, NX - 1) as e:
                    body(e, False)
                body(NX - 1, True)

            with nc.Block() as block:
                @block.sync
                def _(sp):
                    fbr = a["L0_ffn_exp_fc_b"].rearrange("e a (g p) -> (e a g) p", p=128)
                    for k in range(2):
                        sp.dma_start(fb_rows[:, k, :], fbr[96 * k:96 * k + 96, :]).then_inc(bias_in, 16)
                    sp.dma_start(jb_rows[:, :], a["L0_ffn_exp_proj_b"].rearrange("e a (c p) -> (e a c) p", p=128)
                                 ).then_inc(bias_in, 16)

                    def lap(e):
                        for g in range(FG):
                            if g >= R or past(e, 1):
                                sp.wait_ge(wf_split, FG * e + g - R + 1)
                            sp.dma_start(wf[:, g % R, :, :], fc_w[:, bass.ds(e * KC, KC), g * FW:(g + 1) * FW]
                                         ).then_inc(wf_in[g % R], 16)
                            if g >= R or past(e, 1):
                                sp.wait_ge(wj_split, FG * e + g - R + 1)
                            sp.dma_start(wj[:, g % R, :, :], pj_w[:, bass.ds(e * TILES + g * FJ, FJ), :]
                                         ).then_inc(wj_in[g % R], 16)
                    laps(sp, NX, lap)

                @block.gpsimd
                def _(pool):
                    def load(e):
                        pool.dma_start(xs[:, :, :], slot_in[bass.ds(e * CAP, 384), :]
                                       .rearrange("(k p) d -> p k d", p=128)).then_inc(xs_in, 16)
                        pool.dma_start(xs3[:, :], slot_in[bass.ds(e * CAP + 384, 6), :]).then_inc(xs_in, 16)

                    def store(e):
                        pool.wait_ge(y_rows, YU * e + YU)
                        pool.sem_inc(stores, 1)
                        pool.dma_start(slot_out[bass.ds(e * CAP, 384), :].rearrange("(k p) d -> p k d", p=128),
                                       ys[:, :, :]).then_inc(stored, 16)
                        pool.dma_start(slot_out[bass.ds(e * CAP + 384, 6), :], ys3[:, :]).then_inc(stored, 16)

                    load(0)
                    pool.wait_ge(x_turned, KC)
                    pool.sem_inc(loads, 1)
                    load(1)
                    with pool.Fori(1, NX - 1) as e:
                        store(e - 1)
                        pool.wait_ge(x_turned, KC * e + KC)
                        pool.sem_inc(loads, 1)
                        load(e + 1)
                    store(NX - 2)
                    store(NX - 1)
                    pool.wait_ge(stored, 32 * NX)

                @block.tensor
                def _(pe):
                    pe.wait_ge(bias_in, 48)
                    for k in range(2):
                        nc.tensor.transpose(accu[k][:, 0:96], fb_rows[:, k, :], ident[0:96, 0:96]
                                            ).then_inc(bias_turned, 1)
                    nc.tensor.transpose(accu[2][:, 0:48], jb_rows[:, :], ident[0:48, 0:48]).then_inc(bias_turned, 1)
                    pe.wait_ge(bias_taken, 3)

                    def product(bank, weights, moving, start, stop):
                        for k, (p, q) in enumerate(((0, 0), (0, 1), (1, 0))):
                            ins = nc.tensor.matmul(bank, weights[p], moving[q], start=(start and k == 0),
                                                   stop=(stop and k == 2))
                        return ins

                    def turn_in(e, c, bank):
                        pe.wait_ge(xs_in, 32 * (e + 1))
                        for s0, n in ROWS:
                            ins = nc.tensor.transpose(bank[:, s0:s0 + n],
                                                      rows_of(xs, xs3, s0, n)[:, c * 128:c * 128 + 128],
                                                      ident[0:n, 0:n])
                        ins.then_inc(x_turned, 1)

                    def turn_out(i, bank):
                        s0, n = ROWS[i // 2]
                        for c in range(3):
                            ins = nc.tensor.transpose(bank[0:n, c * 128:c * 128 + 128],
                                                      yT[:, 3 * (i % 2) + c, s0:s0 + n], ident[:, :])
                        ins.then_inc(y_turned, 1)

                    def lap(e, last):
                        first = not past(e, 1)
                        uses = [use for use in LAP if not (first and use[0] == "y") and not (last and use[0] == "x")]
                        taken_by = {"up": (up_taken, TILES * e), "y": (y_rows, YU * e - YU),
                                    "x": (x_split, KC * e + KC)}
                        step = iter(range(len(uses)))

                        def claim():
                            u = next(step)
                            if u >= 2:
                                kind, i = uses[u - 2]
                                signal, base = taken_by[kind]
                                pe.wait_ge(signal, base + i + 1)
                            return ring[u % 2]

                        def up(g):
                            pe.wait_ge(wf_split, FG * e + g + 1)
                            for j in range(FJ):
                                bank = claim()
                                for c in range(KC):
                                    ins = product(bank[:, 0:CAP],
                                                  [w[:, g % 2, c, j * 128:j * 128 + 128] for w in wf_part],
                                                  [xT[:, c, :] for xT in xT_part], c == 0, c == KC - 1)
                                ins.then_inc(up_done, 1)

                        def down(g, turns):
                            pe.wait_ge(wj_split, FG * e + g + 1)
                            pe.wait_ge(hid_split, TILES * e + (g + 1) * FJ)
                            if g == 0 and past(e, 1):
                                pe.wait_ge(y_taken, KC * e)
                            for j in range(FJ):
                                for c in range(KC):
                                    ins = product(accu[c][:, 0:CAP],
                                                  [w[:, g % 2, j, c * 128:c * 128 + 128] for w in wj_part],
                                                  [part[:, g % 2, j, :] for part in hid_part],
                                                  g == 0 and j == 0, g == FG - 1 and j == FJ - 1)
                                    if j == FJ - 1 and c == KC - 1:
                                        ins.then_inc(pj_done, 1)
                                    if c % 2 == 1 and turns:
                                        turns.pop(0)()
                            assert not turns

                        pe.wait_ge(x_split, KC * e + KC)
                        for g in range(FG):
                            up(g)
                            if g in (1, 2) and not first:
                                down(g - 1, [lambda i=i: turn_out(i, claim())
                                             for i in range((g - 1) * YU // 2, g * YU // 2)])
                            elif g:
                                down(g - 1, [])
                        down(FG - 1, [] if last else [lambda c=c: turn_in(e + 1, c, claim()) for c in range(KC)])

                    for c in range(KC):
                        if c >= 2:
                            pe.wait_ge(x_split, c - 1)
                        turn_in(0, c, ring[c % 2])
                    expert_laps(pe, lap)
                    pe.wait_ge(y_taken, KC * NX)
                    pe.wait_ge(up_taken, TILES * NX)
                    for i in range(YU):
                        if i >= 2:
                            pe.wait_ge(y_rows, YU * (NX - 1) + i - 1)
                        turn_out(i, ring[i % 2])

                @block.scalar
                def _(act):
                    act.wait_ge(bias_taken, 3)

                    def lap(e, last):
                        def high_fc(g):
                            act.wait_ge(wf_in[g % R], 16 * (FG // R * e + g // R + 1))
                            if g >= 2 or past(e, 1):
                                act.wait_ge(up_done, TILES * e + (g - 1) * FJ)
                            nc.scalar.activation(wf_part[0][:, g % 2, :, :], wf[:, g % R, :, :], ACT.Copy
                                                 ).then_inc(wf_high, 1)

                        if not past(e, 1):
                            high_fc(0)
                        for g in range(FG):
                            if not (last and g == FG - 1):
                                high_fc(g + 1)
                            act.wait_ge(wj_in[g % R], 16 * (FG // R * e + g // R + 1))
                            if g >= 2 or past(e, 1):
                                act.wait_ge(pj_done, FG * e + g - 1)
                            nc.scalar.activation(wj_part[0][:, g % 2, :, :], wj[:, g % R, :, :], ACT.Copy
                                                 ).then_inc(wj_high, 1)
                            for j in range(FJ):
                                i = g * FJ + j
                                act.wait_ge(up_done, TILES * e + i + 1)
                                if i >= 2 or past(e, 1):
                                    act.wait_ge(hid_split, TILES * e + i - 1)
                                nc.scalar.activation(hid[:, i % 2, :], ring[i % 2][:, 0:CAP], ACT.Gelu,
                                                     bias=fb[:, bass.ds(e * TILES + i, 1)]).then_inc(up_taken, 1)
                    expert_laps(act, lap)

                @block.vector
                def _(dve):
                    dve.wait_ge(bias_turned, 3)
                    for k in range(2):
                        nc.vector.tensor_copy(fb[:, 96 * k:96 * k + 96], accu[k][:, 0:96]).then_inc(bias_taken, 1)
                    nc.vector.tensor_copy(jb[:, :], accu[2][:, 0:48]).then_inc(bias_taken, 1)
                    dve.wait_ge(bias_taken, 3)

                    def low(dest, source, high):
                        return nc.vector.tensor_tensor(dest, source, high.bitcast(F32), ALU.subtract)

                    def split_slots(e, c):
                        dve.wait_ge(x_turned, KC * e + c + 1)
                        nc.vector.tensor_copy(xT_part[0][:, c, :], ring[c % 2][:, 0:CAP]).then_inc(x_high, 1)
                        dve.wait_ge(x_high, KC * e + c + 1)
                        low(xT_part[1][:, c, :], ring[c % 2][:, 0:CAP], xT_part[0][:, c, :]).then_inc(x_split, 1)

                    def take_sums(e):
                        dve.wait_ge(pj_done, FG * e + FG)
                        for c in range(KC):
                            nc.vector.tensor_scalar(yT[:, c, :], accu[c][:, 0:CAP], jb[:, bass.ds(e * KC + c, 1)],
                                                    None, ALU.add).then_inc(y_taken, 1)

                    def take_rows(e, i):
                        s0, n = ROWS[i // 2]
                        dve.wait_ge(y_turned, YU * e + i + 1)
                        nc.vector.tensor_copy(rows_of(ys, ys3, s0, n)[:, 384 * (i % 2):384 * (i % 2) + 384],
                                              ring[i % 2][0:n, 0:384]).then_inc(y_rows, 1)

                    def lap(e, last):
                        def low_fc(g):
                            dve.wait_ge(wf_high, FG * e + g + 1)
                            low(wf_part[1][:, g % 2, :, :], wf[:, g % R, :, :], wf_part[0][:, g % 2, :, :]
                                ).then_inc(wf_split, 1)

                        if not past(e, 1):
                            low_fc(0)
                        for g in range(FG):
                            if not (last and g == FG - 1):
                                low_fc(g + 1)
                            dve.wait_ge(wj_high, FG * e + g + 1)
                            low(wj_part[1][:, g % 2, :, :], wj[:, g % R, :, :], wj_part[0][:, g % 2, :, :]
                                ).then_inc(wj_split, 1)
                            if g == 0 and past(e, 1):
                                take_sums(e - 1)
                            for j in range(FJ):
                                i = g * FJ + j
                                dve.wait_ge(up_taken, TILES * e + i + 1)
                                if j == 0 and (g >= 2 or past(e, 1)):
                                    dve.wait_ge(pj_done, FG * e + g - 1)
                                nc.vector.tensor_copy(hid_part[0][:, g % 2, j, :], hid[:, i % 2, :]
                                                      ).then_inc(hid_high, 1)
                                dve.wait_ge(hid_high, TILES * e + i + 1)
                                low(hid_part[1][:, g % 2, j, :], hid[:, i % 2, :], hid_part[0][:, g % 2, j, :]
                                    ).then_inc(hid_split, 1)
                            if g in (1, 2) and past(e, 1):
                                if g == 1 and past(e, 2):
                                    dve.wait_ge(stored, 32 * (e - 1))
                                for i in range((g - 1) * YU // 2, g * YU // 2):
                                    take_rows(e - 1, i)
                        if not last:
                            for c in range(KC):
                                split_slots(e + 1, c)

                    for c in range(KC):
                        split_slots(0, c)
                    expert_laps(dve, lap, peeled=2)
                    take_sums(NX - 1)
                    dve.wait_ge(stored, 32 * (NX - 1))
                    for i in range(YU):
                        take_rows(NX - 1, i)
            end_stage()

        with ExitStack() as ctx:
            got_row = sb("got_row", [P, 4, 2, D], F32, ctx)
            got = [sem(f"got_row{k}") for k in range(4)]
            v11, summed, stored = sem("v11"), sem("out_summed"), sem("out_stored")
            with nc.Block() as block:
                @block.gpsimd
                def _(pool):
                    for t in range(NT):
                        if t >= 4:
                            pool.wait_ge(summed, t - 3)
                        for k in range(2):
                            nc.gpsimd.indirect_dma_start(
                                out=got_row[:, t % 4, k, :], out_offset=None, in_=slot_out,
                                in_offset=bass.IndirectOffsetOnAxis(
                                    ap=slot_read[:, k * NT + t:k * NT + t + 1], axis=0)
                            ).then_inc(got[t % 4], 16)

                @block.vector
                def _(dve):
                    for t in range(NT):
                        dve.wait_ge(got[t % 4], 32 * (t // 4 + 1))
                        for k, s in ((0, v11), (1, summed)):
                            nc.vector.scalar_tensor_tensor(
                                out=x[:, t, :], in0=got_row[:, t % 4, k, :],
                                scalar=wgt[:, k * NT + t:k * NT + t + 1], in1=x[:, t, :],
                                op0=ALU.mult, op1=ALU.add).then_inc(s, 1)
                            if k == 0:
                                dve.wait_ge(v11, t + 1)

                @block.sync
                def _(sp):
                    for t in range(NT):
                        sp.wait_ge(summed, t + 1)
                        sp.dma_start(out[t * P:t * P + P, :], x[:, t, :]).then_inc(stored, 16)
                    sp.wait_ge(stored, 16 * NT)
            end_stage()


_INS = ["x", "src", "dst"] + ["L0_gnn_" + n for n in
                              ("Wsrc", "bsrc", "Wdst", "bdst", "attn", "ln_w", "ln_b", "on_w", "on_b")] + [
    "L0_ffn_" + n for n in ("ln1_w", "ln1_b", "ln2_w", "ln2_b", "attn_qkv_w", "attn_qkv_b", "attn_proj_w",
                            "attn_proj_b", "w_g", "exp_fc_w", "exp_fc_b", "exp_proj_w", "exp_proj_b")]


def kernel(**inputs):
    import numpy as _np
    import concourse.bacc as _bacc
    from concourse import mybir as _mybir
    from concourse.bass_utils import run_bass_kernel_spmd as _run

    nc = _bacc.Bacc("TRN2", target_bir_lowering=False, num_devices=1)
    arrays, args = {}, {}
    for name in _INS:
        v = _np.ascontiguousarray(inputs[name])
        arrays[f"in_{name}_dram"] = v
        args[name] = nc.dram_tensor(f"in_{name}_dram", v.shape, _mybir.dt.from_np(v.dtype), kind="ExternalInput").ap()
    out = nc.dram_tensor("out_0_dram", (N, D), _mybir.dt.float32, kind="ExternalOutput").ap()
    build(nc, args, out)
    r = _run(nc, [arrays], core_ids=[0])
    return r.results[0]["out_0_dram"]
```

```python
from contextlib import ExitStack

import concourse.bass as bass
from concourse import mybir

ALU = mybir.AluOpType
ACT = mybir.ActivationFunctionType
AX = mybir.AxisListType
F32 = mybir.dt.float32
F32R = mybir.dt.float32r
BF16 = mybir.dt.bfloat16
I32 = mybir.dt.int32
U32 = mybir.dt.uint32

N, D = 1250, 768
P, NT = 125, 10
KC = D // 128
E, EP = 20000, 128
ET = -(-E // EP)
ETP = 160
ITEMS = 174
GH, GD = 8, D // 8
DX = D + GH
L = 2
CH = 16
CE = E // CH
NH, HD = 12, 64
PAIRS = NH // 2
NX, F = 8, 4 * D
CAP = 390
SLOTS = NX * CAP
FG = 12
FJ = F // 128 // FG
ROWS = [(0, 128), (128, 128), (256, 128), (384, 6)]
LN_EPS = 1e-5
SLOPE = 0.2
BIG = 1e30
FAR = 1e6
GROUPS = [(0, 4), (4, 4), (8, 2)]


def past(t, n):
    return not isinstance(t, int) or t >= n


class Chain:

    def __init__(self, eng, sem, base=0):
        self.eng, self.sem, self.base, self.n = eng, sem, base, 0

    def do(self, ins):
        ins.then_inc(self.sem, 1)
        self.n += 1

    def wait(self):
        self.eng.wait_ge(self.sem, self.base + self.n)

    def link(self, ins):
        self.do(ins)
        self.wait()


def laps(eng, n, body):
    body(0)
    with eng.Fori(1, n) as i:
        body(i)


def build(nc, a, out):
    with ExitStack() as top:
        def sb(name, shape, dt=F32, ctx=top):
            return ctx.enter_context(nc.sbuf_tensor(name, shape, dt))

        def ps(name, shape, ctx, dt=F32):
            return ctx.enter_context(nc.psum_tensor(name, shape, dt))

        live = []

        def sem(name):
            live.append(nc.alloc_semaphore(name=name))
            return live[-1]

        def end_stage():
            nc.clear_and_free_semaphores(live)
            live.clear()
            nc.all_engine_barrier()

        def dram(name, shape, dt=F32):
            return nc.dram_tensor(name, shape, dt, kind="Internal").ap()

        def spread(row, parts):
            return row.partition_broadcast(parts)

        def rows(t):
            return t.rearrange("(t p) d -> p t d", p=P)

        hs_dram = dram("hs_dram", (N, DX))
        hd_dram = dram("hd_dram", (N, DX))
        logit_dram = dram("logit_dram", (GH, ETP * EP))
        ex_dram = dram("ex_dram", (GH, ETP * EP))
        pair_dram = dram("pair_dram", (128, 2))
        top_dram = dram("top_dram", (128, 2))
        slot_in = dram("slot_in", (SLOTS + 2 * N, D))
        slot_out = dram("slot_out", (SLOTS, D))

        x = sb("x", [P, NT, D])
        wgt = sb("wgt", [P, 2 * NT])
        slot_read = sb("slot_read", [P, 2 * NT], I32)
        ident = sb("ident", [128, 128])
        mid = top.enter_context(ExitStack())
        h = sb("h", [P, NT, D], F32, mid)
        ones = sb("ones", [128, 128], F32, mid)
        edge = mid.enter_context(ExitStack())
        lanes = sb("lanes", [128, P], F32, edge)
        src_item = sb("src_item", [128, ITEMS], I32, edge)
        dst_idx = sb("dst_idx", [128, ETP], I32, edge)
        dst_rel = sb("dst_rel", [128, ITEMS], F32, edge)
        win = sb("win", [1, ITEMS], I32, edge)
        cut_tile = sb("cut_tile", [128, NT - 1], I32, edge)
        dstc = sb("dstc", [128, CE], F32, edge)
        change = sb("change", [128, CE + 1], F32, edge)
        change2 = sb("change2", [GH, 2 * CH + 1], F32, edge)

        def layer_norm(ch, source, dest, temps, w=None, b=None):
            stats, mv, rstd, shift, var_ready, std_ready, shift_ready, scaled, pooled = temps
            for t in range(NT):
                for k in range(2):
                    ch.do(nc.vector.bn_stats(stats[:, t, 6 * k:6 * k + 6], source[:, t, 384 * k:384 * k + 384]))
            ch.wait()
            for t in range(NT):
                ch.do(nc.vector.bn_aggr(mv[:, t, :], stats[:, t, :]))
            ch.wait()
            nc.vector.tensor_scalar(rstd[:, :], mv[:, :, 1], LN_EPS, None, ALU.add).then_inc(var_ready, 1)
            ch.eng.wait_ge(std_ready, 1)
            ch.link(nc.vector.reciprocal(rstd[:, :], rstd[:, :]))
            nc.vector.scalar_tensor_tensor(out=shift[:, :], in0=mv[:, :, 0], scalar=-1.0, in1=rstd[:, :],
                                           op0=ALU.mult, op1=ALU.mult).then_inc(shift_ready, 1)
            if w is None:
                ch.eng.wait_ge(scaled, NT)
                return
            for t in range(0, NT, 2):
                ch.eng.wait_ge(scaled, t + 1)
                ch.link(nc.vector.tensor_tensor(dest[:, t, :], dest[:, t, :], w[:, :], ALU.mult))
                ch.do(nc.vector.tensor_tensor(dest[:, t, :], dest[:, t, :], b[:, :], ALU.add))
                ch.eng.wait_ge(pooled, t // 2 + 1)
                ch.do(nc.vector.tensor_tensor(dest[:, t + 1, :], dest[:, t + 1, :], b[:, :], ALU.add))
            ch.wait()

        def norm_act(act, source, dest, temps):
            stats, mv, rstd, shift, var_ready, std_ready, shift_ready, scaled, pooled = temps
            act.wait_ge(var_ready, 1)
            nc.scalar.activation(rstd[:, :], rstd[:, :], ACT.Sqrt).then_inc(std_ready, 1)
            act.wait_ge(shift_ready, 1)
            for t in range(NT):
                nc.scalar.activation(dest[:, t, :], source[:, t, :], ACT.Identity, bias=shift[:, t:t + 1],
                                     scale=rstd[:, t:t + 1]).then_inc(scaled, 1)

        def norm_pool(pool, dest, temps, w):
            stats, mv, rstd, shift, var_ready, std_ready, shift_ready, scaled, pooled = temps
            for t in range(1, NT, 2):
                pool.wait_ge(scaled, t + 1)
                nc.gpsimd.tensor_tensor(dest[:, t, :], dest[:, t, :], w[:, :], ALU.mult).then_inc(pooled, 1)

        def norm_temps(ctx, name):
            return (sb(f"{name}_stats", [P, NT, 12], F32, ctx), sb(f"{name}_mv", [P, NT, 2], F32, ctx),
                    sb(f"{name}_rstd", [P, NT], F32, ctx), sb(f"{name}_shift", [P, NT], F32, ctx),
                    *(sem(f"{name}_{n}") for n in ("var_ready", "std_ready", "shift_ready", "scaled", "pooled")))

        def turn_pe(pe, source, bank, turned, taken):
            k = 0
            for c in range(KC):
                for t0, n in GROUPS:
                    if k >= len(bank):
                        pe.wait_ge(taken, k - len(bank) + 1)
                    for t in range(n):
                        ins = nc.tensor.transpose(bank[k % len(bank)][:, t * P:t * P + P],
                                                  source[:, t0 + t, c * 128:c * 128 + 128], ident[0:P, 0:P])
                    ins.then_inc(turned, 1)
                    k += 1

        def turn_act(act, dest, bank, turned, taken):
            k = 0
            for c in range(KC):
                for t0, n in GROUPS:
                    act.wait_ge(turned, k + 1)
                    nc.scalar.copy(dest[:, c, t0 * P:(t0 + n) * P], bank[k % len(bank)][:, 0:n * P]).then_inc(taken, 1)
                    k += 1

        TURNS = KC * len(GROUPS)

        with ExitStack() as ctx:
            rows_a = sb("rows_a", [128, 128], I32, ctx)
            rows_b = sb("rows_b", [32, 128], I32, ctx)
            drows_a = sb("drows_a", [128, 128], I32, ctx)
            drows_b = sb("drows_b", [32, 128], I32, ctx)
            fa = sb("fa", [128, 4, 128], F32, ctx)
            dst_f = sb("dst_f", [128, ETP], F32, ctx)
            first = sb("first", [128, ETP], F32, ctx)
            win_f = sb("win_f", [128, ETP], F32, ctx)
            junk = sb("junk", [128, ETP], F32, ctx)
            below = sb("below", [128, NT - 1], F32, ctx)
            cut = sb("cut", [128, NT - 1], F32, ctx)
            cut_i = sb("cut_i", [128, NT - 1], I32, ctx)
            cut_tf = sb("cut_tf", [128, NT - 1], F32, ctx)
            even = sb("even", [128, NT - 1], F32, ctx)
            dc_i = sb("dc_i", [128, CE], I32, ctx)
            pair = sb("pair", [128, 2], F32, ctx)
            pairs8 = sb("pairs8", [GH, 2 * CH], F32, ctx)
            temps = norm_temps(ctx, "ln0")
            turned_p = ps("turned_p", [128, 512], ctx)
            first_p = ps("first_p", [128, 512], ctx)
            cut_p = ps("cut_p", [128, 512], ctx)

            x_in, src_in, dst_in, dc_in = sem("x_in"), sem("src_in"), sem("dst_in"), sem("dc_in")
            padded, consts, iota_done = sem("padded"), sem("consts"), sem("iota_done")
            v0, src_turned, dst_turned = sem("v0"), sem("src_turned"), sem("dst_turned")
            floats, dst_f_ready, first_ready, below_ready, cut_ready = (
                sem("floats"), sem("dst_f_ready"), sem("first_ready"), sem("below_ready"), sem("cut_ready"))
            pair_ready, pair_out, pair_in = sem("pair_ready"), sem("pair_out"), sem("pair_in")
            full = ET - 1 - 128

            with nc.Block() as block:
                @block.sync
                def _(sp):
                    sp.wait_ge(padded, 2)
                    for name, ra, rb, s in (("src", rows_a, rows_b, src_in), ("dst", drows_a, drows_b, dst_in)):
                        v = a[name]
                        sp.dma_start(ra[:, :], v[0:128 * EP].rearrange("(t e) -> t e", e=EP)).then_inc(s, 16)
                        sp.dma_start(rb[0:full, :], v[128 * EP:(128 + full) * EP].rearrange("(t e) -> t e", e=EP)
                                     ).then_inc(s, 16)
                        sp.dma_start(rb[full:full + 1, 0:E - (ET - 1) * EP],
                                     v[(ET - 1) * EP:E].rearrange("(a e) -> a e", a=1)).then_inc(s, 16)
                    for g in range(GH):
                        sp.dma_start(dc_i[g * CH:(g + 1) * CH, :], a["dst"].rearrange("(c e) -> c e", e=CE)
                                     ).then_inc(dc_in, 16)
                    sp.wait_ge(pair_ready, 1)
                    sp.dma_start(pair_dram, pair[:, :]).then_inc(pair_out, 16)
                    sp.wait_ge(pair_out, 16)
                    sp.dma_start(pairs8[:, :], pair_dram.rearrange("(h c) k -> h (c k)", h=GH)).then_inc(pair_in, 16)

                @block.scalar
                def _(act):
                    act.dma_start(x[:, :, :], rows(a["x"])).then_inc(x_in, 16)
                    norm_act(act, x, h, temps)

                @block.gpsimd
                def _(pool):
                    nc.gpsimd.memset(rows_b[:, :], 0).then_inc(padded, 1)
                    nc.gpsimd.memset(drows_b[:, :], int(FAR)).then_inc(padded, 1)
                    nc.gpsimd.memset(ident[:, :], 0.0).then_inc(consts, 1)
                    nc.gpsimd.memset(ones[:, :], 1.0).then_inc(consts, 1)
                    pool.wait_ge(consts, 2)
                    nc.gpsimd.affine_select(out=ident[:, :], in_=ident[:, :], compare_op=ALU.not_equal, fill=1.0,
                                            base=0, pattern=[[-1, 128]], channel_multiplier=1).then_inc(consts, 1)
                    nc.gpsimd.iota(lanes[:, :], [[1, P]], base=0, channel_multiplier=0,
                                   allow_small_or_imprecise_dtypes=True).then_inc(iota_done, 1)
                    pool.wait_ge(iota_done, 1)

                @block.tensor
                def _(pe):
                    pe.wait_ge(consts, 3)
                    pe.wait_ge(floats, 2)
                    nc.tensor.transpose(turned_p[:, 0:128], fa[:, 0, :], ident[:, :]).then_inc(src_turned, 1)
                    nc.tensor.transpose(turned_p[:, 128:160], fa[0:32, 1, :], ident[0:32, 0:32]).then_inc(src_turned, 1)
                    pe.wait_ge(floats, 4)
                    nc.tensor.transpose(turned_p[:, 160:288], fa[:, 2, :], ident[:, :]).then_inc(dst_turned, 1)
                    nc.tensor.transpose(turned_p[:, 288:320], fa[0:32, 3, :], ident[0:32, 0:32]).then_inc(dst_turned, 1)
                    pe.wait_ge(dst_f_ready, 1)
                    nc.tensor.matmul(first_p[:, 0:ETP], ones[0:1, :], dst_f[0:1, :], start=True, stop=True
                                     ).then_inc(first_ready, 1)
                    pe.wait_ge(below_ready, NT - 1)
                    nc.tensor.matmul(cut_p[:, 0:NT - 1], ones[:, :], below[:, :], start=True, stop=True
                                     ).then_inc(cut_ready, 1)

                @block.vector
                def _(dve):
                    ch = Chain(dve, v0)
                    dve.wait_ge(src_in, 48)
                    nc.vector.tensor_copy(fa[:, 0, :], rows_a[:, :]).then_inc(floats, 1)
                    nc.vector.tensor_copy(fa[0:32, 1, :], rows_b[:, :]).then_inc(floats, 1)
                    dve.wait_ge(dst_in, 48)
                    nc.vector.tensor_copy(fa[:, 2, :], drows_a[:, :]).then_inc(floats, 1)
                    nc.vector.tensor_copy(fa[0:32, 3, :], drows_b[:, :]).then_inc(floats, 1)
                    ch.do(nc.vector.memset(src_item[:, ETP:], 0))
                    ch.do(nc.vector.memset(dst_rel[:, ETP:], FAR))
                    ch.do(nc.vector.memset(win[:, ETP:], 0))
                    ch.do(nc.vector.memset(win_f[:, :], 0.0))
                    dve.wait_ge(src_turned, 2)
                    dve.wait_ge(dst_turned, 2)
                    nc.vector.tensor_copy(dst_f[:, :], turned_p[:, ETP:2 * ETP]).then_inc(dst_f_ready, 1)
                    ch.do(nc.vector.tensor_copy(src_item[:, 0:ETP], turned_p[:, 0:ETP]))
                    dve.wait_ge(dst_f_ready, 1)
                    ch.do(nc.vector.tensor_scalar(dst_idx[:, :], dst_f[:, :], float(N - 1), None, ALU.min))
                    for k in range(1, NT):
                        nc.vector.tensor_scalar(junk[:, :], dst_f[:, :], float(P * k), 0.0, ALU.is_lt, ALU.add,
                                                accum_out=below[:, k - 1:k]).then_inc(below_ready, 1)
                        dve.wait_ge(below_ready, k)
                    dve.wait_ge(first_ready, 1)
                    ch.link(nc.vector.tensor_copy(first[:, :], first_p[:, 0:ETP]))
                    for k in range(1, NT):
                        ch.link(nc.vector.scalar_tensor_tensor(out=win_f[:, :], in0=first[:, :], scalar=float(P * k),
                                                               in1=win_f[:, :], op0=ALU.is_ge, op1=ALU.add))
                    ch.do(nc.vector.tensor_copy(win[:, 0:ETP], win_f[0:1, :]))
                    ch.do(nc.vector.scalar_tensor_tensor(out=dst_rel[:, 0:ETP], in0=win_f[:, :], scalar=-float(P),
                                                         in1=dst_f[:, :], op0=ALU.mult, op1=ALU.add))
                    dve.wait_ge(cut_ready, 1)
                    ch.do(nc.vector.tensor_copy(cut[:, :], cut_p[:, 0:NT - 1]))
                    ch.link(nc.vector.tensor_copy(cut_i[:, :], cut_p[:, 0:NT - 1]))
                    ch.link(nc.vector.tensor_scalar(cut_tile[:, :], cut_i[:, :], 7, None, ALU.arith_shift_right))
                    ch.link(nc.vector.tensor_copy(cut_tf[:, :], cut_tile[:, :]))
                    ch.link(nc.vector.scalar_tensor_tensor(out=even[:, :], in0=cut_tf[:, :], scalar=-float(EP),
                                                           in1=cut[:, :], op0=ALU.mult, op1=ALU.add))
                    ch.link(nc.vector.tensor_scalar(even[:, :], even[:, :], 0.0, FAR, ALU.is_equal, ALU.mult))
                    for k in range(1, NT):
                        t = nc.vector.value_load(cut_tile[0:1, k - 1:k], min_val=0, max_val=ETP - 1)
                        ch.do(nc.vector.tensor_copy(src_item[:, ETP + k - 1:ETP + k], src_item[:, bass.ds(t, 1)]))
                        ch.do(nc.vector.tensor_scalar(dst_rel[:, ETP + k - 1:ETP + k], dst_f[:, bass.ds(t, 1)],
                                                      -float(P * k), even[:, k - 1:k], ALU.add, ALU.add))
                        ch.do(nc.vector.memset(win[:, ETP + k - 1:ETP + k], k))
                    dve.wait_ge(dc_in, 16 * GH)
                    ch.do(nc.vector.tensor_copy(dstc[:, :], dc_i[:, :]))
                    ch.do(nc.vector.memset(change[:, :], -BIG))
                    ch.do(nc.vector.memset(change2[:, :], -BIG))
                    ch.wait()
                    ch.do(nc.vector.tensor_tensor(change[:, 1:CE], dstc[:, 1:CE], dstc[:, 0:CE - 1], ALU.not_equal))
                    ch.do(nc.vector.tensor_copy(pair[:, 0:1], dstc[:, 0:1]))
                    ch.do(nc.vector.tensor_copy(pair[:, 1:2], dstc[:, CE - 1:CE]))
                    ch.wait()
                    dve.sem_inc(pair_ready, 1)
                    ch.do(nc.vector.tensor_scalar(change[:, 1:CE], change[:, 1:CE], -BIG, None, ALU.mult))
                    dve.wait_ge(x_in, 16)
                    layer_norm(ch, x, h, temps)
                    dve.wait_ge(pair_in, 16)
                    ch.link(nc.vector.tensor_tensor(change2[:, 1:2 * CH], pairs8[:, 1:2 * CH], pairs8[:, 0:2 * CH - 1],
                                                    ALU.not_equal))
                    ch.link(nc.vector.tensor_scalar(change2[:, 1:2 * CH], change2[:, 1:2 * CH], -BIG, None, ALU.mult))
            end_stage()

        with nc.Fori(0, L) as l:

            with ExitStack() as ctx:
                hT_part = [sb(f"hT_{n}", [128, KC, N], F32R, ctx) for n in ("high", "low")]
                w = sb("w", [128, KC, D], F32, ctx)
                w_part = [sb(f"w_{n}", [128, KC, D], F32R, ctx) for n in ("high", "low")]
                bias = sb("gbias", [P, 2, D], F32, ctx)
                att = sb("att", [P, D], F32, ctx)
                rowx = [sb(f"rowx{k}_", [P, DX], F32, ctx) for k in range(2)]
                prod = sb("prod", [P, D], F32, ctx)
                bank = [ps(f"lin{k}_", [128, 512], ctx) for k in range(8)]
                (w_in, b_in, turned, h_high, h_split, w_high, w_split, w_used, lin_done, v1) = (
                    sem(n) for n in ("w_in", "b_in", "turned", "h_high", "h_split", "w_high", "w_split", "w_used",
                                     "lin_done", "v1_"))
                stored = [sem(f"stored{k}_") for k in range(2)]
                PER = 3
                PLACES = [(c, t0, n) for c in range(KC) for t0, n in GROUPS]

                with nc.Block() as block:
                    @block.sync
                    def _(sp):
                        sp.dma_start(w[:, :, :], a["L0_gnn_Wsrc"][bass.ds(l, 1)]
                                     .rearrange("a (c p) n -> p (a c) n", p=128)).then_inc(w_in, 16)
                        for k, name in enumerate(("bsrc", "bdst")):
                            sp.dma_start(bias[:, k, :], spread(a[f"L0_gnn_{name}"][bass.ds(l, 1)]
                                                               .rearrange("a d -> (a d)"), P)).then_inc(b_in, 16)
                        sp.dma_start(att[:, :], spread(a["L0_gnn_attn"][bass.ds(l, 1)]
                                                       .rearrange("a h d -> (a h d)"), P)).then_inc(b_in, 16)
                        sp.wait_ge(w_split, KC)
                        sp.dma_start(w[:, :, :], a["L0_gnn_Wdst"][bass.ds(l, 1)]
                                     .rearrange("a (c p) n -> p (a c) n", p=128)).then_inc(w_in, 16)
                        for m in range(2 * NT):
                            k, t = m // NT, m % NT
                            sp.wait_ge(v1, PER * (m + 1) + 1)
                            sp.dma_start((hs_dram, hd_dram)[k][t * P:t * P + P, :], rowx[m % 2][:, :]
                                         ).then_inc(stored[m % 2], 16)
                        for s in stored:
                            sp.wait_ge(s, 16 * NT)

                    @block.gpsimd
                    def _(pool):
                        for c in range(KC):
                            pool.wait_ge(w_high, c + 1)
                            nc.gpsimd.tensor_tensor(w_part[1][:, c, :], w[:, c, :], w_part[0][:, c, :].bitcast(F32),
                                                    ALU.subtract).then_inc(w_split, 1)

                    @block.tensor
                    def _(pe):
                        turn_pe(pe, h, bank, turned, h_split)
                        pe.wait_ge(h_split, len(PLACES))
                        for m in range(2 * NT):
                            k, t = m // NT, m % NT
                            if m >= 4:
                                pe.wait_ge(v1, PER * (m - 4) + 2)
                            for c in range(KC):
                                if t == 0:
                                    pe.wait_ge(w_split, KC * k + c + 1)
                                for q, (p_h, p_w) in enumerate(((0, 0), (0, 1), (1, 0))):
                                    for half in range(2):
                                        ins = nc.tensor.matmul(bank[2 * (m % 4) + half][0:P, 0:384],
                                                               hT_part[p_h][:, c, t * P:t * P + P],
                                                               w_part[p_w][:, c, 384 * half:384 * half + 384],
                                                               start=(c == 0 and q == 0), stop=(c == KC - 1 and q == 2))
                                if m == NT - 1 and c < KC - 1:
                                    ins.then_inc(w_used, 1)
                            ins.then_inc(lin_done, 1)

                    @block.scalar
                    def _(act):
                        for k, (c, t0, n) in enumerate(PLACES):
                            act.wait_ge(turned, k + 1)
                            nc.scalar.copy(hT_part[0][:, c, t0 * P:(t0 + n) * P], bank[k % len(bank)][:, 0:n * P]
                                           ).then_inc(h_high, 1)
                            if k >= len(PLACES) - KC:
                                act.wait_ge(w_in, 16)
                                c = k - (len(PLACES) - KC)
                                nc.scalar.copy(w_part[0][:, c, :], w[:, c, :]).then_inc(w_high, 1)
                        act.wait_ge(w_in, 32)
                        for c in range(KC):
                            if c < KC - 1:
                                act.wait_ge(w_used, c + 1)
                            else:
                                act.wait_ge(lin_done, NT)
                            nc.scalar.copy(w_part[0][:, c, :], w[:, c, :]).then_inc(w_high, 1)

                    @block.vector
                    def _(dve):
                        ch = Chain(dve, v1)
                        for k, (c, t0, n) in enumerate(PLACES):
                            dve.wait_ge(h_high, k + 1)
                            at = slice(t0 * P, (t0 + n) * P)
                            nc.vector.tensor_tensor(hT_part[1][:, c, at], bank[k % len(bank)][:, 0:n * P],
                                                    hT_part[0][:, c, at].bitcast(F32), ALU.subtract
                                                    ).then_inc(h_split, 1)
                        dve.wait_ge(b_in, 48)
                        ch.link(nc.vector.tensor_scalar(att[:, :], att[:, :], SLOPE, None, ALU.mult))
                        for m in range(2 * NT):
                            k, t = m // NT, m % NT
                            r = rowx[m % 2]
                            if m == NT:
                                for c in range(KC):
                                    dve.wait_ge(w_high, KC + c + 1)
                                    nc.vector.tensor_tensor(w_part[1][:, c, :], w[:, c, :],
                                                            w_part[0][:, c, :].bitcast(F32), ALU.subtract
                                                            ).then_inc(w_split, 1)
                            dve.wait_ge(lin_done, m + 1)
                            if m >= 2:
                                dve.wait_ge(stored[m % 2], 16 * (m // 2))
                            nc.vector.tensor_tensor(r[:, 0:384], bank[2 * (m % 4)][0:P, 0:384], bias[:, k, 0:384],
                                                    ALU.add)
                            ch.link(nc.vector.tensor_tensor(r[:, 384:D], bank[2 * (m % 4) + 1][0:P, 0:384],
                                                            bias[:, k, 384:D], ALU.add))
                            ch.link(nc.vector.tensor_tensor(prod[:, :], r[:, 0:D], att[:, :], ALU.mult))
                            ch.link(nc.vector.tensor_reduce(r[:, D:DX], prod[:, :].rearrange("p (h d) -> p h d", h=GH),
                                                            AX.X, ALU.add))
                end_stage()

            with ExitStack() as ctx:
                R = 8
                HALF = R // 2
                LAPS = ETP // R

                def tile_laps(eng, body):
                    body(0, R)
                    with eng.Fori(1, LAPS - 1) as i:
                        body(i, R)
                    body(LAPS - 1, ET - R * (LAPS - 1))
                gs = sb("gs", [128, R, DX], F32, ctx)
                gd = sb("gd", [128, R, DX], F32, ctx)
                cur = sb("cur", [128, 2, R], I32, ctx)
                rz = sb("rz", [128, 2, D], F32, ctx)
                acol = sb("acol", [128, KC], F32, ctx)
                arow = sb("arow", [KC, 128], F32, ctx)
                a8 = sb("a8", [128, KC, GH], F32, ctx)
                lg = sb("lg", [GH, 2, HALF * EP], F32, ctx)
                zt = [ps(f"zt{k}_", [128, 1024], ctx) for k in range(2)]
                lp = [ps(f"lp{k}_", [128, HALF * EP], ctx) for k in range(2)]
                ap_ = ps("ap_", [128, 512], ctx)
                a_in, a_turned, mask0, a8_ready, v2 = (sem("a_in"), sem("a_turned"), sem("mask0_"),
                                                       sem("a8_ready"), sem("v2_"))
                picked, handed = sem("picked"), sem("handed")
                got = [sem(f"got{k}_") for k in range(R)]
                z_ready, z_turned, relu_done, l_done, l_taken = (
                    sem("z_ready"), sem("z_turned"), sem("relu_done"), sem("l_done"), sem("l_taken"))
                l_out = [sem(f"l_out{half}_") for half in range(2)]

                with nc.Block() as block:
                    @block.sync
                    def _(sp):
                        sp.dma_start(arow[:, :], a["L0_gnn_attn"][bass.ds(l, 1)].rearrange("a h d -> (a h d)")
                                     .rearrange("(c p) -> c p", p=128)).then_inc(a_in, 16)

                        for half in range(2):
                            sp.sem_inc(l_out[half], 16)

                        def lap(i):
                            for half in range(2):
                                sp.wait_ge(l_taken, 2 * i + half + 1)
                                sp.dma_start(logit_dram[:, bass.ds(i * (R * EP) + half * (HALF * EP), HALF * EP)],
                                             lg[:, half, :]).then_inc(l_out[half], 16)
                        laps(sp, LAPS, lap)
                        for half in range(2):
                            sp.wait_ge(l_out[half], 16 * (LAPS + 1))

                    @block.gpsimd
                    def _(pool):
                        nc.gpsimd.memset(a8[:, :, :], 1.0 - SLOPE).then_inc(mask0, 1)
                        pool.wait_ge(mask0, 1)
                        nc.gpsimd.affine_select(out=a8[:, :, :], in_=a8[:, :, :], compare_op=ALU.is_ge, fill=0.0, base=0,
                                                pattern=[[128, KC], [-GD, GH]], channel_multiplier=1).then_inc(mask0, 1)
                        pool.wait_ge(mask0, 2)
                        nc.gpsimd.affine_select(out=a8[:, :, :], in_=a8[:, :, :], compare_op=ALU.is_ge, fill=0.0,
                                                base=GD - 1, pattern=[[-128, KC], [GD, GH]], channel_multiplier=-1
                                                ).then_inc(mask0, 1)

                        def lap(i, tiles):
                            for half in range(2):
                                t0 = R * i + half * HALF
                                if past(i, 1):
                                    pool.wait_ge(z_ready, t0 - R + HALF)
                                at = slice(half * HALF, half * HALF + HALF)
                                nc.gpsimd.tensor_copy(cur[:, 0, at], src_item[:, bass.ds(t0, HALF)]).then_inc(picked, 1)
                                nc.gpsimd.tensor_copy(cur[:, 1, at], dst_idx[:, bass.ds(t0, HALF)]).then_inc(picked, 1)
                                pool.wait_ge(picked, 4 * i + 2 * half + 2)
                                for j in range(half * HALF, min(half * HALF + HALF, tiles)):
                                    if past(i, 1):
                                        pool.wait_ge(l_done, R * i + j - R + 1)
                                    pool.sem_inc(handed, 1)
                                    for k, (g, table) in enumerate(((gs, hs_dram), (gd, hd_dram))):
                                        nc.gpsimd.indirect_dma_start(
                                            out=g[:, j, :], out_offset=None, in_=table,
                                            in_offset=bass.IndirectOffsetOnAxis(ap=cur[:, k, j:j + 1], axis=0)
                                        ).then_inc(got[j], 16)
                        tile_laps(pool, lap)

                    @block.vector
                    def _(dve):
                        dve.wait_ge(a_turned, 1)
                        nc.vector.tensor_copy(acol[:, :], ap_[:, 0:KC]).then_inc(v2, 1)
                        dve.wait_ge(v2, 1)
                        dve.wait_ge(mask0, 3)
                        nc.vector.tensor_tensor(a8[:, :, :], a8[:, :, :],
                                                acol[:, :].unsqueeze(2).to_broadcast([128, KC, GH]), ALU.mult
                                                ).then_inc(a8_ready, 1)

                        def take(i, half, tiles=R):
                            dve.wait_ge(l_done, R * i + min((half + 1) * HALF, tiles))
                            dve.wait_ge(l_out[half], 16 * (i + 1))
                            nc.vector.tensor_copy(lg[:, half, :], lp[half][0:GH, :]).then_inc(l_taken, 1)

                        def lap(i, tiles):
                            for j in range(tiles):
                                dve.wait_ge(got[j], 32 * (i + 1))
                                nc.vector.tensor_tensor(gs[:, j, :], gs[:, j, :], gd[:, j, :], ALU.add
                                                        ).then_inc(z_ready, 1)
                                if j == 2 and past(i, 1):
                                    take(i - 1, 1)
                                if j == min(2 + HALF, tiles - 1):
                                    take(i, 0)
                        tile_laps(dve, lap)
                        take(LAPS - 1, 1, ET - R * (LAPS - 1))

                    @block.tensor
                    def _(pe):
                        pe.wait_ge(a_in, 16)
                        nc.tensor.transpose(ap_[:, 0:KC], arow[:, :], ident[0:KC, 0:KC]).then_inc(a_turned, 1)
                        pe.wait_ge(a8_ready, 1)

                        def turn(t, j):
                            pe.wait_ge(z_ready, t + 1)
                            if past(t, 2):
                                pe.wait_ge(relu_done, t - 1)
                            for c in range(KC):
                                ins = nc.tensor.transpose(zt[j % 2][:, c * 128:c * 128 + 128],
                                                          gs[:, j, c * 128:c * 128 + 128], ident[:, :])
                            ins.then_inc(z_turned, 1)

                        def logits(t, i, j):
                            pe.wait_ge(relu_done, t + 1)
                            if j % HALF == 0 and past(i, 1):
                                pe.wait_ge(l_taken, 2 * i + j // HALF - 1)
                            at = lp[j // HALF][0:GH, j % HALF * EP:j % HALF * EP + EP]
                            for c in range(KC):
                                nc.tensor.matmul(at, a8[:, c, :], rz[:, j % 2, c * 128:c * 128 + 128],
                                                 start=(c == 0), stop=False)
                            nc.tensor.matmul(at, gs[:, j, D:DX], ident[:, :], start=False, stop=True
                                             ).then_inc(l_done, 1)

                        def lap(i, tiles):
                            for j in range(tiles):
                                turn(R * i + j, j)
                                if j:
                                    logits(R * i + j - 1, i, j - 1)
                            logits(R * i + tiles - 1, i, tiles - 1)
                        tile_laps(pe, lap)

                    @block.scalar
                    def _(act):
                        def lap(i, tiles):
                            for j in range(tiles):
                                t = R * i + j
                                act.wait_ge(z_turned, t + 1)
                                if past(t, 2):
                                    act.wait_ge(l_done, t - 1)
                                nc.scalar.activation(rz[:, j % 2, 0:512], zt[j % 2][:, 0:512], ACT.Relu)
                                nc.scalar.activation(rz[:, j % 2, 512:D], zt[j % 2][:, 512:D], ACT.Relu
                                                     ).then_inc(relu_done, 1)
                        tile_laps(act, lap)
                end_stage()

            with ExitStack() as ctx:
                lt = sb("lt", [128, CE], F32, ctx)
                fwd = sb("fwd", [128, CE], F32, ctx)
                bwd = sb("bwd", [128, CE], F32, ctx)
                pen = sb("pen", [128, CE], F32, ctx)
                ends = sb("ends", [128, 2], F32, ctx)
                ends8 = sb("ends8_", [GH, 2 * CH], F32, ctx)
                fwd8 = sb("fwd8_", [GH, 2 * CH], F32, ctx)
                bwd8 = sb("bwd8_", [GH, 2 * CH], F32, ctx)
                tops = sb("tops", [128, 2], F32, ctx)
                blank = sb("blank", [GH, ETP * EP - E], F32, ctx)
                lt_in, v3, ends_ready, ends_out, ends_in, tops_ready, tops_out, tops_in = (
                    sem(n) for n in ("lt_in", "v3_", "ends_ready", "ends_out", "ends_in", "tops_ready",
                                          "tops_out", "tops_in"))
                less_ready, ex_ready, ex_out, blank_ready = (
                    sem("less_ready"), sem("ex_ready"), sem("ex_out"), sem("blank_ready"))

                with nc.Block() as block:
                    @block.sync
                    def _(sp):
                        for g in range(GH):
                            sp.dma_start(lt[g * CH:g * CH + CH, :],
                                         logit_dram[g, 0:E].rearrange("(c e) -> c e", e=CE)).then_inc(lt_in, 16)
                        sp.wait_ge(ends_ready, 1)
                        sp.dma_start(pair_dram, ends[:, :]).then_inc(ends_out, 16)
                        sp.wait_ge(ends_out, 16)
                        sp.dma_start(ends8[:, :], pair_dram.rearrange("(h c) k -> h (c k)", h=GH)).then_inc(ends_in, 16)
                        sp.wait_ge(tops_ready, 1)
                        sp.dma_start(top_dram.rearrange("(h c) k -> h (c k)", h=GH), fwd8[:, :]).then_inc(tops_out, 16)
                        sp.wait_ge(tops_out, 16)
                        sp.dma_start(tops[:, :], top_dram).then_inc(tops_in, 16)
                        sp.wait_ge(blank_ready, 1)
                        sp.dma_start(ex_dram[:, E:], blank[:, :]).then_inc(ex_out, 16)
                        sp.wait_ge(ex_ready, 1)
                        for g in range(GH):
                            sp.dma_start(ex_dram[g, 0:E].rearrange("(c e) -> c e", e=CE),
                                         bwd[g * CH:g * CH + CH, :]).then_inc(ex_out, 16)
                        sp.wait_ge(ex_out, 16 * (GH + 1))

                    @block.scalar
                    def _(act):
                        act.wait_ge(less_ready, 1)
                        nc.scalar.activation(bwd[:, :], fwd[:, :], ACT.Exp).then_inc(ex_ready, 1)

                    @block.vector
                    def _(dve):
                        ch = Chain(dve, v3)
                        nc.vector.memset(blank[:, :], 0.0).then_inc(blank_ready, 1)
                        dve.wait_ge(lt_in, 16 * GH)
                        ch.do(nc.vector.tensor_tensor_scan(fwd[:, :], change[:, 0:CE], lt[:, :], -BIG, ALU.add, ALU.max))
                        ch.do(nc.vector.tensor_tensor_scan(bwd[:, ::-1], change[:, CE:0:-1], lt[:, ::-1], -BIG,
                                                           ALU.add, ALU.max))
                        ch.wait()
                        ch.link(nc.vector.tensor_tensor(fwd[:, :], fwd[:, :], bwd[:, :], ALU.max))
                        ch.do(nc.vector.tensor_copy(ends[:, 0:1], fwd[:, 0:1]))
                        ch.do(nc.vector.tensor_copy(ends[:, 1:2], fwd[:, CE - 1:CE]))
                        ch.wait()
                        dve.sem_inc(ends_ready, 1)
                        dve.wait_ge(ends_in, 16)
                        ch.do(nc.vector.tensor_tensor_scan(fwd8[:, :], change2[:, 0:2 * CH], ends8[:, :], -BIG,
                                                           ALU.add, ALU.max))
                        ch.do(nc.vector.tensor_tensor_scan(bwd8[:, ::-1], change2[:, 2 * CH:0:-1], ends8[:, ::-1], -BIG,
                                                           ALU.add, ALU.max))
                        ch.wait()
                        nc.vector.tensor_tensor(fwd8[:, :], fwd8[:, :], bwd8[:, :], ALU.max).then_inc(tops_ready, 1)
                        dve.wait_ge(tops_in, 16)
                        for k, e in enumerate((0, CE - 1)):
                            ch.link(nc.vector.tensor_scalar(pen[:, :], dstc[:, :], dstc[:, e:e + 1], -BIG,
                                                            ALU.not_equal, ALU.mult))
                            ch.link(nc.vector.scalar_tensor_tensor(out=fwd[:, :], in0=pen[:, :], scalar=tops[:, k:k + 1],
                                                                   in1=fwd[:, :], op0=ALU.add, op1=ALU.max))
                        ch.link(nc.vector.tensor_tensor(fwd[:, :], lt[:, :], fwd[:, :], ALU.subtract))
                        dve.sem_inc(less_ready, 1)
                end_stage()

            with ExitStack() as ctx:
                R = 6
                HALF = R // 2
                LAPS = ITEMS // R
                USED = ETP + NT - 1

                def item_laps(eng, body):
                    body(0, R)
                    with eng.Fori(1, LAPS - 1) as i:
                        body(i, R)
                    body(LAPS - 1, USED - R * (LAPS - 1))
                ACT_HEADS = 5
                DVE_HEADS = GH - ACT_HEADS
                Q = ETP // 4
                acc = sb("acc", [P, NT, DX], F32, ctx)
                gr = sb("gr", [128, R, DX], F32, ctx)
                cur = sb("curb", [128, R], I32, ctx)
                oh = sb("oh", [128, R, P], F32, ctx)
                exr = sb("exr", [GH, 2, Q * EP], F32, ctx)
                exT = sb("exT", [128, ITEMS, GH], F32, ctx)
                sinv = sb("sinv", [P, NT, GH], F32, ctx)
                neg = sb("neg", [P, 4, D], F32, ctx)
                lnw = sb("lnw", [P, D], F32, ctx)
                lnb = sb("lnb", [P, D], F32, ctx)
                temps = norm_temps(ctx, "lng")
                SUMS = 3
                sums = [ps(f"sums{k}_", [128, 2, 512], ctx) for k in range(SUMS)]
                turned_ex = [sums[0][:, 0, :], sums[0][:, 1, :], sums[1][:, 0, :], sums[1][:, 1, :]]
                ex_in = [sem(f"ex_in{k}_") for k in range(2)]
                ln_in, ex_turned, ex_taken, v4, v5 = (sem(n) for n in ("ln_in", "ex_turned", "ex_taken", "v4_",
                                                                            "v5_"))
                picked, handed = sem("picked2_"), sem("handed2_")
                got = [sem(f"got2{k}_") for k in range(R)]
                weighed, weighed_act, summed, added, neg_ready, mean_ready, elu_done, exp_done, exT_ready = (
                    sem(n) for n in ("weighed", "weighed_act", "summed", "added", "neg_ready", "mean_ready",
                                     "elu_done", "exp_done", "exT_ready"))

                with nc.Block() as block:
                    @block.sync
                    def _(sp):
                        for to, name in ((lnw, "ln_w"), (lnb, "ln_b")):
                            sp.dma_start(to[:, :], spread(a[f"L0_gnn_{name}"][bass.ds(l, 1)].rearrange("a d -> (a d)"), P)
                                         ).then_inc(ln_in, 16)
                        for q in range(4):
                            if q >= 2:
                                sp.wait_ge(ex_turned, q - 1)
                            sp.dma_start(exr[:, q % 2, :], ex_dram[:, q * Q * EP:(q + 1) * Q * EP]
                                         ).then_inc(ex_in[q % 2], 16)

                    @block.gpsimd
                    def _(pool):
                        def lap(i, items):
                            for half in range(2):
                                t0 = R * i + half * HALF
                                if past(i, 1):
                                    pool.wait_ge(weighed, t0 - R + HALF)
                                at = slice(half * HALF, half * HALF + HALF)
                                nc.gpsimd.tensor_copy(cur[:, at], src_item[:, bass.ds(t0, HALF)]).then_inc(picked, 1)
                                pool.wait_ge(picked, 2 * i + half + 1)
                                for j in range(half * HALF, min(half * HALF + HALF, items)):
                                    if past(i, 1):
                                        pool.wait_ge(summed, R * i + j - R + 1)
                                    pool.sem_inc(handed, 1)
                                    nc.gpsimd.indirect_dma_start(
                                        out=gr[:, j, :], out_offset=None, in_=hs_dram,
                                        in_offset=bass.IndirectOffsetOnAxis(ap=cur[:, j:j + 1], axis=0)
                                    ).then_inc(got[j], 16)
                        item_laps(pool, lap)
                        pool.wait_ge(ln_in, 32)
                        norm_pool(pool, h, temps, lnw)

                    @block.tensor
                    def _(pe):
                        for q in range(4):
                            pe.wait_ge(ex_in[q % 2], 16 * (q // 2 + 1))
                            for t in range(Q):
                                ins = nc.tensor.transpose(turned_ex[q][:, t * GH:t * GH + GH],
                                                          exr[:, q % 2, t * EP:t * EP + EP], ident[0:GH, 0:GH])
                            ins.then_inc(ex_turned, 1)
                        pe.wait_ge(ex_taken, 4)

                        def lap(i, items):
                            for j in range(items):
                                t = R * i + j
                                pe.wait_ge(weighed, t + 1)
                                pe.wait_ge(weighed_act, t + 1)
                                if past(t, SUMS):
                                    pe.wait_ge(added, t - SUMS + 1)
                                for k in range(2):
                                    ins = nc.tensor.matmul(sums[j % SUMS][0:P, k, 0:DX // 2], oh[:, j, :],
                                                           gr[:, j, k * (DX // 2):(k + 1) * (DX // 2)],
                                                           start=True, stop=True)
                                ins.then_inc(summed, 1)
                        item_laps(pe, lap)

                    @block.scalar
                    def _(act):
                        act.wait_ge(exT_ready, 1)

                        def lap(i, items):
                            for j in range(items):
                                t = R * i + j
                                act.wait_ge(got[j], 16 * (i + 1))
                                for g in range(DVE_HEADS, GH):
                                    part = gr[:, j, g * GD:(g + 1) * GD]
                                    nc.scalar.activation(part, part, ACT.Copy,
                                                         scale=exT[:, bass.ds(t, 1), g:g + 1]
                                                         .rearrange("p a h -> p (a h)"))
                                nc.scalar.copy(gr[:, j, D:DX], exT[:, bass.ds(t, 1), :].rearrange("p a h -> p (a h)")
                                               ).then_inc(weighed_act, 1)
                        item_laps(act, lap)
                        for t in range(NT):
                            act.wait_ge(mean_ready, t + 1)
                            if t >= 4:
                                act.wait_ge(elu_done, t - 3)
                            nc.scalar.activation(neg[:, t % 4, :], acc[:, t, 0:D], ACT.Exp).then_inc(exp_done, 1)
                            act.wait_ge(exp_done, t + 1)
                            nc.scalar.activation(neg[:, t % 4, :], neg[:, t % 4, :], ACT.Copy, bias=-1.0
                                                 ).then_inc(neg_ready, 1)
                        norm_act(act, h, h, temps)

                    @block.vector
                    def _(dve):
                        ch = Chain(dve, v4)
                        ch.do(nc.vector.memset(acc[:, :, :], 0.0))
                        ch.do(nc.vector.memset(exT[:, ETP + NT - 1:, :], 0.0))
                        for q in range(4):
                            dve.wait_ge(ex_turned, q + 1)
                            nc.vector.tensor_copy(exT[:, q * Q:(q + 1) * Q, :],
                                                  turned_ex[q][:, 0:Q * GH].rearrange("p (t h) -> p t h", h=GH)
                                                  ).then_inc(ex_taken, 1)
                        dve.wait_ge(ex_taken, 4)
                        for k in range(NT - 1):
                            t = nc.vector.value_load(cut_tile[0:1, k:k + 1], min_val=0, max_val=ETP - 1)
                            ch.do(nc.vector.tensor_copy(exT[:, ETP + k:ETP + k + 1, :], exT[:, bass.ds(t, 1), :]))
                        ch.wait()
                        dve.sem_inc(exT_ready, 1)

                        def weigh(t, i, j):
                            e = exT[:, bass.ds(t, 1), 0:DVE_HEADS]
                            dve.wait_ge(got[j], 16 * (i + 1))
                            g3 = gr[:, j, 0:DVE_HEADS * GD].rearrange("p (h d) -> p h d", h=DVE_HEADS)
                            nc.vector.tensor_tensor(
                                g3, g3, e.rearrange("p a h -> p h a").to_broadcast([128, DVE_HEADS, GD]), ALU.mult)
                            nc.vector.tensor_scalar(oh[:, j, :], lanes[:, :], dst_rel[:, bass.ds(t, 1)], None,
                                                    ALU.is_equal).then_inc(weighed, 1)

                        def add(t, j):
                            w = nc.vector.value_load(win[0:1, bass.ds(t, 1)], min_val=0, max_val=NT - 1)
                            dve.wait_ge(summed, t + 1)
                            if past(t, 1):
                                dve.wait_ge(added, t)
                            to = acc[:, bass.ds(w, 1), :].rearrange("p a (k n) -> p (a k) n", k=2)
                            nc.vector.tensor_tensor(to, to, sums[j % SUMS][0:P, :, 0:DX // 2], ALU.add).then_inc(added, 1)

                        def lap(i, items):
                            for j in range(items):
                                t = R * i + j
                                weigh(t, i, j)
                                if past(t, 2):
                                    add(t - 2, (j - 2) % R)
                        item_laps(dve, lap)
                        for t in (USED - 2, USED - 1):
                            add(t, t % R)
                        dve.wait_ge(added, USED)

                        ch = Chain(dve, v5)
                        ch.link(nc.vector.tensor_scalar(sinv[:, :, :], acc[:, :, D:DX], 1e-30, None, ALU.max))
                        ch.link(nc.vector.reciprocal(sinv[:, :, :], sinv[:, :, :]))
                        for t in range(NT):
                            o3 = acc[:, t, 0:D].rearrange("p (h d) -> p h d", h=GH)
                            nc.vector.tensor_tensor(o3, o3, sinv[:, t, :].unsqueeze(2).to_broadcast([P, GH, GD]),
                                                    ALU.mult).then_inc(mean_ready, 1)
                            if t:
                                dve.wait_ge(mean_ready, t)
                                ch.do(nc.vector.scalar_tensor_tensor(out=h[:, t - 1, :], in0=acc[:, t - 1, 0:D],
                                                                     scalar=0.0, in1=h[:, t - 1, :], op0=ALU.max,
                                                                     op1=ALU.add))
                        dve.wait_ge(mean_ready, NT)
                        ch.link(nc.vector.scalar_tensor_tensor(out=h[:, NT - 1, :], in0=acc[:, NT - 1, 0:D], scalar=0.0,
                                                               in1=h[:, NT - 1, :], op0=ALU.max, op1=ALU.add))
                        for t in range(NT):
                            dve.wait_ge(neg_ready, t + 1)
                            nc.vector.scalar_tensor_tensor(out=h[:, t, :], in0=neg[:, t % 4, :], scalar=0.0,
                                                           in1=h[:, t, :], op0=ALU.min, op1=ALU.add
                                                           ).then_inc(elu_done, 1)
                        dve.wait_ge(elu_done, NT)
                        dve.wait_ge(ln_in, 32)
                        layer_norm(ch, h, h, temps, w=lnw, b=lnb)
                end_stage()

        edge.close()

        with ExitStack() as ctx:
            onw = sb("onw", [P, D], F32, ctx)
            onb = sb("onb", [P, D], F32, ctx)
            temps = norm_temps(ctx, "lno")
            temps2 = norm_temps(ctx, "lny")
            on_in, v6 = sem("on_in"), sem("v6")
            with nc.Block() as block:
                @block.sync
                def _(sp):
                    sp.dma_start(onw[:, :], spread(a["L0_gnn_on_w"], P)).then_inc(on_in, 16)
                    sp.dma_start(onb[:, :], spread(a["L0_gnn_on_b"], P)).then_inc(on_in, 16)

                @block.gpsimd
                def _(pool):
                    pool.wait_ge(on_in, 32)
                    norm_pool(pool, h, temps, onw)

                @block.scalar
                def _(act):
                    norm_act(act, h, h, temps)
                    norm_act(act, x, h, temps2)

                @block.vector
                def _(dve):
                    ch = Chain(dve, v6)
                    dve.wait_ge(on_in, 32)
                    layer_norm(ch, h, h, temps, w=onw, b=onb)
                    ch.link(nc.vector.tensor_tensor(x[:, :, :], x[:, :, :], h[:, :, :], ALU.add))
                    layer_norm(ch, x, h, temps2)
            end_stage()

        o_full = sb("o", [128, NT, D], F32, mid)
        o = o_full[0:P, :, :]
        oT = (o_full[:, :, :].rearrange("p t d -> p (t d)")[:, 0:KC * N].rearrange("p (c n) -> p c n", c=KC))
        with ExitStack() as ctx:
            w1 = sb("ln1w", [P, D], F32, ctx)
            b1 = sb("ln1b", [P, D], F32, ctx)
            temps = norm_temps(ctx, "ln1")
            tT = sb("tT", [128, KC, N], F32, ctx)
            wp = [sb(f"wp{k}_", [128, KC, 3, 128], F32, ctx) for k in range(2)]
            brow = sb("brow", [3 * KC, 128], F32, ctx)
            bcol = sb("bcol", [128, 3 * KC], F32, ctx)
            bv = sb("bv", [P, D], F32, ctx)
            qT = sb("qT", [128, N], F32, ctx)
            kT = sb("kT", [128, N], F32, ctx)
            v = sb("v", [P, NT, 128], F32, ctx)
            prob = sb("prob", [P, 2, N], F32, ctx)
            pT = sb("pT", [P, 2, 3, 4 * P], F32, ctx)
            bank_high = sb("bank_high", [P, 4, 3], F32, ctx)
            high = sb("high", [P, 4], F32, ctx)
            low = sb("low", [P, 4], F32, ctx)
            zero = sb("zero", [120, D], F32, ctx)
            part = sb("part", [P, 2, 3], F32, ctx)
            total = sb("total", [P, 2], F32, ctx)
            tinv = sb("tinv", [P, 2], F32, ctx)
            ident_h = sb("ident_h", [P, P], BF16, ctx)
            causal = sb("causal", [P, P], BF16, ctx)
            S = [ps(f"S{k}_", [128, 3, 512], ctx) for k in range(2)]
            O = [ps(f"O{k}_", [128, 512], ctx) for k in range(2)]
            banks = [S[k][:, b, :] for k in range(2) for b in range(3)]
            (ln1_in, v7, normed, turned, taken, brow_in, b_turned, b_taken, bv_in, masks, qk_done, v_done,
             qk_taken, v_taken, s_done, low_ready, exp_done, p_ready, p_turned, pt_act, pt_dve, o_done, o_taken, v8) = (
                sem(n) for n in ("ln1_in", "v7", "t_normed", "t_turned", "t_taken", "brow_in", "b_turned",
                                 "b_taken", "bv_in", "masks", "qk_done", "v_done", "qk_taken",
                                 "v_taken", "s_done", "low_ready", "exps_in", "p_ready", "p_turned", "pt_act", "pt_dve",
                                 "o_done", "o_taken", "v8"))
            w_in = [sem(f"wp_in{k}") for k in range(2)]
            zero_ready, zeroed, x_done = sem("zero_ready"), sem("zeroed"), sem("x_done")

            def pair_laps(eng, body):
                def two(i):
                    for k in range(2):
                        body(2 * i + k, k, i)
                laps(eng, PAIRS // 2, two)

            IT = 2 * NT
            ORDER = [0, 9, 1, 7, 2, 8, 3, 6, 4, 5]
            BANKS = len(banks)
            CHUNKS = [(0, 500), (500, 500), (1000, 250)]
            qkv_w = a["L0_ffn_attn_qkv_w"].rearrange("(c p) (k n) -> p c k n", p=128, k=3)

            def groups(n):
                qi = ORDER[n % NT]
                return [(b, min(4, qi + 1 - 4 * b)) for b in range((qi + 4) // 4)]

            V_BANKS = [banks[1], banks[2], O[0]]
            home = [BANKS // 2 + sum(len(groups(m)) for m in range(n)) for n in range(IT)]
            owner = [n for n in range(IT) for _ in groups(n)]
            assert len(owner) % BANKS == 0

            def bank_of(n, b):
                return banks[(home[n] + b) % BANKS]

            def held_by(n):
                g = home[n] - home[0] + len(groups(n)) - 1 - BANKS
                return owner[g] if g >= 0 else -1

            assert all(held_by(n) <= max(n - 3, -1) for n in range(IT))

            AHEAD = 3
            early, made_items = [], 0
            for n in range(-1, IT):
                early.append([])
                while made_items < min(IT, n + AHEAD + 1) and held_by(made_items) < max(n, 0):
                    early[-1].append(made_items)
                    made_items += 1

            many = [sum(len(groups(m)) > 1 for m in range(n + 1)) for n in range(IT)]
            MANY = many[-1]

            SMALL = sum(len(groups(n)) + 3 for n in range(IT))

            with nc.Block() as block:
                @block.sync
                def _(sp):
                    sp.dma_start(w1[:, :], spread(a["L0_ffn_ln1_w"], P)).then_inc(ln1_in, 16)
                    sp.dma_start(b1[:, :], spread(a["L0_ffn_ln1_b"], P)).then_inc(ln1_in, 16)
                    sp.dma_start(brow[:, :], a["L0_ffn_attn_qkv_b"].rearrange("(c p) -> c p", p=128)
                                 ).then_inc(brow_in, 16)
                    sp.dma_start(bv[:, :], spread(a["L0_ffn_attn_qkv_b"][2 * D:3 * D], P)).then_inc(bv_in, 16)

                    def lap(i, w, lap_i):
                        if past(i, 2):
                            sp.wait_ge(v_done, 3 * i - 3)
                        for k in range(3):
                            sp.dma_start(wp[w][:, :, k, :], qkv_w[:, :, k, bass.ds(i * 128, 128)]
                                         ).then_inc(w_in[w], 16)
                    pair_laps(sp, lap)
                    sp.wait_ge(zero_ready, 1)
                    sp.dma_start(slot_in[0:SLOTS, :].rearrange("(p r) d -> p r d", p=120),
                                 zero[:, :].unsqueeze(1).to_broadcast([120, SLOTS // 120, D])).then_inc(zeroed, 16)
                    sp.wait_ge(zeroed, 16)

                @block.gpsimd
                def _(pool):
                    nc.gpsimd.memset(zero[:, :], 0.0).then_inc(zero_ready, 1)
                    nc.gpsimd.memset(ident_h[:, :], 0.0).then_inc(masks, 1)
                    nc.gpsimd.memset(causal[:, :], 0.0).then_inc(masks, 1)
                    pool.wait_ge(masks, 2)
                    nc.gpsimd.affine_select(out=ident_h[:, :], in_=ident_h[:, :], compare_op=ALU.not_equal, fill=1.0,
                                            base=0, pattern=[[-1, P]], channel_multiplier=1).then_inc(masks, 1)
                    nc.gpsimd.affine_select(out=causal[:, :], in_=causal[:, :], compare_op=ALU.is_ge, fill=-BIG,
                                            base=0, pattern=[[-1, P]], channel_multiplier=1).then_inc(masks, 1)
                    pool.wait_ge(ln1_in, 32)
                    norm_pool(pool, o, temps, w1)
                    for t in range(NT):
                        nc.gpsimd.tensor_tensor(x[:, t, :], x[:, t, :], h[:, t, :], ALU.add).then_inc(x_done, 1)
                    pool.wait_ge(x_done, NT)

                @block.tensor
                def _(pe):
                    pe.wait_ge(normed, 1)
                    turn_pe(pe, o, banks, turned, taken)
                    pe.wait_ge(taken, TURNS)
                    pe.wait_ge(brow_in, 16)
                    nc.tensor.transpose(O[0][:, 0:3 * KC], brow[:, :], ident[0:3 * KC, 0:3 * KC]).then_inc(b_turned, 1)
                    pe.wait_ge(masks, 4)
                    pe.wait_ge(b_taken, 1)

                    def scores(n):
                        r, qi = 64 * (n // NT), ORDER[n % NT]
                        for b, m in groups(n):
                            nc.tensor.matmul(bank_of(n, b)[0:P, 0:m * P], qT[r:r + 64, qi * P:qi * P + P],
                                             kT[r:r + 64, 4 * b * P:(4 * b + m) * P], start=True,
                                             stop=(b != qi // 4))
                        nc.tensor.matmul(bank_of(n, qi // 4)[0:P, (qi % 4) * P:(qi % 4) * P + P], ident_h[:, :],
                                         causal[:, :], start=False, stop=True).then_inc(s_done, 1)

                    def lap(i, w, lap_i):
                        pe.wait_ge(w_in[w], 48 * (lap_i + 1))
                        for k in range(2):
                            for b, (s, m) in enumerate(CHUNKS):
                                for c in range(KC):
                                    ins = nc.tensor.matmul(S[k][:, b, 0:m], wp[w][:, c, k, :], tT[:, c, s:s + m],
                                                           start=(c == 0), stop=(c == KC - 1))
                            ins.then_inc(qk_done, 1)
                        pe.wait_ge(qk_taken, 6 * i + 6)
                        scores(0)
                        scores(1)
                        if past(i, 1):
                            pe.wait_ge(o_taken, IT * i)
                        for b, (t0, m) in enumerate(GROUPS):
                            for t in range(m):
                                for c in range(KC):
                                    ins = nc.tensor.matmul(V_BANKS[b][0:P, t * 128:t * 128 + 128],
                                                           tT[:, c, (t0 + t) * P:(t0 + t) * P + P], wp[w][:, c, 2, :],
                                                           start=(c == 0), stop=(c == KC - 1))
                            ins.then_inc(v_done, 1)
                        pe.wait_ge(v_taken, 3 * i + 3)

                        def read_out(m):
                            pe.wait_ge(pt_act, IT * i + m + 1)
                            if many[m] or past(i, 1):
                                pe.wait_ge(pt_dve, MANY * i + many[m])

                        for n in range(-1, IT + 1):
                            if 0 <= n < IT:
                                pe.wait_ge(p_ready, IT * i + n + 1)
                                for b, m in groups(n):
                                    for t in range(m):
                                        ins = nc.tensor.transpose(
                                            bank_of(n, b)[0:P, t * P:t * P + P],
                                            prob[:, n % 2, (4 * b + t) * P:(4 * b + t + 1) * P], ident[0:P, 0:P])
                                ins.then_inc(p_turned, 1)
                            for m in early[n + 1] if n < IT else ():
                                if held_by(m) >= 0:
                                    read_out(held_by(m))
                                if m >= 2:
                                    scores(m)
                            if n >= 1:
                                m = n - 1
                                hh, qi = m // NT, ORDER[m % NT]
                                read_out(m)
                                if m >= 2 or past(i, 1):
                                    pe.wait_ge(o_taken, IT * i + m - 1)
                                for t in range(qi + 1):
                                    ins = nc.tensor.matmul(O[m % 2][0:HD, 0:P], v[:, t, HD * hh:HD * hh + HD],
                                                           pT[:, m % 2, t // 4, (t % 4) * P:(t % 4) * P + P],
                                                           start=(t == 0), stop=(t == qi))
                                ins.then_inc(o_done, 1)
                    pair_laps(pe, lap)

                @block.scalar
                def _(act):
                    norm_act(act, h, o, temps)
                    turn_act(act, tT, banks, turned, taken)
                    act.wait_ge(b_taken, 1)

                    def lap(i, *_):
                        for k, to in enumerate((qT, kT)):
                            act.wait_ge(qk_done, 2 * i + k + 1)
                            for b, (s, m) in enumerate(CHUNKS):
                                nc.scalar.activation(to[:, s:s + m], S[k][:, b, 0:m], ACT.Identity,
                                                     bias=bcol[:, bass.ds(i + k * KC, 1)]).then_inc(qk_taken, 1)
                        for n in range(IT + 3):
                            if 2 <= n < IT + 2:
                                m = n - 2
                                act.wait_ge(p_turned, IT * i + m + 1)
                                if m >= 2 or past(i, 1):
                                    act.wait_ge(o_done, IT * i + m - 1)
                                k = groups(m)[0][1] * P
                                nc.scalar.copy(pT[:, m % 2, 0, 0:k], bank_of(m, 0)[0:P, 0:k]).then_inc(pt_act, 1)
                            if n < IT:
                                act.wait_ge(low_ready, IT * i + n + 1)
                                if n >= 2 or past(i, 1):
                                    act.wait_ge(p_turned, IT * i + n - 1)
                                for b, m in groups(n):
                                    ins = nc.scalar.activation(prob[:, n % 2, 4 * b * P:(4 * b + m) * P],
                                                               bank_of(n, b)[0:P, 0:m * P], ACT.Exp,
                                                               bias=low[:, n % 4:n % 4 + 1], scale=HD ** -0.5,
                                                               accum_out=part[:, n % 2, b:b + 1])
                                ins.then_inc(exp_done, 1)
                            if n >= 3:
                                m = n - 3
                                r, q = HD * (m // NT), ORDER[m % NT] * P
                                act.wait_ge(o_done, IT * i + m + 1)
                                nc.scalar.copy(oT[r:r + HD, bass.ds(i, 1), q:q + P].rearrange("p a n -> p (a n)"),
                                               O[m % 2][0:HD, 0:P]).then_inc(o_taken, 1)
                    pair_laps(act, lap)

                @block.vector
                def _(dve):
                    ch = Chain(dve, v7)
                    dve.wait_ge(ln1_in, 32)
                    layer_norm(ch, h, o, temps, w=w1, b=b1)
                    dve.sem_inc(normed, 1)
                    dve.wait_ge(b_turned, 1)
                    nc.vector.tensor_copy(bcol[:, :], O[0][:, 0:3 * KC]).then_inc(b_taken, 1)
                    dve.wait_ge(bv_in, 16)

                    def lap(i, *_):
                        small = Chain(dve, v8, base=SMALL * i)

                        def highest(n):
                            k = n % 4
                            dve.wait_ge(s_done, IT * i + n + 1)
                            for b, m in groups(n):
                                small.do(nc.vector.tensor_reduce(bank_high[:, k, b:b + 1],
                                                                 bank_of(n, b)[0:P, 0:m * P], AX.X, ALU.max))
                            small.wait()
                            small.link(nc.vector.tensor_reduce(high[:, k:k + 1], bank_high[:, k, 0:len(groups(n))],
                                                               AX.X, ALU.max))
                            nc.vector.tensor_scalar(low[:, k:k + 1], high[:, k:k + 1], -HD ** -0.5, None,
                                                    ALU.mult).then_inc(low_ready, 1)

                        for n in range(IT + 2):
                            if 1 <= n <= IT:
                                m, k = n - 1, (n - 1) % 2
                                dve.wait_ge(exp_done, IT * i + m + 1)
                                small.link(nc.vector.tensor_reduce(total[:, k:k + 1], part[:, k, 0:len(groups(m))],
                                                                   AX.X, ALU.add))
                                small.link(nc.vector.reciprocal(tinv[:, k:k + 1], total[:, k:k + 1]))
                                keys = prob[:, k, 0:(ORDER[m % NT] + 1) * P]
                                nc.vector.tensor_scalar(keys, keys, tinv[:, k:k + 1], None, ALU.mult
                                                        ).then_inc(p_ready, 1)
                            if n >= 2:
                                m, k = n - 2, n % 2
                                dve.wait_ge(p_turned, IT * i + m + 1)
                                if m >= 2 or past(i, 1):
                                    dve.wait_ge(o_done, IT * i + m - 1)
                                for b, c in groups(m)[1:]:
                                    ins = nc.vector.tensor_copy(pT[:, k, b, 0:c * P], bank_of(m, b)[0:P, 0:c * P])
                                if len(groups(m)) > 1:
                                    ins.then_inc(pt_dve, 1)
                            if n < IT:
                                highest(n)
                            if n == 1:
                                for b, (t0, m) in enumerate(GROUPS):
                                    dve.wait_ge(v_done, 3 * i + b + 1)
                                    nc.vector.tensor_tensor(
                                        v[:, t0:t0 + m, :],
                                        V_BANKS[b][0:P, 0:m * 128].rearrange("p (t n) -> p t n", n=128),
                                        bv[:, bass.ds(i * 128, 128)].unsqueeze(1).to_broadcast([P, m, 128]), ALU.add
                                    ).then_inc(v_taken, 1)
                        assert small.n == SMALL
                    pair_laps(dve, lap)
            end_stage()

        with ExitStack() as ctx:
            wo = sb("wo", [128, KC, D], F32, ctx)
            bo = sb("bo", [P, D], F32, ctx)
            w2 = sb("ln2w", [P, D], F32, ctx)
            b2 = sb("ln2b", [P, D], F32, ctx)
            row = sb("row", [P, D], F32, ctx)
            temps = norm_temps(ctx, "ln2")
            bank = [ps(f"pr{k}_", [128, 512], ctx) for k in range(8)]
            wo_in, b_in, done, v9 = (sem(n) for n in ("wo_in", "bo_in", "proj_done", "v9"))
            with nc.Block() as block:
                @block.sync
                def _(sp):
                    sp.dma_start(wo[:, :, :], a["L0_ffn_attn_proj_w"].rearrange("(c p) n -> p c n", p=128)
                                 ).then_inc(wo_in, 16)
                    sp.dma_start(bo[:, :], spread(a["L0_ffn_attn_proj_b"], P)).then_inc(b_in, 16)
                    sp.dma_start(w2[:, :], spread(a["L0_ffn_ln2_w"], P)).then_inc(b_in, 16)
                    sp.dma_start(b2[:, :], spread(a["L0_ffn_ln2_b"], P)).then_inc(b_in, 16)

                @block.tensor
                def _(pe):
                    pe.wait_ge(wo_in, 16)
                    for t in range(NT):
                        if t >= 4:
                            pe.wait_ge(v9, 3 * (t - 4) + 1)
                        for k in range(2):
                            for c in range(KC):
                                ins = nc.tensor.matmul(bank[2 * (t % 4) + k][0:P, 0:384], oT[:, c, t * P:t * P + P],
                                                       wo[:, c, 384 * k:384 * k + 384], start=(c == 0),
                                                       stop=(c == KC - 1))
                        ins.then_inc(done, 1)

                @block.gpsimd
                def _(pool):
                    pool.wait_ge(b_in, 48)
                    norm_pool(pool, o, temps, w2)

                @block.scalar
                def _(act):
                    norm_act(act, h, o, temps)

                @block.vector
                def _(dve):
                    ch = Chain(dve, v9)
                    dve.wait_ge(b_in, 48)
                    for t in range(NT):
                        dve.wait_ge(done, t + 1)
                        nc.vector.tensor_tensor(row[:, 0:384], bank[2 * (t % 4)][0:P, 0:384], bo[:, 0:384], ALU.add)
                        ch.link(nc.vector.tensor_tensor(row[:, 384:D], bank[2 * (t % 4) + 1][0:P, 0:384],
                                                        bo[:, 384:D], ALU.add))
                        ch.do(nc.vector.tensor_tensor(h[:, t, :], h[:, t, :], row[:, :], ALU.add))
                        ch.do(nc.vector.tensor_tensor(x[:, t, :], x[:, t, :], row[:, :], ALU.add))
                        ch.wait()
                    layer_norm(ch, h, o, temps, w=w2, b=b2)
            end_stage()

        with ExitStack() as ctx:
            uT = sb("uT", [128, KC, N], F32, ctx)
            wg = sb("wg", [128, KC, NX], F32, ctx)
            tri = sb("tri", [P, P], F32, ctx)
            expert = sb("expert", [P, NX], F32, ctx)
            spare = sb("spare", [P, 2 * NT], F32, ctx)
            lgt = sb("lgt", [P, NT, NX], F32, ctx)
            best = sb("best", [P, NT, NX], F32, ctx)
            which = sb("which", [P, NT, NX], U32, ctx)
            which_f = sb("which_f", [P, 2, NT], F32, ctx)
            gap = sb("gap", [P, NT], F32, ctx)
            prob0 = sb("prob0", [P, 2, NT], F32, ctx)
            hot = sb("hot", [P, 2, NT, NX], F32, ctx)
            base = sb("base", [P, 2 * NT, NX], F32, ctx)
            tot = sb("tot", [P, 2 * NT, NX], F32, ctx)
            rank = sb("rank", [P, 2 * NT], F32, ctx)
            keep = sb("keep", [P, 2 * NT], F32, ctx)
            slot = sb("slot", [P, 2 * NT], F32, ctx)
            slot_write = sb("slot_write", [P, 2 * NT], I32, ctx)
            bank = [ps(f"ro{k}_", [128, 512], ctx) for k in range(4)]
            lg_p = ps("lg_p", [128, 512], ctx)
            cum_p = ps("cum_p", [128, 512], ctx)
            tot_p = ps("tot_p", [128, 512], ctx)
            turned, taken, wg_in, made, lg_done, gap_ready, exp_done, hot_ready, counted, v10, slots_ready, sent = (
                sem(n) for n in ("u_turned", "uT_taken", "wg_in", "made", "lg_done", "gap_ready", "gap_exp",
                                 "hot_ready", "counted", "v10", "slots_ready", "sent"))
            with nc.Block() as block:
                @block.sync
                def _(sp):
                    sp.dma_start(wg[:, :, :], a["L0_ffn_w_g"].rearrange("(c p) e -> p c e", p=128)).then_inc(wg_in, 16)

                @block.gpsimd
                def _(pool):
                    nc.gpsimd.memset(tri[:, :], 1.0).then_inc(made, 1)
                    nc.gpsimd.iota(expert[:, :], [[1, NX]], base=0, channel_multiplier=0,
                                   allow_small_or_imprecise_dtypes=True).then_inc(made, 1)
                    nc.gpsimd.iota(spare[:, :], [[P, 2 * NT]], base=SLOTS, channel_multiplier=1,
                                   allow_small_or_imprecise_dtypes=True).then_inc(made, 1)
                    pool.wait_ge(made, 3)
                    nc.gpsimd.affine_select(out=tri[:, :], in_=tri[:, :], compare_op=ALU.is_ge, fill=0.0, base=0,
                                            pattern=[[1, P]], channel_multiplier=-1).then_inc(made, 1)
                    pool.wait_ge(slots_ready, 1)
                    for k in range(2):
                        for t in range(NT):
                            b = k * NT + t
                            nc.gpsimd.indirect_dma_start(
                                out=slot_in, in_=o[:, t, :], in_offset=None,
                                out_offset=bass.IndirectOffsetOnAxis(ap=slot_write[:, b:b + 1], axis=0)
                            ).then_inc(sent, 16)
                    pool.wait_ge(sent, 32 * NT)

                @block.tensor
                def _(pe):
                    turn_pe(pe, o, bank, turned, taken)
                    pe.wait_ge(taken, TURNS)
                    pe.wait_ge(wg_in, 16)
                    for t in range(NT):
                        for c in range(KC):
                            ins = nc.tensor.matmul(lg_p[0:P, t * NX:t * NX + NX], uT[:, c, t * P:t * P + P],
                                                   wg[:, c, :], start=(c == 0), stop=(c == KC - 1))
                    ins.then_inc(lg_done, 1)
                    pe.wait_ge(made, 4)
                    pe.wait_ge(hot_ready, 2)
                    all_hot = hot[:, :, :, :].rearrange("p k t e -> p (k t e)")
                    nc.tensor.matmul(cum_p[0:P, 0:2 * NT * NX], tri[:, :], all_hot, start=True, stop=True
                                     ).then_inc(counted, 1)
                    nc.tensor.matmul(tot_p[0:P, 0:2 * NT * NX], ones[0:P, 0:P], all_hot, start=True, stop=True
                                     ).then_inc(counted, 1)

                @block.scalar
                def _(act):
                    turn_act(act, uT, bank, turned, taken)
                    act.wait_ge(gap_ready, 1)
                    nc.scalar.activation(gap[:, :], gap[:, :], ACT.Exp).then_inc(exp_done, 1)

                @block.vector
                def _(dve):
                    ch = Chain(dve, v10)
                    dve.wait_ge(lg_done, 1)
                    ch.link(nc.vector.tensor_copy(lgt[:, :, :], lg_p[0:P, 0:NT * NX].rearrange("p (t e) -> p t e", e=NX)))
                    for t in range(NT):
                        ch.do(nc.vector.max(best[:, t, :], lgt[:, t, :]))
                    ch.wait()
                    for t in range(NT):
                        ch.do(nc.vector.max_index(which[:, t, :], best[:, t, :], lgt[:, t, :]))
                    ch.wait()
                    nc.vector.tensor_tensor(gap[:, :], best[:, :, 1], best[:, :, 0], ALU.subtract).then_inc(gap_ready, 1)
                    for k in range(2):
                        ch.do(nc.vector.tensor_copy(which_f[:, k, :], which[:, :, k]))
                    ch.wait()
                    dve.wait_ge(made, 3)
                    for k in range(2):
                        nc.vector.tensor_tensor(hot[:, k, :, :], expert[:, :].unsqueeze(1).to_broadcast([P, NT, NX]),
                                                which_f[:, k, :].unsqueeze(2).to_broadcast([P, NT, NX]),
                                                ALU.is_equal).then_inc(hot_ready, 1)
                    dve.wait_ge(exp_done, 1)
                    ch.link(nc.vector.tensor_scalar(prob0[:, 0, :], gap[:, :], 1.0, None, ALU.add))
                    ch.link(nc.vector.reciprocal(prob0[:, 0, :], prob0[:, 0, :]))
                    ch.link(nc.vector.tensor_tensor(prob0[:, 1, :], prob0[:, 0, :], gap[:, :], ALU.mult))
                    dve.wait_ge(counted, 2)
                    ch.do(nc.vector.tensor_copy(tot[:, :, :], tot_p[0:P, 0:2 * NT * NX]
                                                .rearrange("p (b e) -> p b e", e=NX)))
                    ch.do(nc.vector.memset(base[:, 0, :], 0.0))
                    ch.wait()
                    for b in range(1, 2 * NT):
                        ch.link(nc.vector.tensor_tensor(base[:, b, :], base[:, b - 1, :], tot[:, b - 1, :], ALU.add))
                    ch.link(nc.vector.tensor_tensor(base[:, :, :], base[:, :, :], cum_p[0:P, 0:2 * NT * NX]
                                                    .rearrange("p (b e) -> p b e", e=NX), ALU.add))
                    ch.link(nc.vector.tensor_tensor(base[:, :, :], base[:, :, :],
                                                    hot[:, :, :, :].rearrange("p k t e -> p (k t) e"), ALU.mult))
                    ch.link(nc.vector.tensor_reduce(rank[:, :], base[:, :, :], AX.X, ALU.add))
                    ch.link(nc.vector.tensor_scalar(keep[:, :], rank[:, :], float(CAP), None, ALU.is_le))
                    ch.link(nc.vector.scalar_tensor_tensor(out=slot[:, :], scalar=float(CAP), in1=rank[:, :],
                                                           in0=which_f[:, :, :].rearrange("p k t -> p (k t)"),
                                                           op0=ALU.mult, op1=ALU.add))
                    ch.link(nc.vector.tensor_scalar(slot[:, :], slot[:, :], -1.0, None, ALU.add))
                    ch.link(nc.vector.tensor_tensor(rank[:, :], slot[:, :], keep[:, :], ALU.mult))
                    ch.do(nc.vector.tensor_copy(slot_read[:, :], rank[:, :]))
                    ch.do(nc.vector.tensor_tensor(wgt[:, :], prob0[:, :, :].rearrange("p k t -> p (k t)"),
                                                  keep[:, :], ALU.mult))
                    ch.do(nc.vector.tensor_tensor(slot[:, :], slot[:, :], spare[:, :], ALU.subtract))
                    ch.wait()
                    ch.link(nc.vector.tensor_tensor(slot[:, :], slot[:, :], keep[:, :], ALU.mult))
                    ch.link(nc.vector.tensor_tensor(slot[:, :], slot[:, :], spare[:, :], ALU.add))
                    nc.vector.tensor_copy(slot_write[:, :], slot[:, :]).then_inc(slots_ready, 1)
            end_stage()

        mid.close()

        with ExitStack() as ctx:
            R = 3
            FW = FJ * 128
            TILES = FG * FJ
            wf = sb("wf", [128, R, KC, FW], F32, ctx)
            wj = sb("wj", [128, R, FJ, D], F32, ctx)
            wf_part = [sb(f"wf_{n}", [128, 2, KC, FW], F32R, ctx) for n in ("high", "low")]
            wj_part = [sb(f"wj_{n}", [128, 2, FJ, D], F32R, ctx) for n in ("high", "low")]
            xT_part = [sb(f"xT_{n}", [128, KC, CAP], F32R, ctx) for n in ("high", "low")]
            hid_part = [sb(f"hid_{n}", [128, 2, FJ, CAP], F32R, ctx) for n in ("high", "low")]
            hid = sb("hid", [128, 2, CAP], F32, ctx)
            xs = sb("xs", [128, 3, D], F32, ctx)
            xs3 = sb("xs3", [6, D], F32, ctx)
            yT = sb("yT", [128, KC, CAP], F32, ctx)
            ys = sb("ys", [128, 3, D], F32, ctx)
            ys3 = sb("ys3", [6, D], F32, ctx)
            fb_rows = sb("fb_rows", [96, 2, 128], F32, ctx)
            jb_rows = sb("jb_rows", [48, 128], F32, ctx)
            fb = sb("fb", [128, NX * TILES], F32, ctx)
            jb = sb("jb", [128, NX * KC], F32, ctx)
            ring = [ps(f"ring{k}_", [128, 512], ctx) for k in range(2)]
            accu = [ps(f"accu{k}_", [128, 512], ctx) for k in range(KC)]
            wf_in = [sem(f"wf_in{k}") for k in range(R)]
            wj_in = [sem(f"wj_in{k}") for k in range(R)]
            (bias_in, bias_turned, bias_taken, xs_in, loads, stores, wf_high, wf_split, wj_high, wj_split, x_turned,
             x_high, x_split, up_done, up_taken, hid_high, hid_split, pj_done, y_taken, y_turned, y_rows, stored) = (
                sem(n) for n in ("bias_in", "bias_turned", "bias_taken", "xs_in", "loads", "stores", "wf_high",
                                 "wf_split", "wj_high", "wj_split", "x_turned", "x_high", "x_split", "up_done",
                                 "up_taken", "hid_high", "hid_split", "pj_done", "y_taken", "y_turned", "y_rows",
                                 "stored"))
            YU = 2 * len(ROWS)
            LAP = ([("up", i) for i in range(2 * FJ)] + [("y", i) for i in range(YU // 2)]
                   + [("up", i) for i in range(2 * FJ, 3 * FJ)] + [("y", i) for i in range(YU // 2, YU)]
                   + [("up", i) for i in range(3 * FJ, TILES)] + [("x", i) for i in range(KC)])
            fc_w = a["L0_ffn_exp_fc_w"].rearrange("e (c p) f -> p (e c) f", p=128)
            pj_w = a["L0_ffn_exp_proj_w"].rearrange("e (j p) d -> p (e j) d", p=128)

            def rows_of(big, small, s0, n):
                return big[:, s0 // 128, :] if n == 128 else small[:, :]

            def expert_laps(eng, body, peeled=1):
                for e in range(peeled):
                    body(e, False)
                with eng.Fori(peeled, NX - 1) as e:
                    body(e, False)
                body(NX - 1, True)

            with nc.Block() as block:
                @block.sync
                def _(sp):
                    fbr = a["L0_ffn_exp_fc_b"].rearrange("e a (g p) -> (e a g) p", p=128)
                    for k in range(2):
                        sp.dma_start(fb_rows[:, k, :], fbr[96 * k:96 * k + 96, :]).then_inc(bias_in, 16)
                    sp.dma_start(jb_rows[:, :], a["L0_ffn_exp_proj_b"].rearrange("e a (c p) -> (e a c) p", p=128)
                                 ).then_inc(bias_in, 16)

                    def lap(e):
                        for g in range(FG):
                            if g >= R or past(e, 1):
                                sp.wait_ge(wf_split, FG * e + g - R + 1)
                            sp.dma_start(wf[:, g % R, :, :], fc_w[:, bass.ds(e * KC, KC), g * FW:(g + 1) * FW]
                                         ).then_inc(wf_in[g % R], 16)
                            if g >= R or past(e, 1):
                                sp.wait_ge(wj_split, FG * e + g - R + 1)
                            sp.dma_start(wj[:, g % R, :, :], pj_w[:, bass.ds(e * TILES + g * FJ, FJ), :]
                                         ).then_inc(wj_in[g % R], 16)
                    laps(sp, NX, lap)

                @block.gpsimd
                def _(pool):
                    def load(e):
                        pool.dma_start(xs[:, :, :], slot_in[bass.ds(e * CAP, 384), :]
                                       .rearrange("(k p) d -> p k d", p=128)).then_inc(xs_in, 16)
                        pool.dma_start(xs3[:, :], slot_in[bass.ds(e * CAP + 384, 6), :]).then_inc(xs_in, 16)

                    def store(e):
                        pool.wait_ge(y_rows, YU * e + YU)
                        pool.sem_inc(stores, 1)
                        pool.dma_start(slot_out[bass.ds(e * CAP, 384), :].rearrange("(k p) d -> p k d", p=128),
                                       ys[:, :, :]).then_inc(stored, 16)
                        pool.dma_start(slot_out[bass.ds(e * CAP + 384, 6), :], ys3[:, :]).then_inc(stored, 16)

                    load(0)
                    pool.wait_ge(x_turned, KC)
                    pool.sem_inc(loads, 1)
                    load(1)
                    with pool.Fori(1, NX - 1) as e:
                        store(e - 1)
                        pool.wait_ge(x_turned, KC * e + KC)
                        pool.sem_inc(loads, 1)
                        load(e + 1)
                    store(NX - 2)
                    store(NX - 1)
                    pool.wait_ge(stored, 32 * NX)

                @block.tensor
                def _(pe):
                    pe.wait_ge(bias_in, 48)
                    for k in range(2):
                        nc.tensor.transpose(accu[k][:, 0:96], fb_rows[:, k, :], ident[0:96, 0:96]
                                            ).then_inc(bias_turned, 1)
                    nc.tensor.transpose(accu[2][:, 0:48], jb_rows[:, :], ident[0:48, 0:48]).then_inc(bias_turned, 1)
                    pe.wait_ge(bias_taken, 3)

                    def product(bank, weights, moving, start, stop):
                        for k, (p, q) in enumerate(((0, 0), (0, 1), (1, 0))):
                            ins = nc.tensor.matmul(bank, weights[p], moving[q], start=(start and k == 0),
                                                   stop=(stop and k == 2))
                        return ins

                    def turn_in(e, c, bank):
                        pe.wait_ge(xs_in, 32 * (e + 1))
                        for s0, n in ROWS:
                            ins = nc.tensor.transpose(bank[:, s0:s0 + n],
                                                      rows_of(xs, xs3, s0, n)[:, c * 128:c * 128 + 128],
                                                      ident[0:n, 0:n])
                        ins.then_inc(x_turned, 1)

                    def turn_out(i, bank):
                        s0, n = ROWS[i // 2]
                        for c in range(3):
                            ins = nc.tensor.transpose(bank[0:n, c * 128:c * 128 + 128],
                                                      yT[:, 3 * (i % 2) + c, s0:s0 + n], ident[:, :])
                        ins.then_inc(y_turned, 1)

                    def lap(e, last):
                        first = not past(e, 1)
                        uses = [use for use in LAP if not (first and use[0] == "y") and not (last and use[0] == "x")]
                        taken_by = {"up": (up_taken, TILES * e), "y": (y_rows, YU * e - YU),
                                    "x": (x_split, KC * e + KC)}
                        step = iter(range(len(uses)))

                        def claim():
                            u = next(step)
                            if u >= 2:
                                kind, i = uses[u - 2]
                                signal, base = taken_by[kind]
                                pe.wait_ge(signal, base + i + 1)
                            return ring[u % 2]

                        def up(g):
                            pe.wait_ge(wf_split, FG * e + g + 1)
                            for j in range(FJ):
                                bank = claim()
                                for c in range(KC):
                                    ins = product(bank[:, 0:CAP],
                                                  [w[:, g % 2, c, j * 128:j * 128 + 128] for w in wf_part],
                                                  [xT[:, c, :] for xT in xT_part], c == 0, c == KC - 1)
                                ins.then_inc(up_done, 1)

                        def down(g, turns):
                            pe.wait_ge(wj_split, FG * e + g + 1)
                            pe.wait_ge(hid_split, TILES * e + (g + 1) * FJ)
                            if g == 0 and past(e, 1):
                                pe.wait_ge(y_taken, KC * e)
                            for j in range(FJ):
                                for c in range(KC):
                                    ins = product(accu[c][:, 0:CAP],
                                                  [w[:, g % 2, j, c * 128:c * 128 + 128] for w in wj_part],
                                                  [part[:, g % 2, j, :] for part in hid_part],
                                                  g == 0 and j == 0, g == FG - 1 and j == FJ - 1)
                                    if j == FJ - 1 and c == KC - 1:
                                        ins.then_inc(pj_done, 1)
                                    if c % 2 == 1 and turns:
                                        turns.pop(0)()
                            assert not turns

                        pe.wait_ge(x_split, KC * e + KC)
                        for g in range(FG):
                            up(g)
                            if g in (1, 2) and not first:
                                down(g - 1, [lambda i=i: turn_out(i, claim())
                                             for i in range((g - 1) * YU // 2, g * YU // 2)])
                            elif g:
                                down(g - 1, [])
                        down(FG - 1, [] if last else [lambda c=c: turn_in(e + 1, c, claim()) for c in range(KC)])

                    for c in range(KC):
                        if c >= 2:
                            pe.wait_ge(x_split, c - 1)
                        turn_in(0, c, ring[c % 2])
                    expert_laps(pe, lap)
                    pe.wait_ge(y_taken, KC * NX)
                    pe.wait_ge(up_taken, TILES * NX)
                    for i in range(YU):
                        if i >= 2:
                            pe.wait_ge(y_rows, YU * (NX - 1) + i - 1)
                        turn_out(i, ring[i % 2])

                @block.scalar
                def _(act):
                    act.wait_ge(bias_taken, 3)

                    def lap(e, last):
                        def high_fc(g):
                            act.wait_ge(wf_in[g % R], 16 * (FG // R * e + g // R + 1))
                            if g >= 2 or past(e, 1):
                                act.wait_ge(up_done, TILES * e + (g - 1) * FJ)
                            nc.scalar.activation(wf_part[0][:, g % 2, :, :], wf[:, g % R, :, :], ACT.Copy
                                                 ).then_inc(wf_high, 1)

                        if not past(e, 1):
                            high_fc(0)
                        for g in range(FG):
                            if not (last and g == FG - 1):
                                high_fc(g + 1)
                            act.wait_ge(wj_in[g % R], 16 * (FG // R * e + g // R + 1))
                            if g >= 2 or past(e, 1):
                                act.wait_ge(pj_done, FG * e + g - 1)
                            nc.scalar.activation(wj_part[0][:, g % 2, :, :], wj[:, g % R, :, :], ACT.Copy
                                                 ).then_inc(wj_high, 1)
                            for j in range(FJ):
                                i = g * FJ + j
                                act.wait_ge(up_done, TILES * e + i + 1)
                                if i >= 2 or past(e, 1):
                                    act.wait_ge(hid_split, TILES * e + i - 1)
                                nc.scalar.activation(hid[:, i % 2, :], ring[i % 2][:, 0:CAP], ACT.Gelu,
                                                     bias=fb[:, bass.ds(e * TILES + i, 1)]).then_inc(up_taken, 1)
                    expert_laps(act, lap)

                @block.vector
                def _(dve):
                    dve.wait_ge(bias_turned, 3)
                    for k in range(2):
                        nc.vector.tensor_copy(fb[:, 96 * k:96 * k + 96], accu[k][:, 0:96]).then_inc(bias_taken, 1)
                    nc.vector.tensor_copy(jb[:, :], accu[2][:, 0:48]).then_inc(bias_taken, 1)
                    dve.wait_ge(bias_taken, 3)

                    def low(dest, source, high):
                        return nc.vector.tensor_tensor(dest, source, high.bitcast(F32), ALU.subtract)

                    def split_slots(e, c):
                        dve.wait_ge(x_turned, KC * e + c + 1)
                        nc.vector.tensor_copy(xT_part[0][:, c, :], ring[c % 2][:, 0:CAP]).then_inc(x_high, 1)
                        dve.wait_ge(x_high, KC * e + c + 1)
                        low(xT_part[1][:, c, :], ring[c % 2][:, 0:CAP], xT_part[0][:, c, :]).then_inc(x_split, 1)

                    def take_sums(e):
                        dve.wait_ge(pj_done, FG * e + FG)
                        for c in range(KC):
                            nc.vector.tensor_scalar(yT[:, c, :], accu[c][:, 0:CAP], jb[:, bass.ds(e * KC + c, 1)],
                                                    None, ALU.add).then_inc(y_taken, 1)

                    def take_rows(e, i):
                        s0, n = ROWS[i // 2]
                        dve.wait_ge(y_turned, YU * e + i + 1)
                        nc.vector.tensor_copy(rows_of(ys, ys3, s0, n)[:, 384 * (i % 2):384 * (i % 2) + 384],
                                              ring[i % 2][0:n, 0:384]).then_inc(y_rows, 1)

                    def lap(e, last):
                        def low_fc(g):
                            dve.wait_ge(wf_high, FG * e + g + 1)
                            low(wf_part[1][:, g % 2, :, :], wf[:, g % R, :, :], wf_part[0][:, g % 2, :, :]
                                ).then_inc(wf_split, 1)

                        if not past(e, 1):
                            low_fc(0)
                        for g in range(FG):
                            if not (last and g == FG - 1):
                                low_fc(g + 1)
                            dve.wait_ge(wj_high, FG * e + g + 1)
                            low(wj_part[1][:, g % 2, :, :], wj[:, g % R, :, :], wj_part[0][:, g % 2, :, :]
                                ).then_inc(wj_split, 1)
                            if g == 0 and past(e, 1):
                                take_sums(e - 1)
                            for j in range(FJ):
                                i = g * FJ + j
                                dve.wait_ge(up_taken, TILES * e + i + 1)
                                if j == 0 and (g >= 2 or past(e, 1)):
                                    dve.wait_ge(pj_done, FG * e + g - 1)
                                nc.vector.tensor_copy(hid_part[0][:, g % 2, j, :], hid[:, i % 2, :]
                                                      ).then_inc(hid_high, 1)
                                dve.wait_ge(hid_high, TILES * e + i + 1)
                                low(hid_part[1][:, g % 2, j, :], hid[:, i % 2, :], hid_part[0][:, g % 2, j, :]
                                    ).then_inc(hid_split, 1)
                            if g in (1, 2) and past(e, 1):
                                if g == 1 and past(e, 2):
                                    dve.wait_ge(stored, 32 * (e - 1))
                                for i in range((g - 1) * YU // 2, g * YU // 2):
                                    take_rows(e - 1, i)
                        if not last:
                            for c in range(KC):
                                split_slots(e + 1, c)

                    for c in range(KC):
                        split_slots(0, c)
                    expert_laps(dve, lap, peeled=2)
                    take_sums(NX - 1)
                    dve.wait_ge(stored, 32 * (NX - 1))
                    for i in range(YU):
                        take_rows(NX - 1, i)
            end_stage()

        with ExitStack() as ctx:
            got_row = sb("got_row", [P, 4, 2, D], F32, ctx)
            got = [sem(f"got_row{k}") for k in range(4)]
            v11, summed, stored = sem("v11"), sem("out_summed"), sem("out_stored")
            with nc.Block() as block:
                @block.gpsimd
                def _(pool):
                    for t in range(NT):
                        if t >= 4:
                            pool.wait_ge(summed, t - 3)
                        for k in range(2):
                            nc.gpsimd.indirect_dma_start(
                                out=got_row[:, t % 4, k, :], out_offset=None, in_=slot_out,
                                in_offset=bass.IndirectOffsetOnAxis(
                                    ap=slot_read[:, k * NT + t:k * NT + t + 1], axis=0)
                            ).then_inc(got[t % 4], 16)

                @block.vector
                def _(dve):
                    for t in range(NT):
                        dve.wait_ge(got[t % 4], 32 * (t // 4 + 1))
                        for k, s in ((0, v11), (1, summed)):
                            nc.vector.scalar_tensor_tensor(
                                out=x[:, t, :], in0=got_row[:, t % 4, k, :],
                                scalar=wgt[:, k * NT + t:k * NT + t + 1], in1=x[:, t, :],
                                op0=ALU.mult, op1=ALU.add).then_inc(s, 1)
                            if k == 0:
                                dve.wait_ge(v11, t + 1)

                @block.sync
                def _(sp):
                    for t in range(NT):
                        sp.wait_ge(summed, t + 1)
                        sp.dma_start(out[t * P:t * P + P, :], x[:, t, :]).then_inc(stored, 16)
                    sp.wait_ge(stored, 16 * NT)
            end_stage()


_INS = ["x", "src", "dst"] + ["L0_gnn_" + n for n in
                              ("Wsrc", "bsrc", "Wdst", "bdst", "attn", "ln_w", "ln_b", "on_w", "on_b")] + [
    "L0_ffn_" + n for n in ("ln1_w", "ln1_b", "ln2_w", "ln2_b", "attn_qkv_w", "attn_qkv_b", "attn_proj_w",
                            "attn_proj_b", "w_g", "exp_fc_w", "exp_fc_b", "exp_proj_w", "exp_proj_b")]


def kernel(**inputs):
    import numpy as _np
    import concourse.bacc as _bacc
    from concourse import mybir as _mybir
    from concourse.bass_utils import run_bass_kernel_spmd as _run

    nc = _bacc.Bacc("TRN2", target_bir_lowering=False, num_devices=1)
    arrays, args = {}, {}
    for name in _INS:
        v = _np.ascontiguousarray(inputs[name])
        arrays[f"in_{name}_dram"] = v
        args[name] = nc.dram_tensor(f"in_{name}_dram", v.shape, _mybir.dt.from_np(v.dtype), kind="ExternalInput").ap()
    out = nc.dram_tensor("out_0_dram", (N, D), _mybir.dt.float32, kind="ExternalOutput").ap()
    build(nc, args, out)
    r = _run(nc, [arrays], core_ids=[0])
    return r.results[0]["out_0_dram"]
```
